# Optimizing a Trainium2 kernel written in Bass

```python
import numpy as np
import jax
import jax.numpy as jnp

def _softmax(x, axis=-1):
    return jax.nn.softmax(x, axis=axis)

def _gelu(x):
    return jax.nn.gelu(x, approximate=True)

def _silu(x):
    return jax.nn.silu(x)

def _sigmoid(x):
    return jax.nn.sigmoid(x)

def _layernorm(x, axis=-1, eps=1e-05):
    m = jnp.mean(x, axis=axis, keepdims=True)
    v = jnp.var(x, axis=axis, keepdims=True)
    return (x - m) / jnp.sqrt(v + eps)

def _scatter_add(tgt, idx, src, axis=0):
    return tgt.at[idx].add(src)

def _segment_sum(src, seg, n):
    return jax.ops.segment_sum(src, seg, n)
kernel_name = 'mk_recurrent_d1_jaxref_r4_70e197'

def setup_inputs(seed: int=0):
    np.random.seed(seed)
    _w = jnp.asarray

    def _L0_attn_setup():
        import jax, jax.numpy as jnp
        import numpy as np
        B, T, E = (4, 512, 256)
        NUM_HEADS = 16
        HEAD_SIZE = E // NUM_HEADS

        def _rope_tables(T, E):
            thetas = 10000.0 ** (-jnp.arange(0, E, 2, dtype=jnp.float32) / E)
            thetas = jnp.repeat(thetas, 2)
            angles = jnp.arange(T, dtype=jnp.float32)[:, None] * thetas[None, :]
            return (jnp.sin(angles), jnp.cos(angles))

        def _rotate(x, sin, cos):
            Bx, Tx, Ex = x.shape
            xp = x.reshape(Bx, Tx, Ex // 2, 2)
            rot = jnp.stack([-xp[..., 1], xp[..., 0]], axis=-1).reshape(Bx, Tx, Ex)
            return x * cos + rot * sin
        key = jax.random.key(seed)
        ks = jax.random.split(key, 6)
        scale = 1.0 / np.sqrt(E)
        return {'input': jax.random.normal(ks[0], (B, T, E), dtype=jnp.float32), 'Wq': jax.random.normal(ks[1], (E, E), dtype=jnp.float32) * scale, 'Wk': jax.random.normal(ks[2], (E, E), dtype=jnp.float32) * scale, 'Wv': jax.random.normal(ks[3], (E, E), dtype=jnp.float32) * scale, 'Wo': jax.random.normal(ks[4], (E, E), dtype=jnp.float32) * scale, 'bo': jnp.zeros((E,), dtype=jnp.float32)}
    _L0_attn_in = _L0_attn_setup()

    def _L0_ffn_setup():
        import jax, jax.numpy as jnp
        import numpy as np
        import math
        B, S, D = (2, 512, 256)
        H = 16
        HD = D // H
        FFN = 512
        E = 8
        TOP_K = 2
        CAP_FACTOR = 1.25
        EPS = 1e-06
        BASE = 10000.0
        CAP = max(math.ceil(B * S * TOP_K * CAP_FACTOR / E), 1)

        def _rmsnorm(x, w):
            rms = jax.lax.rsqrt(jnp.mean(x * x, axis=-1, keepdims=True) + EPS)
            return w * x * rms

        def _rope(x, cos, sin):
            xr = x[..., 0::2]
            xi = x[..., 1::2]
            c = cos[None, None]
            s_ = sin[None, None]
            out_r = xr * c - xi * s_
            out_i = xr * s_ + xi * c
            return jnp.stack([out_r, out_i], axis=-1).reshape(x.shape)

        def _mha(x, w_qkv, w_o):
            b, s, d = x.shape
            qkv = x @ w_qkv
            q, k, v = jnp.split(qkv, 3, axis=-1)
            to_heads = lambda z: z.reshape(b, s, H, HD).transpose(0, 2, 1, 3)
            q, k, v = (to_heads(q), to_heads(k), to_heads(v))
            theta = BASE ** (-2.0 * (jnp.arange(HD // 2, dtype=jnp.float32) / HD))
            freqs = jnp.arange(s, dtype=jnp.float32)[:, None] * theta[None, :]
            cos, sin = (jnp.cos(freqs), jnp.sin(freqs))
            q = _rope(q, cos, sin)
            k = _rope(k, cos, sin)
            scores = jnp.einsum('bhqd,bhkd->bhqk', q, k) / jnp.sqrt(jnp.float32(HD))
            causal = jnp.tril(jnp.ones((s, s), dtype=bool))
            scores = jnp.where(causal, scores, -jnp.inf)
            attn = jax.nn.softmax(scores, axis=-1)
            y = jnp.einsum('bhqk,bhkd->bhqd', attn, v)
            y = y.transpose(0, 2, 1, 3).reshape(b, s, d)
            return y @ w_o

        def _moe(x, w_router, w1, w2):
            b, s, d = x.shape
            t = b * s
            xf = x.reshape(t, d)
            logits = xf.astype(jnp.float32) @ w_router.astype(jnp.float32)
            probs = jax.nn.softmax(logits, axis=-1)
            g, eidx = jax.lax.top_k(probs, TOP_K)
            fg = g.reshape(t * TOP_K)
            fe = eidx.reshape(t * TOP_K)
            tok_of = jnp.arange(t * TOP_K) // TOP_K
            masked = jnp.where(fe[None, :] == jnp.arange(E)[:, None], fg[None, :], -jnp.inf)
            vals, idx = jax.lax.top_k(masked, CAP)
            valid = jnp.isfinite(vals)
            gates = jnp.where(valid, vals, 0.0)
            tok = tok_of[idx]
            xe = xf[tok]
            h = jax.nn.relu(jnp.einsum('ecd,edf->ecf', xe, w1))
            ye = jnp.einsum('ecf,efd->ecd', h, w2) * gates[..., None]
            y = jnp.zeros_like(xf).at[tok.reshape(-1)].add(ye.reshape(-1, d))
            return y.reshape(b, s, d)
        key = jax.random.key(seed)
        ks = jax.random.split(key, 6)
        sd = 0.02
        return {'x': jax.random.normal(ks[0], (B, S, D), jnp.float32), 'g1': jnp.ones((D,), jnp.float32), 'w_qkv': jax.random.normal(ks[1], (D, 3 * D), jnp.float32) * sd, 'w_o': jax.random.normal(ks[2], (D, D), jnp.float32) * sd, 'g2': jnp.ones((D,), jnp.float32), 'w_router': jax.random.normal(ks[3], (D, E), jnp.float32) * sd, 'w1': jax.random.normal(ks[4], (E, D, FFN), jnp.float32) * sd, 'w2': jax.random.normal(ks[5], (E, FFN, D), jnp.float32) * sd}
    _L0_ffn_in = _L0_ffn_setup()
    _d = {'L0_attn_input': _L0_attn_in['input'], 'L0_attn_Wq': _L0_attn_in['Wq'], 'L0_attn_Wk': _L0_attn_in['Wk'], 'L0_attn_Wv': _L0_attn_in['Wv'], 'L0_attn_Wo': _L0_attn_in['Wo'], 'L0_attn_bo': _L0_attn_in['bo'], 'L0_ffn_g1': _L0_ffn_in['g1'], 'L0_ffn_w_qkv': _L0_ffn_in['w_qkv'], 'L0_ffn_w_o': _L0_ffn_in['w_o'], 'L0_ffn_g2': _L0_ffn_in['g2'], 'L0_ffn_w_router': _L0_ffn_in['w_router'], 'L0_ffn_w1': _L0_ffn_in['w1'], 'L0_ffn_w2': _L0_ffn_in['w2']}
    _x0 = _d['L0_attn_input']
    _d['L0_attn_input'] = jax.random.normal(jax.random.fold_in(jax.random.key(seed), 1), (8, 1024, 256), dtype=_x0.dtype)
    del _x0
    return _d

def reference(L0_attn_input, L0_attn_Wq, L0_attn_Wk, L0_attn_Wv, L0_attn_Wo, L0_attn_bo, L0_ffn_g1, L0_ffn_w_qkv, L0_ffn_w_o, L0_ffn_g2, L0_ffn_w_router, L0_ffn_w1, L0_ffn_w2):

    def _L0_attn_ref(input, Wq, Wk, Wv, Wo, bo):
        import jax, jax.numpy as jnp
        import numpy as np
        B, T, E = (4, 512, 256)
        NUM_HEADS = 16
        HEAD_SIZE = E // NUM_HEADS

        def _rope_tables(T, E):
            thetas = 10000.0 ** (-jnp.arange(0, E, 2, dtype=jnp.float32) / E)
            thetas = jnp.repeat(thetas, 2)
            angles = jnp.arange(T, dtype=jnp.float32)[:, None] * thetas[None, :]
            return (jnp.sin(angles), jnp.cos(angles))

        def _rotate(x, sin, cos):
            Bx, Tx, Ex = x.shape
            xp = x.reshape(Bx, Tx, Ex // 2, 2)
            rot = jnp.stack([-xp[..., 1], xp[..., 0]], axis=-1).reshape(Bx, Tx, Ex)
            return x * cos + rot * sin
        Bx, Tx, Ex = input.shape
        sin, cos = _rope_tables(Tx, Ex)
        rx = _rotate(input, sin, cos)
        q = rx @ Wq.T
        k = rx @ Wk.T
        v = input @ Wv.T

        def split_heads(t):
            return t.reshape(Bx, Tx, NUM_HEADS, HEAD_SIZE).transpose(0, 2, 1, 3)
        q, k, v = (split_heads(q), split_heads(k), split_heads(v))
        scores = jnp.einsum('bhqd,bhkd->bhqk', q, k)
        causal = jnp.tril(jnp.ones((Tx, Tx), dtype=bool))
        scores = jnp.where(causal[None, None], scores, -jnp.inf) / np.sqrt(HEAD_SIZE)
        attn = jax.nn.softmax(scores, axis=-1)
        out = jnp.einsum('bhqk,bhkd->bhqd', attn, v)
        out = out.transpose(0, 2, 1, 3).reshape(Bx, Tx, Ex)
        return out @ Wo.T + bo

    def _L0_ffn_ref(x, g1, w_qkv, w_o, g2, w_router, w1, w2):
        import jax, jax.numpy as jnp
        import numpy as np
        import math
        B, S, D = (2, 512, 256)
        H = 16
        HD = D // H
        FFN = 512
        E = 8
        TOP_K = 2
        CAP_FACTOR = 1.25
        EPS = 1e-06
        BASE = 10000.0
        CAP = max(math.ceil(B * S * TOP_K * CAP_FACTOR / E), 1)

        def _rmsnorm(x, w):
            rms = jax.lax.rsqrt(jnp.mean(x * x, axis=-1, keepdims=True) + EPS)
            return w * x * rms

        def _rope(x, cos, sin):
            xr = x[..., 0::2]
            xi = x[..., 1::2]
            c = cos[None, None]
            s_ = sin[None, None]
            out_r = xr * c - xi * s_
            out_i = xr * s_ + xi * c
            return jnp.stack([out_r, out_i], axis=-1).reshape(x.shape)

        def _mha(x, w_qkv, w_o):
            b, s, d = x.shape
            qkv = x @ w_qkv
            q, k, v = jnp.split(qkv, 3, axis=-1)
            to_heads = lambda z: z.reshape(b, s, H, HD).transpose(0, 2, 1, 3)
            q, k, v = (to_heads(q), to_heads(k), to_heads(v))
            theta = BASE ** (-2.0 * (jnp.arange(HD // 2, dtype=jnp.float32) / HD))
            freqs = jnp.arange(s, dtype=jnp.float32)[:, None] * theta[None, :]
            cos, sin = (jnp.cos(freqs), jnp.sin(freqs))
            q = _rope(q, cos, sin)
            k = _rope(k, cos, sin)
            scores = jnp.einsum('bhqd,bhkd->bhqk', q, k) / jnp.sqrt(jnp.float32(HD))
            causal = jnp.tril(jnp.ones((s, s), dtype=bool))
            scores = jnp.where(causal, scores, -jnp.inf)
            attn = jax.nn.softmax(scores, axis=-1)
            y = jnp.einsum('bhqk,bhkd->bhqd', attn, v)
            y = y.transpose(0, 2, 1, 3).reshape(b, s, d)
            return y @ w_o

        def _moe(x, w_router, w1, w2):
            b, s, d = x.shape
            t = b * s
            xf = x.reshape(t, d)
            logits = xf.astype(jnp.float32) @ w_router.astype(jnp.float32)
            probs = jax.nn.softmax(logits, axis=-1)
            g, eidx = jax.lax.top_k(probs, TOP_K)
            fg = g.reshape(t * TOP_K)
            fe = eidx.reshape(t * TOP_K)
            tok_of = jnp.arange(t * TOP_K) // TOP_K
            masked = jnp.where(fe[None, :] == jnp.arange(E)[:, None], fg[None, :], -jnp.inf)
            vals, idx = jax.lax.top_k(masked, CAP)
            valid = jnp.isfinite(vals)
            gates = jnp.where(valid, vals, 0.0)
            tok = tok_of[idx]
            xe = xf[tok]
            h = jax.nn.relu(jnp.einsum('ecd,edf->ecf', xe, w1))
            ye = jnp.einsum('ecf,efd->ecd', h, w2) * gates[..., None]
            y = jnp.zeros_like(xf).at[tok.reshape(-1)].add(ye.reshape(-1, d))
            return y.reshape(b, s, d)
        x = x + _mha(_rmsnorm(x, g1), w_qkv, w_o)
        x = x + _moe(_rmsnorm(x, g2), w_router, w1, w2)
        return x
    x = L0_attn_input
    xn = _layernorm(x, axis=-1)
    s = _L0_attn_ref(xn, L0_attn_Wq, L0_attn_Wk, L0_attn_Wv, L0_attn_Wo, L0_attn_bo)
    g = _silu(_L0_ffn_ref(xn, L0_ffn_g1, L0_ffn_w_qkv, L0_ffn_w_o, L0_ffn_g2, L0_ffn_w_router, L0_ffn_w1, L0_ffn_w2))
    x = x + s * g
    return x

_drawn_inputs = setup_inputs


def setup_inputs(seed=0):
    import zlib

    import numpy as np

    out = dict(_drawn_inputs(seed))
    spreads = {'L0_attn_bo': (0.0, 0.1), 'L0_ffn_g1': (1.0, 0.6), 'L0_ffn_g2': (1.0, 0.6)}
    factors = {'L0_ffn_w_qkv': 8.0,
     'L0_ffn_w_o': 8.0,
     'L0_ffn_w_router': 8.0,
     'L0_ffn_w1': 8.0,
     'L0_ffn_w2': 8.0}
    for name, (base, spread) in spreads.items():
        noise = np.random.default_rng([zlib.crc32(name.encode()), seed]).standard_normal(out[name].shape)
        drawn = base * np.exp(spread * noise) if base else spread * noise
        out[name] = jnp.asarray(drawn.astype(out[name].dtype))
    for name, factor in factors.items():
        out[name] = (out[name] * factor).astype(out[name].dtype)
    return out
```

```python
from contextlib import ExitStack

import concourse.bass as bass
from concourse import mybir

FP32, BF16 = mybir.dt.float32, mybir.dt.bfloat16
I32, U32 = mybir.dt.int32, mybir.dt.uint32
ALU = mybir.AluOpType
ACT = mybir.ActivationFunctionType
AX = mybir.AxisListType

B, T, E = 8, 1024, 256
TOK = B * T
P = 128
HEADS, HD = 16, 16
GROUPS, GH = 4, 4
KC = E // P
CH = 512
CT = CH // P
TT = T // P
TILES = TOK // P
UNITS = 2 * B * GROUPS
UB = B * GROUPS
VW = 32
PARTS = 3
Q_PART = (0, 0, 1, 1, 0, 2)
K_PART = (0, 1, 0, 1, 2, 0)
BANDS = len(Q_PART)
SROWS = BANDS * HD
EXPERTS, FFN, CAP = 8, 512, 320
SLOTB = (CAP + P - 1) // P
LN_EPS, RMS_EPS = 1e-5, 1e-6
BIG = 3e38


def apart(engine, sem, value, passed):
    engine.wait_ge(sem, value)
    engine.sem_inc(passed, 1)


def looped(engine, count, body):
    body(0)
    with engine.Fori(1, count) as i:
        body(i)


class Chain:

    def __init__(self, engine, sem, base):
        self.engine, self.sem, self.base, self.n = engine, sem, base, 0

    def __call__(self, instruction):
        self.n += 1
        instruction.then_inc(self.sem, 1)
        self.engine.wait_ge(self.sem, self.base + self.n)


NORM_STEPS = 6


def project(nc, x, w_main_t, w_qkv, g1, rope_main, rope_head, identity, xn_d, qk_d, v_d):
    with ExitStack() as ctx:
        sb = lambda name, shape, dt=FP32: ctx.enter_context(nc.sbuf_tensor("a_" + name, shape, dt))
        sem = lambda name: ctx.enter_context(nc.semaphore("a_" + name))
        pair = lambda name: [sem(f"{name}{n}") for n in range(2)]

        w1 = sb("w1", [P, KC, 3 * E])
        w2 = sb("w2", [P, KC, 3 * E])
        g1c = sb("g1c", [P, KC])
        ident = sb("ident", [P, P])
        cs1 = sb("cs1", [P, 2, TT, E])
        cs2 = sb("cs2", [P, 2, TT, HD])
        xin = [sb(f"xin{n}", [P, CT, E]) for n in range(2)]
        xn = [sb(f"xn{n}", [P, CT, E]) for n in range(2)]
        xr = [sb(f"xr{n}", [P, CT, E]) for n in range(2)]
        rx = [sb(f"rx{n}", [P, CT, E]) for n in range(2)]
        rope_a = sb("rope_a", [P, CT, E])
        rope_b = sb("rope_b", [P, CT, E])
        junk = sb("junk", [P, CT, E])
        stats = sb("stats", [P, CT, 6])
        mv = sb("mv", [P, CT, 2])
        var = sb("var", [P, CT])
        rstd = sb("rstd", [P, CT])
        ssq = sb("ssq", [P, CT])
        ms = sb("ms", [P, CT])
        rrms = sb("rrms", [P, CT])
        neghalf = sb("neghalf", [P, CT])
        xt = [sb(f"xt{n}", [P, 3, KC, CH]) for n in range(2)]
        qkr = sb("qkr", [P, CT, 2 * E])
        ra = sb("ra", [P, 2, 2 * E])
        rb = sb("rb", [P, 2, 2 * E])
        parts = [sb(f"parts{n}", [P, PARTS, CH], BF16) for n in range(2)]
        rest = [sb(f"rest{n}", [P, CH]) for n in range(2)]
        vst = [sb(f"vst{n}", [P, 2, CT, HEADS, VW]) for n in range(2)]
        ps = ctx.enter_context(nc.psum_tensor("a_ps", [P, 8, 512], FP32))

        w_in = sem("w_in")
        x_in = pair("x_in")
        xn_out = pair("xn_out")
        qk_out = pair("qk_out")
        v_out = pair("v_out")
        consts = sem("consts")
        vconst = sem("vconst")
        w_ready = sem("w_ready")
        var_ready = sem("var_ready")
        rsq = sem("rsq")
        dchain = sem("dchain")
        passed = sem("passed")
        normed = sem("normed")
        flipped = sem("flipped")
        xt_ready = sem("xt_ready")
        proj = sem("proj")
        rel_dve = sem("rel_dve")
        rel_act = sem("rel_act")
        rotated = sem("rotated")
        hi_ready = sem("hi_ready")
        rest_ready = sem("rest_ready")
        mid_ready = sem("mid_ready")
        lo_ready = pair("lo_ready")

        def chunk_rows(b, half):
            return bass.ds(b * T + half * CH, CH)

        with nc.Block() as block:

            @block.sync
            def _(sp):
                for dst, src in ((w1[:, :, :], w_main_t.rearrange("(k p) n -> p k n", p=P)),
                                 (w2[:, :, :], w_qkv.rearrange("(k p) n -> p k n", p=P)),
                                 (g1c[:, :], g1),
                                 (ident[:, :], identity),
                                 (cs1[:, :, :, :], rope_main.rearrange("c (t p) e -> p c t e", p=P)),
                                 (cs2[:, :, :, :], rope_head.rearrange("c (t p) e -> p c t e", p=P))):
                    sp.dma_start(dst, src).then_inc(w_in, 16)

                def store(b, half):
                    c = 2 * b + half
                    sp.wait_ge(normed, c + 1)
                    sp.dma_start(xn_d[chunk_rows(b, half), :].rearrange("(t p) e -> p t e", p=P),
                                 xn[half][:, :, :]).then_inc(xn_out[half], 16)
                    sp.wait_ge(rel_act, CT * c + CT)
                    for a in range(2):
                        for g in range(GROUPS):
                            unit = b * GROUPS + (a * UB + g)
                            sp.dma_start(
                                v_d[unit, half * CH:(half + 1) * CH, :].rearrange("(t p) n -> p t n", p=P),
                                vst[half][:, a, :, g * GH:(g + 1) * GH, :].rearrange("p t h v -> p t (h v)"),
                            ).then_inc(v_out[half], 16)
                    for n in range(8):
                        a, m = 1 - n // 4, n % 4
                        sp.wait_ge(lo_ready[n % 2], 4 * c + n // 2 + 1)
                        for gi in range(2):
                            unit = b * GROUPS + (a * UB + 2 * (m % 2) + gi)
                            sp.dma_start(
                                qk_d[unit, m // 2, :, :, half * CH:(half + 1) * CH].rearrange("s r t -> r s t"),
                                parts[n % 2][64 * gi:64 * gi + 64, :, :],
                            ).then_inc(qk_out[n % 2], 16)

                def turn(b):
                    for half in range(2):
                        store(b, half)

                looped(sp, B, turn)
                for half in range(2):
                    sp.wait_ge(xn_out[half], 16 * B)
                    sp.wait_ge(v_out[half], 16 * 2 * GROUPS * B)
                    sp.wait_ge(qk_out[half], 16 * 2 * 4 * 2 * B)

            @block.gpsimd
            def _(pool):
                nc.gpsimd.memset(neghalf[:, :], -0.5).then_inc(consts, 1)
                for n in range(2):
                    nc.gpsimd.memset(vst[n][:, :, :, :, HD + 1:VW], 0.0).then_inc(vconst, 1)
                    nc.gpsimd.memset(vst[n][:, :, :, :, HD:HD + 1], 1.0).then_inc(vconst, 1)
                pool.wait_ge(consts, 1)

                def load(b, half):
                    pool.dma_start(xin[half][:, :, :],
                                   x[chunk_rows(b, half), :].rearrange("(t p) e -> p t e", p=P)
                                   ).then_inc(x_in[half], 16)

                def roots(c):
                    pool.wait_ge(var_ready, 2 * c + 1)
                    nc.gpsimd.tensor_tensor(out=rstd[:, :], in0=var[:, :], in1=neghalf[:, :],
                                            op=ALU.pow).then_inc(rsq, 1)
                    pool.wait_ge(var_ready, 2 * c + 2)
                    nc.gpsimd.tensor_tensor(out=rrms[:, :], in0=ms[:, :], in1=neghalf[:, :],
                                            op=ALU.pow).then_inc(rsq, 1)

                def lows(c):
                    for n in range(8):
                        s = n % 2
                        pool.wait_ge(mid_ready, 8 * c + n + 1)
                        nc.gpsimd.tensor_tensor(out=parts[s][:, 2, :], in0=rest[s][:, :], in1=parts[s][:, 1, :],
                                                op=ALU.subtract).then_inc(lo_ready[s], 1)

                def step(b, half):
                    c = 2 * b + half
                    roots(c + 1)
                    load(b + 1, half)
                    lows(c)

                load(0, 0)
                load(0, 1)
                roots(0)
                def turn(b):
                    for half in range(2):
                        step(b, half)

                looped(pool, B - 1, turn)
                roots(2 * B - 1)
                lows(2 * B - 2)
                lows(2 * B - 1)

            @block.vector
            def _(dve):
                dve.wait_ge(w_in, 16 * 6)
                for k in range(KC):
                    nc.vector.tensor_scalar(w2[:, k, :], w2[:, k, :], g1c[:, k:k + 1], None,
                                            ALU.mult).then_inc(w_ready, 1)
                dve.wait_ge(w_ready, KC)
                nc.vector.tensor_scalar(w1[:, :, 0:E], w1[:, :, 0:E], 0.25, None, ALU.mult).then_inc(w_ready, 1)
                nc.vector.tensor_scalar(w2[:, :, 0:E], w2[:, :, 0:E], 0.25, None, ALU.mult).then_inc(w_ready, 1)

                def norms(b, half, first=False):
                    c = 2 * b + half
                    chain = Chain(dve, dchain, c * NORM_STEPS)
                    dve.wait_ge(x_in[half], 16 * b + 16)
                    if not first:
                        dve.wait_ge(flipped, CT * (c - 1))
                        dve.wait_ge(xn_out[half], 16 * b)
                    for t in range(CT):
                        last = nc.vector.bn_stats(stats[:, t, :], xin[half][:, t, :])
                    chain(last)
                    dve.sem_inc(passed, 1)
                    for t in range(CT):
                        last = nc.vector.bn_aggr(mv[:, t, :], stats[:, t, :])
                    chain(last)
                    nc.vector.tensor_scalar(var[:, :], mv[:, :, 1], LN_EPS, None, ALU.add).then_inc(var_ready, 1)
                    dve.wait_ge(rsq, 2 * c + 1)
                    for t in range(CT):
                        last = nc.vector.tensor_scalar(xn[half][:, t, :], xin[half][:, t, :], mv[:, t, 0:1],
                                                       rstd[:, t:t + 1], ALU.subtract, ALU.mult)
                    chain(last)
                    for t in range(CT):
                        last = nc.vector.tensor_tensor_reduce(
                            out=junk[:, t, :], in0=xn[half][:, t, :], in1=xn[half][:, t, :], scale=1.0, scalar=0.0,
                            op0=ALU.mult, op1=ALU.add, accum_out=ssq[:, t:t + 1])
                    chain(last)
                    nc.vector.tensor_scalar(ms[:, :], ssq[:, :], 1.0 / E, RMS_EPS, ALU.mult,
                                            ALU.add).then_inc(var_ready, 1)
                    cos = cs1[:, 0, half * CT:(half + 1) * CT, :]
                    sin = cs1[:, 1, half * CT:(half + 1) * CT, :]
                    nc.vector.tensor_tensor(rope_a[:, :, :], xn[half][:, :, :], cos, ALU.mult)
                    for o in range(2):
                        last = nc.vector.tensor_tensor(rope_b[:, :, o::2], xn[half][:, :, 1 - o::2],
                                                       sin[:, :, o::2], ALU.mult)
                    chain(last)
                    chain(nc.vector.tensor_tensor(rx[half][:, :, :], rope_a[:, :, :], rope_b[:, :, :], ALU.add))
                    dve.wait_ge(rsq, 2 * c + 2)
                    for t in range(CT):
                        last = nc.vector.tensor_scalar(xr[half][:, t, :], xn[half][:, t, :], rrms[:, t:t + 1],
                                                       None, ALU.mult)
                    last.then_inc(normed, 1)
                    assert chain.n == NORM_STEPS

                def rotate(b, half):
                    c = 2 * b + half
                    for t in range(CT):
                        dve.wait_ge(proj, 16 * c + 2 * t + 1)
                        qk = ps[:, 4 + (2 * t) % 4, :].rearrange("p (h d) -> p h d", d=HD)
                        cos = cs2[:, 0, half * CT + t, :].rearrange("p (o d) -> p o d", o=1).broadcast_to((P, 2 * HEADS, HD))
                        sin = cs2[:, 1, half * CT + t, :].rearrange("p (o d) -> p o d", o=1).broadcast_to((P, 2 * HEADS, HD))
                        ra_v = ra[:, t % 2, :].rearrange("p (h d) -> p h d", d=HD)
                        rb_v = rb[:, t % 2, :].rearrange("p (h d) -> p h d", d=HD)
                        if t != 1:
                            dve.wait_ge(rotated, CT * c + max(t - 1, 0))
                        nc.vector.tensor_tensor(ra_v, qk, cos, ALU.mult)
                        nc.vector.tensor_tensor(rb_v[:, :, 0::2], qk[:, :, 1::2], sin[:, :, 0::2], ALU.mult)
                        nc.vector.tensor_tensor(rb_v[:, :, 1::2], qk[:, :, 0::2], sin[:, :, 1::2],
                                                ALU.mult).then_inc(rel_dve, 1)
                        dve.wait_ge(rel_dve, 12 * c + t + 1)
                        nc.vector.tensor_tensor(qkr[:, t, :], ra[:, t % 2, :], rb[:, t % 2, :], ALU.add).then_inc(rotated, 1)

                def rests(b, half):
                    c = 2 * b + half
                    for n in range(8):
                        s = n % 2
                        dve.wait_ge(hi_ready, 8 * c + n + 1)
                        dve.wait_ge(lo_ready[s], 4 * c + n // 2)
                        nc.vector.tensor_tensor(rest[s][:, :], ps[:, 4 + n % 4, :], parts[s][:, 0, :],
                                                ALU.subtract).then_inc(rel_dve, 1)

                norms(0, 0, first=True)
                def turn(b):
                    for half in range(2):
                        norms(b + half, 1 - half)
                        rotate(b, half)
                        rests(b, half)

                looped(dve, B - 1, turn)
                norms(B - 1, 1)
                for half in range(2):
                    rotate(B - 1, half)
                    rests(B - 1, half)

            @block.scalar
            def _(act):
                act.wait_ge(vconst, 4)
                def evacuate(b, half):
                    c = 2 * b + half
                    for t in range(CT):
                        act.wait_ge(flipped, CT * c + t + 1)
                        bank = 2 * (t % 2)
                        nc.scalar.copy(xt[half][:, :, :, t * P:(t + 1) * P].rearrange("p s k t -> p (s k) t"),
                                       ps[:, bank:bank + 2, :].rearrange("p b c -> p (b c)")[:, 0:6 * P]
                                       .rearrange("p (s t) -> p s t", t=P)).then_inc(xt_ready, 1)
                    act.wait_ge(v_out[half], 16 * 2 * GROUPS * b)
                    for t in range(CT):
                        act.wait_ge(proj, 16 * c + 2 * t + 2)
                        nc.scalar.copy(vst[half][:, :, t, :, 0:HD],
                                       ps[:, 4 + (2 * t + 1) % 4, :].rearrange("p (a h d) -> p a h d", a=2, d=HD)
                                       ).then_inc(rel_act, 1)
                    for n in range(8):
                        s = n % 2
                        act.wait_ge(proj, 16 * c + 8 + n + 1)
                        act.wait_ge(qk_out[s], 32 * (4 * c + n // 2))
                        nc.scalar.copy(parts[s][:, 0, :], ps[:, 4 + n % 4, :]).then_inc(hi_ready, 1)
                        act.wait_ge(rel_dve, 12 * c + 4 + n + 1)
                        nc.scalar.copy(parts[s][:, 1, :], rest[s][:, :]).then_inc(mid_ready, 1)

                def turn(b):
                    for half in range(2):
                        evacuate(b, half)

                looped(act, B, turn)

            @block.tensor
            def _(pe):
                pe.wait_ge(w_in, 16 * 6)
                pe.wait_ge(w_ready, KC + 2)

                def chunk(b, half):
                    c = 2 * b + half
                    pe.wait_ge(normed, c + 1)
                    for t in range(CT):
                        if t < 2:
                            pe.wait_ge(xt_ready, CT * c)
                        else:
                            pe.wait_ge(xt_ready, CT * c + t - 1)
                        for s, src in enumerate((xn[half], rx[half], xr[half])):
                            for k in range(KC):
                                col = (s * KC + k) * P
                                last = nc.tensor.transpose(ps[:, 2 * (t % 2) + col // 512, col % 512:col % 512 + P],
                                                           src[:, t, k * P:(k + 1) * P], ident[:, :])
                        last.then_inc(flipped, 1)
                    pe.wait_ge(rel_dve, 12 * c)
                    pe.wait_ge(rel_act, CT * c)
                    for t in range(CT):
                        if t >= 2:
                            pe.wait_ge(rel_dve, 12 * c + t - 1)
                        pe.wait_ge(xt_ready, CT * c + t + 1)
                        tok = slice(t * P, (t + 1) * P)
                        for k in range(KC):
                            last = nc.tensor.matmul(ps[:, 4 + (2 * t) % 4, :], xt[half][:, 2, k, tok],
                                                    w2[:, k, 0:2 * E], start=(k == 0), stop=(k == KC - 1))
                        last.then_inc(proj, 1)
                        if t >= 2:
                            pe.wait_ge(rel_act, CT * c + t - 1)
                        for a, (s, w) in enumerate(((2, w2), (0, w1))):
                            for k in range(KC):
                                last = nc.tensor.matmul(ps[:, 4 + (2 * t + 1) % 4, a * E:(a + 1) * E],
                                                        xt[half][:, s, k, tok], w[:, k, 2 * E:3 * E],
                                                        start=(k == 0), stop=(k == KC - 1))
                        last.then_inc(proj, 1)
                    for m in range(4):
                        if m % 2 == 0:
                            pe.wait_ge(rel_dve, 12 * c + 3 + m // 2)
                        else:
                            pe.wait_ge(rel_act, CT * c + 3 + m // 2)
                        for k in range(KC):
                            last = nc.tensor.matmul(ps[:, 4 + m, :], w1[:, k, m * P:(m + 1) * P],
                                                    xt[half][:, 1, k, :], start=(k == 0), stop=(k == KC - 1))
                        last.then_inc(proj, 1)
                    pe.wait_ge(rotated, CT * (c + 1))
                    for m in range(4):
                        pe.wait_ge(rel_dve, 12 * c + 4 + m + 1)
                        for t in range(CT):
                            last = nc.tensor.transpose(ps[:, 4 + m, t * P:(t + 1) * P],
                                                       qkr[:, t, m * P:(m + 1) * P], ident[:, :])
                        last.then_inc(proj, 1)

                def turn(b):
                    for half in range(2):
                        chunk(b, half)

                looped(pe, B, turn)


RING = 3
PBUFS = 4
AHEAD = 10
ROW_LAG = 5


def maximum_pass():
    own = [[("max", h, t, p) for t in range(TT) for p in range(1 + (t >= TT // 2))] for h in range(GH)]
    items = []
    for h in range(GH):
        rows = [("row", 0 if h else -1, (h - 1) % GH, half) for half in range(2)]
        items += own[h][:ROW_LAG] + rows + own[h][ROW_LAG:]
    return items


ITEMS = maximum_pass()
LAST_MAX = [max(k for k, it in enumerate(ITEMS) if it[:2] == ("max", h)) for h in range(GH)]


def maxima_before(k, bank):
    return sum(1 for n in range(k) if ITEMS[n][0] == "max" and n % 2 == bank)


MAX_PER_UNIT = [maxima_before(len(ITEMS), bank) for bank in range(2)]


def unit_steps():
    exp_cost = [(TT - j) * P / 1.2 + 140 for j in range(TT) for _ in range(GH)]
    stream = [("item", 1, k) for k in range(AHEAD, len(ITEMS))] + [("item", 2, k) for k in range(AHEAD)]
    cost = [200.0 if ITEMS[k][0] == "row" else min((ITEMS[k][2] + 1) * P - 512 * ITEMS[k][3], 512) / 0.96 + 100
            for _, _, k in stream]
    steps, done, spent, taken = [], 0.0, 0.0, 0
    for s in range(TT * GH):
        j, h = divmod(s, GH)
        steps.append(("scores", j, h))
        done += exp_cost[s]
        while taken < len(stream) and (spent + cost[taken] / 2) / sum(cost) <= done / sum(exp_cost):
            steps.append(stream[taken])
            spent += cost[taken]
            taken += 1
        du, jv = (0, j - 2) if j >= 2 else (-1, j + TT - 2)
        if jv < TT // 2:
            if h % 2:
                steps.append(("values", du, jv, h // 2))
        elif h == 2:
            steps.append(("values", du, jv, 1))
    return steps + stream[taken:]


STEPS = unit_steps()


def attend(nc, identity, causal_mask, qk_d, v_d, y_d):
    with ExitStack() as ctx:
        sb = lambda name, shape, dt=FP32: ctx.enter_context(nc.sbuf_tensor("b_" + name, shape, dt))
        pb = lambda name, shape: ctx.enter_context(nc.psum_tensor("b_" + name, shape, FP32))
        sem = lambda name: ctx.enter_context(nc.semaphore("b_" + name))
        many = lambda name, n: [sem(f"{name}{i}") for i in range(n)]

        qs = [sb(f"qs{r}", [P, GH, T], BF16) for r in range(RING)]
        ks = [sb(f"ks{r}", [P, GH, T], BF16) for r in range(RING)]
        vv = [sb(f"vv{r}", [P, TT, GH * VW]) for r in range(RING)]
        yo = [sb(f"yo{r}", [P, T]) for r in range(RING)]
        probs = [sb(f"probs{r}", [P, GH, T]) for r in range(PBUFS)]
        ident_f = sb("ident_f", [P, P])
        ident = sb("ident", [P, P], BF16)
        mask = sb("mask", [P, 512])
        junk = sb("junk", [P, 2, 512])
        pmax = sb("pmax", [P, GH, TT, 2])
        negm = sb("negm", [P, GH, TT])
        nrest = sb("nrest", [P, GH, TT])
        mparts = sb("mparts", [P, GH, TT, PARTS], BF16)
        acc = pb("acc", [P, 2, 512])
        st = [pb(f"st{n}", [P, 2, 512]) for n in range(2)]
        sm = pb("sm", [P, 2, 512])

        const_in, consts = sem("const_in"), sem("consts")
        qk_in, v_in, y_out = many("qk_in", RING), many("v_in", RING), many("y_out", RING)
        st_ready, exp_done = many("st_ready", 2), many("exp_done", 2)
        mask_done, pv_done = many("mask_done", PBUFS), many("pv_done", PBUFS)
        max_ready, max_done = many("max_ready", 2), many("max_done", 2)
        row_ready, row_done = many("row_ready", 2), many("row_done", 2)
        negm_ready, split_chain, mparts_ready = sem("negm_ready"), sem("split_chain"), sem("mparts_ready")
        y_ready = sem("y_ready")
        dve_passed, pool_passed = sem("dve_passed"), sem("pool_passed")

        def shifted(i, r, d):
            return i + (r + d) // RING, (r + d) % RING

        def over_units(engine, do_step):
            last = UNITS - 1

            def unit(i, r):
                for step in STEPS:
                    d = step[1] if step[0] != "scores" else 0
                    if isinstance(i, int):
                        w = RING * i + r + d
                        row = step[0] == "item" and ITEMS[step[2]][0] == "row"
                        if w < 0 or w > last + (row and ITEMS[step[2]][1] == -1):
                            continue
                    do_step(*shifted(i, r, d), step)

            for k in range(len(ITEMS)):
                if ITEMS[k][:2] != ("row", -1):
                    do_step(0, 0, ("item", 0, k))
            for k in range(AHEAD):
                do_step(0, 1, ("item", 0, k))
            whole = UNITS // RING - 1
            for r in range(RING):
                unit(0, r)
            with engine.Fori(1, whole) as i:
                for r in range(RING):
                    unit(i, r)
            for w in range(whole * RING, UNITS):
                unit(w // RING, w % RING)
            for step in STEPS:
                if step[0] == "values" and step[1] == -1:
                    do_step(last // RING, last % RING, step)

        with nc.Block() as block:

            @block.sync
            def _(sp):
                sp.dma_start(ident_f[:, :], identity).then_inc(const_in, 16)
                sp.dma_start(mask[:, :], causal_mask).then_inc(const_in, 16)

                def load(i, r):
                    unit = RING * i + r
                    for band in range(BANDS):
                        rows = slice(band * HD, (band + 1) * HD)
                        for which, part, dst in ((0, Q_PART[band], qs[r]), (1, K_PART[band], ks[r])):
                            sp.dma_start(dst[rows, :, :],
                                         qk_d[unit, which, part, :, :].rearrange("(h f) t -> f h t", f=HD)
                                         ).then_inc(qk_in[r], 16)
                    sp.dma_start(vv[r][:, :, :], v_d[unit, :, :].rearrange("(t p) n -> p t n", p=P)
                                 ).then_inc(v_in[r], 16)

                def store(i, r):
                    sp.wait_ge(y_ready, RING * i + r + 1)
                    sp.dma_start(y_d[RING * i + r, :, :], yo[r][:, :]).then_inc(y_out[r], 16)

                def turn(i):
                    for r in range(RING):
                        sp.wait_ge(pv_done[3], 2 * (RING * i + r + 1))
                        load(i + 1, r)
                        store(i, r)

                for r in range(RING):
                    load(0, r)
                looped(sp, UNITS // RING - 1, turn)
                i = UNITS // RING - 1
                sp.wait_ge(pv_done[3], 2 * (RING * i + 1))
                load(i + 1, 0)
                for r in range(RING):
                    store(i, r)
                store(i + 1, 0)
                sp.wait_ge(y_out[0], 16 * (i + 2))
                for r in range(1, RING):
                    sp.wait_ge(y_out[r], 16 * (i + 1))

            @block.tensor
            def _(pe):
                pe.wait_ge(const_in, 32)
                pe.wait_ge(consts, RING + 2)

                def item(i, r, k):
                    unit, bank = RING * i + r, k % 2
                    if k == 0:
                        pe.wait_ge(qk_in[r], 16 * 2 * BANDS * (i + 1))
                    n = k - 2
                    if isinstance(unit, int) and unit == UNITS:
                        n = k % 2 - 2
                    if isinstance(unit, int) and unit == 0 and n >= 0 and ITEMS[n][:2] == ("row", -1):
                        n -= 2
                    w = unit if n >= 0 else unit - 1
                    n %= len(ITEMS)
                    if not isinstance(w, int) or w >= 0:
                        if ITEMS[n][0] == "max":
                            pe.wait_ge(max_done[bank], MAX_PER_UNIT[bank] * w + maxima_before(n + 1, bank))
                        else:
                            pe.wait_ge(row_done[bank], GH * (w + ITEMS[n][1]) + ITEMS[n][2] + 1)
                    if ITEMS[k][0] == "max":
                        _, h, t, piece = ITEMS[k]
                        n = min((t + 1) * P - 512 * piece, 512)
                        nc.tensor.matmul(sm[:, bank, 0:n], qs[r][0:SROWS, h, t * P:(t + 1) * P],
                                         ks[r][0:SROWS, h, 512 * piece:512 * piece + n], start=True,
                                         stop=True).then_inc(max_ready[bank], 1)
                    else:
                        _, dw, h, half = ITEMS[k]
                        pe.wait_ge(mparts_ready, GH * (unit + dw) + h + 1)
                        for n in range(4):
                            last = nc.tensor.matmul(sm[SROWS:SROWS + PARTS, bank, n * P:(n + 1) * P],
                                                    mparts[:, h, 4 * half + n, :], ident[:, :], start=True, stop=True)
                        last.then_inc(row_ready[bank], 1)

                def scores(i, r, j, h):
                    unit, n = RING * i + r, GH * j + h
                    if j == 0:
                        for bank in range(2):
                            pe.wait_ge(row_done[bank], GH * unit + h + 1)
                    pe.wait_ge(exp_done[n % 2], 16 * unit + n // 2)
                    for half in range(j // 4, 2):
                        lo = max(j * P - 512 * half, 0)
                        last = nc.tensor.matmul(st[n % 2][:, half, lo:512],
                                                ks[r][0:SROWS + PARTS, h, j * P:(j + 1) * P],
                                                qs[r][0:SROWS + PARTS, h, 512 * half + lo:512 * (half + 1)],
                                                start=True, stop=True)
                    last.then_inc(st_ready[n % 2], 1)

                def values(i, r, j, half):
                    unit = RING * i + r
                    if j == 0 and half == 0:
                        pe.wait_ge(y_ready, unit)
                        pe.wait_ge(v_in[r], 16 * (i + 1))
                    if half == j // 4:
                        pe.wait_ge(mask_done[j % PBUFS], 2 * unit + j // PBUFS + 1)
                    lo = max(j * P - 512 * half, 0)
                    for h in range(GH):
                        last = nc.tensor.matmul(acc[VW * h:VW * (h + 1), half, lo:512],
                                                vv[r][:, j, VW * h:VW * (h + 1)],
                                                probs[j % PBUFS][:, h, 512 * half + lo:512 * (half + 1)],
                                                start=(j == 0), stop=(j == (3 if half == 0 else 7)))
                    if half:
                        last.then_inc(pv_done[j % PBUFS], 1)

                def do_step(i, r, step):
                    if step[0] == "scores":
                        scores(i, r, *step[1:])
                    elif step[0] == "item":
                        item(i, r, step[2])
                    else:
                        values(i, r, *step[2:])

                over_units(pe, do_step)

            @block.scalar
            def _(act):
                act.wait_ge(consts, RING + 2)

                def do_step(i, r, step):
                    unit = RING * i + r
                    if step[0] == "scores":
                        _, j, h = step
                        n = GH * j + h
                        if h == 0:
                            act.wait_ge(pv_done[j % PBUFS], 2 * unit + j // PBUFS)
                        act.wait_ge(st_ready[n % 2], 16 * unit + n // 2 + 1)
                        nc.scalar.activation(probs[j % PBUFS][:, h, j * P:T],
                                             st[n % 2][:, :, :].rearrange("p b c -> p (b c)")[:, j * P:T],
                                             ACT.Exp).then_inc(exp_done[n % 2], 1)
                    elif step[0] == "item" and ITEMS[step[2]][0] == "row":
                        bank = step[2] % 2
                        _, dw, h, half = ITEMS[step[2]]
                        act.wait_ge(row_ready[bank], GH * (unit + dw) + h + 1)
                        nc.scalar.copy(qs[(r + dw) % RING][SROWS:SROWS + PARTS, h, 512 * half:512 * (half + 1)],
                                       sm[SROWS:SROWS + PARTS, bank, :]).then_inc(row_done[bank], 1)
                    elif step[0] == "values" and step[2] == TT - 1:
                        act.wait_ge(pv_done[3], 2 * (unit + 1))
                        act.wait_ge(y_out[r], 16 * i)
                        nc.scalar.copy(yo[r][:, :], acc[:, :, :].rearrange("p b c -> p (b c)")).then_inc(y_ready, 1)

                over_units(act, do_step)

            @block.vector
            def _(dve):
                def do_step(i, r, step):
                    if step[0] != "item" or ITEMS[step[2]][0] != "max":
                        return
                    unit, k = RING * i + r, step[2]
                    _, h, t, piece = ITEMS[k]
                    bank = k % 2
                    n = min((t + 1) * P - 512 * piece, 512)
                    ready = MAX_PER_UNIT[bank] * unit + maxima_before(k, bank) + 1
                    if piece == t // 4:
                        apart(dve, max_ready[bank], ready, dve_passed)
                        nc.vector.tensor_tensor_reduce(
                            out=junk[:, bank, 0:n], in0=sm[:, bank, 0:n], in1=mask[:, 512 - n:512], scale=1.0,
                            scalar=-BIG, op0=ALU.add, op1=ALU.max,
                            accum_out=pmax[:, h, t, 1:2]).then_inc(max_done[bank], 1)
                    else:
                        dve.wait_ge(max_ready[bank], ready)
                        nc.vector.tensor_reduce(pmax[:, h, t, 0:1], sm[:, bank, 0:n], AX.X,
                                                ALU.max).then_inc(max_done[bank], 1)
                    if k == LAST_MAX[h]:
                        for b in range(2):
                            dve.wait_ge(max_done[b], MAX_PER_UNIT[b] * unit + maxima_before(k + 1, b))
                        nc.vector.tensor_reduce(negm[:, h, :], pmax[:, h, :, :], AX.X, ALU.max,
                                                negate=True).then_inc(negm_ready, 1)

                for r in range(RING):
                    nc.vector.memset(ks[r][SROWS:SROWS + PARTS, :, :], 1.0).then_inc(consts, 1)
                nc.vector.memset(pmax[:, :, :, :], -BIG).then_inc(consts, 1)
                dve.wait_ge(const_in, 32)
                nc.vector.tensor_copy(ident[:, :], ident_f[:, :]).then_inc(consts, 1)
                dve.wait_ge(consts, RING + 2)
                over_units(dve, do_step)

            @block.gpsimd
            def _(pool):
                def do_step(i, r, step):
                    unit = RING * i + r
                    if step[0] == "scores" and step[2] == GH - 1:
                        j = step[1]
                        for n in range(2):
                            apart(pool, exp_done[n], 16 * unit + 2 * (j + 1), pool_passed)
                        diag = probs[j % PBUFS][:, :, j * P:(j + 1) * P]
                        nc.gpsimd.affine_select(out=diag, in_=diag, compare_op=ALU.is_ge, fill=0.0, base=0,
                                                pattern=[[0, GH], [1, P]],
                                                channel_multiplier=-1).then_inc(mask_done[j % PBUFS], 1)
                    elif step[0] == "item" and step[2] in LAST_MAX:
                        h = LAST_MAX.index(step[2])
                        apart(pool, negm_ready, GH * unit + h + 1, pool_passed)
                        chain = Chain(pool, split_chain, 3 * (GH * unit + h))
                        chain(nc.gpsimd.tensor_copy(mparts[:, h, :, 0], negm[:, h, :]))
                        chain(nc.gpsimd.tensor_tensor(out=nrest[:, h, :], in0=negm[:, h, :], in1=mparts[:, h, :, 0],
                                                      op=ALU.subtract))
                        pool.sem_inc(pool_passed, 1)
                        chain(nc.gpsimd.tensor_copy(mparts[:, h, :, 1], nrest[:, h, :]))
                        nc.gpsimd.tensor_tensor(out=mparts[:, h, :, 2], in0=nrest[:, h, :], in1=mparts[:, h, :, 1],
                                                op=ALU.subtract).then_inc(mparts_ready, 1)

                over_units(pool, do_step)


class HeadsOut:

    def __init__(self, nc, ctx, tag, ps, attention, w_out, ident, y_d):
        sb = lambda name, shape, dt=FP32: ctx.enter_context(nc.sbuf_tensor(f"{tag}_{name}", shape, dt))
        sem = lambda name: ctx.enter_context(nc.semaphore(f"{tag}_{name}"))
        self.nc, self.ps, self.attention, self.w_out, self.ident, self.y_d = nc, ps, attention, w_out, ident, y_d
        self.yt = [sb(f"yt{n}", [P, GROUPS, CH]) for n in range(2)]
        self.yn = [sb(f"yn{n}", [P, E]) for n in range(2)]
        self.ynt = [sb(f"ynt{n}", [P, KC, P]) for n in range(2)]
        self.rden = [sb(f"rden{n}", [P, HEADS]) for n in range(2)]
        self.y_in = [sem(f"y_in{n}") for n in range(2)]
        self.flipped, self.rden_ready, self.yn_ready = sem("flipped"), sem("rden_ready"), sem("yn_ready")
        self.back, self.ynt_ready, self.projected, self.taken = sem("back"), sem("ynt_ready"), sem("projected"), sem("taken")

    def load(self, queue, b, half):
        unit = b * GROUPS + self.attention * UB
        queue.dma_start(self.yt[half][:, :, :],
                        self.y_d[bass.ds(unit, GROUPS), :, half * CH:(half + 1) * CH].rearrange("g r t -> r g t")
                        ).then_inc(self.y_in[half], 16)

    def tensor(self, pe, b, half):
        c, nc, ps = 2 * b + half, self.nc, self.ps

        def flip(t):
            pe.wait_ge(self.yn_ready, CT * c + max(t - 1, 0))
            for g in range(GROUPS):
                last = nc.tensor.transpose(ps[:, t % 2, g * P:(g + 1) * P],
                                           self.yt[half][:, g, t * P:(t + 1) * P], self.ident[:, :])
            last.then_inc(self.flipped, 1)

        def back(t):
            pe.wait_ge(self.yn_ready, CT * c + t + 1)
            if t != 1:
                pe.wait_ge(self.ynt_ready, CT * c + max(t - 1, 0))
            for k in range(KC):
                last = nc.tensor.transpose(ps[:, 2 + t % 2, k * P:(k + 1) * P],
                                           self.yn[t % 2][:, k * P:(k + 1) * P], self.ident[:, :])
            last.then_inc(self.back, 1)

        def out(t):
            pe.wait_ge(self.ynt_ready, CT * c + t + 1)
            if t != 1:
                pe.wait_ge(self.taken, CT * c + max(t - 1, 0))
            for k in range(KC):
                last = nc.tensor.matmul(ps[:, 4 + t % 2, 0:E], self.ynt[t % 2][:, k, :], self.w_out[:, k, :],
                                        start=(k == 0), stop=(k == KC - 1))
            last.then_inc(self.projected, 1)

        pe.wait_ge(self.y_in[half], 16 * b + 16)
        flip(0)
        flip(1)
        back(0)
        for t in range(2, CT):
            flip(t)
            back(t - 1)
            out(t - 2)
        back(CT - 1)
        out(CT - 2)
        out(CT - 1)

    def vector(self, dve, b, half, t):
        c, nc = 2 * b + half, self.nc
        dve.wait_ge(self.flipped, CT * c + t + 1)
        y = self.ps[:, t % 2, :].rearrange("p (h v) -> p h v", v=VW)
        nc.vector.reciprocal(self.rden[t % 2][:, :], y[:, :, HD]).then_inc(self.rden_ready, 1)
        dve.wait_ge(self.rden_ready, CT * c + t + 1)
        if t != 1:
            dve.wait_ge(self.back, CT * c + max(t - 1, 0))
        nc.vector.tensor_tensor(self.yn[t % 2][:, :].rearrange("p (h d) -> p h d", d=HD), y[:, :, 0:HD],
                                self.rden[t % 2][:, :].rearrange("p (h o) -> p h o", o=1)
                                .broadcast_to((P, HEADS, HD)), ALU.mult).then_inc(self.yn_ready, 1)

    def scalar(self, act, b, half, t):
        c = 2 * b + half
        act.wait_ge(self.back, CT * c + t + 1)
        if t != 1:
            act.wait_ge(self.projected, CT * c + max(t - 1, 0))
        self.nc.scalar.copy(self.ynt[t % 2][:, :, :],
                            self.ps[:, 2 + t % 2, 0:KC * P].rearrange("p (k t) -> p k t", k=KC)
                            ).then_inc(self.ynt_ready, 1)


def staggered(engine, lead, follow):
    lead(0, 0)
    def turn(b):
        for half in range(2):
            lead(b + half, 1 - half)
            follow(b, half)

    looped(engine, B - 1, turn)
    lead(B - 1, 1)
    for half in range(2):
        follow(B - 1, half)


def block_mid(nc, w_o, w_router, g2, identity, xn_d, y_d, z_d, h_d, logits):
    with ExitStack() as ctx:
        sb = lambda name, shape, dt=FP32: ctx.enter_context(nc.sbuf_tensor("c_" + name, shape, dt))
        sem = lambda name: ctx.enter_context(nc.semaphore("c_" + name))
        pair = lambda name: [sem(f"{name}{n}") for n in range(2)]
        wo = sb("wo", [P, KC, E])
        wr = sb("wr", [P, KC, EXPERTS])
        g2c = sb("g2c", [P, KC])
        ident = sb("ident", [P, P])
        xn = [sb(f"xn{n}", [P, CT, E]) for n in range(2)]
        z = [sb(f"z{n}", [P, CT, E]) for n in range(2)]
        h = [sb(f"h{n}", [P, CT, E]) for n in range(2)]
        ht = sb("ht", [P, KC, CH])
        junk = sb("junk", [P, CT, E])
        ssq = sb("ssq", [P, CT])
        ms = sb("ms", [P, CT])
        rrms = sb("rrms", [P, CT])
        neghalf = sb("neghalf", [P, CT])
        zeros = sb("zeros", [P, SLOTB, E])
        ps = ctx.enter_context(nc.psum_tensor("c_ps", [P, 8, 512], FP32))
        w_in, consts = sem("w_in"), sem("consts")
        xn_in, z_out, h_out = pair("xn_in"), pair("z_out"), pair("h_out")
        ms_ready, rsq, h_ready, h_flipped, ht_ready = sem("ms_ready"), sem("rsq"), sem("h_ready"), sem("h_flipped"), sem("ht_ready")
        routed, logits_ready, ssq_ready, dump_out = sem("routed"), sem("logits_ready"), sem("ssq_ready"), sem("dump_out")
        heads = HeadsOut(nc, ctx, "c_out", ps, 0, wo, ident, y_d)

        def rows(b, half):
            return bass.ds(b * T + half * CH, CH)

        with nc.Block() as block:

            @block.sync
            def _(sp):
                for dst, src in ((wo[:, :, :], w_o.rearrange("(k p) n -> p k n", p=P)),
                                 (wr[:, :, :], w_router.rearrange("(k p) n -> p k n", p=P)),
                                 (g2c[:, :], g2), (ident[:, :], identity)):
                    sp.dma_start(dst, src).then_inc(w_in, 16)

                def load(b, half):
                    heads.load(sp, b, half)
                    sp.dma_start(xn[half][:, :, :], xn_d[rows(b, half), :].rearrange("(t p) e -> p t e", p=P)
                                 ).then_inc(xn_in[half], 16)

                load(0, 0)
                load(0, 1)
                def turn(b):
                    for half in range(2):
                        sp.wait_ge(h_ready, 2 * b + half + 1)
                        load(b + 1, half)

                looped(sp, B - 1, turn)

            @block.gpsimd
            def _(pool):
                nc.gpsimd.memset(neghalf[:, :], -0.5).then_inc(consts, 1)
                nc.gpsimd.memset(zeros[:, :, :], 0.0).then_inc(consts, 1)
                pool.wait_ge(consts, 2)
                pool.dma_start(z_d[TOK:TOK + SLOTB * P, :].rearrange("(s p) e -> p s e", p=P), zeros[:, :, :]
                               ).then_inc(dump_out, 16)
                def turn(b):
                    for half in range(2):
                        c = 2 * b + half
                        pool.wait_ge(ms_ready, c + 1)
                        nc.gpsimd.tensor_tensor(out=rrms[:, :], in0=ms[:, :], in1=neghalf[:, :],
                                                op=ALU.pow).then_inc(rsq, 1)
                        pool.dma_start(z_d[rows(b, half), :].rearrange("(t p) e -> p t e", p=P), z[half][:, :, :]
                                       ).then_inc(z_out[half], 16)
                        pool.wait_ge(h_ready, c + 1)
                        pool.dma_start(h_d[rows(b, half), 0:E].rearrange("(t p) e -> p t e", p=P), h[half][:, :, :]
                                       ).then_inc(h_out[half], 16)

                looped(pool, B, turn)
                pool.wait_ge(dump_out, 16)
                for half in range(2):
                    pool.wait_ge(z_out[half], 16 * B)
                    pool.wait_ge(h_out[half], 16 * B)

            @block.tensor
            def _(pe):
                pe.wait_ge(w_in, 16 * 4)

                def route(b, half):
                    c = 2 * b + half
                    pe.wait_ge(h_ready, c + 1)
                    pe.wait_ge(logits_ready, c)
                    pe.wait_ge(ht_ready, 2 * c)
                    for k in range(KC):
                        for t in range(CT):
                            last = nc.tensor.transpose(ps[:, 6 + k, t * P:(t + 1) * P],
                                                       h[half][:, t, k * P:(k + 1) * P], ident[:, :])
                    last.then_inc(h_flipped, 1)
                    pe.wait_ge(ht_ready, 2 * c + 2)
                    for t in range(CT):
                        for k in range(KC):
                            last = nc.tensor.matmul(ps[:, 6, t * EXPERTS:(t + 1) * EXPERTS],
                                                    ht[:, k, t * P:(t + 1) * P], wr[:, k, :],
                                                    start=(k == 0), stop=(k == KC - 1))
                    last.then_inc(routed, 1)

                staggered(pe, lambda b, half: heads.tensor(pe, b, half), route)

            @block.scalar
            def _(act):
                act.wait_ge(w_in, 16 * 4)

                def lead(b, half):
                    for t in range(CT):
                        heads.scalar(act, b, half, t)

                def follow(b, half):
                    c = 2 * b + half
                    act.wait_ge(h_flipped, c + 1)
                    act.wait_ge(routed, c)
                    for k in range(KC):
                        nc.scalar.activation(ht[:, k, :], ps[:, 6 + k, :], ACT.Copy,
                                             scale=g2c[:, k:k + 1]).then_inc(ht_ready, 1)

                staggered(act, lead, follow)

            @block.vector
            def _(dve):
                def lead(b, half):
                    c = 2 * b + half
                    dve.wait_ge(xn_in[half], 16 * b + 16)
                    dve.wait_ge(z_out[half], 16 * b)
                    dve.wait_ge(h_out[half], 16 * b)
                    for t in range(CT + 2):
                        if t < CT:
                            heads.vector(dve, b, half, t)
                        if t >= 2:
                            dve.wait_ge(heads.projected, CT * c + t - 1)
                            nc.vector.tensor_tensor(z[half][:, t - 2, :], ps[:, 4 + t % 2, 0:E], xn[half][:, t - 2, :],
                                                    ALU.add).then_inc(heads.taken, 1)
                    dve.wait_ge(heads.taken, CT * (c + 1))
                    for t in range(CT):
                        last = nc.vector.tensor_tensor_reduce(
                            out=junk[:, t, :], in0=z[half][:, t, :], in1=z[half][:, t, :], scale=1.0, scalar=0.0,
                            op0=ALU.mult, op1=ALU.add, accum_out=ssq[:, t:t + 1])
                    last.then_inc(ssq_ready, 1)
                    dve.wait_ge(ssq_ready, c + 1)
                    nc.vector.tensor_scalar(ms[:, :], ssq[:, :], 1.0 / E, RMS_EPS, ALU.mult, ALU.add).then_inc(ms_ready, 1)
                    dve.wait_ge(rsq, c + 1)
                    for t in range(CT):
                        last = nc.vector.tensor_scalar(h[half][:, t, :], z[half][:, t, :], rrms[:, t:t + 1], None,
                                                       ALU.mult)
                    last.then_inc(h_ready, 1)

                def follow(b, half):
                    c = 2 * b + half
                    dve.wait_ge(routed, c + 1)
                    nc.vector.tensor_copy(logits[:, :, bass.ds(b * TT + half * CT, CT)],
                                          ps[:, 6, 0:CT * EXPERTS].rearrange("p (t e) -> p e t", e=EXPERTS)
                                          ).then_inc(logits_ready, 1)

                staggered(dve, lead, follow)


def route(nc, ones_in, upper_in, iota_in, token_parts, slot_rows, h_d, logits, occupied, gather_row, scatter_row):
    N = EXPERTS * TILES
    VALS = 3
    with ExitStack() as ctx:
        sb = lambda name, shape, dt=FP32: ctx.enter_context(nc.sbuf_tensor("d_" + name, shape, dt))
        sem = lambda name: ctx.enter_context(nc.semaphore("d_" + name))
        ones = sb("ones", [P, P])
        upper = sb("upper", [P, P])
        iota_f = sb("iota_f", [P, P])
        iota = sb("iota", [P, P], BF16)
        tparts = sb("tparts", [P, TILES, VALS])
        slots = sb("slots", [P, SLOTB])
        zero = sb("zero", [P, P], BF16)
        probs = sb("probs", [P, EXPERTS, TILES])
        gate = sb("gate", [P, EXPERTS, TILES])
        gate_t = sb("gate_t", [P, TILES, EXPERTS])
        rank = sb("rank", [P, EXPERTS, TILES])
        tmp = sb("tmp", [P, EXPERTS, TILES])
        tmp2 = sb("tmp2", [P, EXPERTS, TILES])
        tied = sb("tied", [P, EXPERTS, TILES])
        chosen = sb("chosen", [P, EXPERTS, TILES])
        total = sb("total", [P, EXPERTS, TILES])
        onesrow = sb("onesrow", [P, TILES])
        top = sb("top", [P, TILES])
        den = sb("den", [P, TILES])
        thr = sb("thr", [P, EXPERTS], I32)
        cand = sb("cand", [P, EXPERTS], I32)
        bit = sb("bit", [P, EXPERTS], I32)
        keep = sb("keep", [P, EXPERTS], I32)
        part = sb("part", [P, EXPERTS])
        need = sb("need", [P, EXPERTS])
        slot = sb("slot", [P, EXPERTS, TILES])
        blk = sb("blk", [P, EXPERTS, TILES])
        slot_t = sb("slot_t", [P, TILES, EXPERTS])
        rhs = sb("rhs", [P, TILES, EXPERTS, SLOTB, VALS], BF16)
        onehot = [sb(f"onehot{n}", [P, EXPERTS, P], BF16) for n in range(2)]
        found = sb("found", [P, EXPERTS, SLOTB, VALS])
        row_f = sb("row_f", [P, EXPERTS, SLOTB])
        row_g = sb("row_g", [P, EXPERTS, SLOTB])
        ps = ctx.enter_context(nc.psum_tensor("d_ps", [P, 4, 512], FP32))
        const_in, steps, exp_ready, gates_out = sem("const_in"), sem("steps"), sem("exp_ready"), sem("gates_out")
        search_steps, counted, cmp_ready = sem("search_steps"), sem("counted"), sem("cmp_ready")
        prefixed, prefix_ask = sem("prefixed"), sem("prefix_ask")
        oh_ready, oh_used, compacted, rhs_ready, gate_ready = sem("oh_ready"), sem("oh_used"), sem("compacted"), sem("rhs_ready"), sem("gate_ready")
        max_sub = sem("max_sub")
        passed = sem("passed")
        BITS = 30
        SEARCH = 5

        def spread(ap, n):
            return ap.rearrange("p (e o) -> p e o", o=1).broadcast_to((P, EXPERTS, n))

        def over_experts(ap):
            return ap.rearrange("p (o t) -> p o t", o=1).broadcast_to((P, EXPERTS, TILES))

        with nc.Block() as block:

            @block.sync
            def _(sp):
                for dst, src in ((ones[:, :], ones_in), (upper[:, :], upper_in), (iota_f[:, :], iota_in),
                                 (tparts[:, :, :], token_parts), (slots[:, :], slot_rows)):
                    sp.dma_start(dst, src).then_inc(const_in, 16)
                sp.wait_ge(gate_ready, 1)
                sp.dma_start(h_d[:, E:E + EXPERTS].rearrange("(t p) e -> p t e", p=P), gate_t[:, :, :]
                             ).then_inc(gates_out, 16)
                sp.wait_ge(gates_out, 16)

            @block.scalar
            def _(act):
                act.wait_ge(max_sub, 1)
                nc.scalar.activation(probs[:, :, :], tmp[:, :, :], ACT.Exp).then_inc(exp_ready, 1)

            @block.tensor
            def _(pe):
                pe.wait_ge(const_in, 16 * 5)
                with pe.Fori(0, BITS) as i:
                    pe.wait_ge(cmp_ready, i + 1)
                    nc.tensor.matmul(ps[:, 0, 0:EXPERTS], ones[:, :], part[:, :], start=True, stop=True
                                     ).then_inc(counted, 1)
                for n, src in enumerate((tmp, tied, chosen)):
                    pe.wait_ge(prefix_ask, n + 1)
                    last = nc.tensor.matmul(ps[:, 1, :], ones[:, :], src[:, :, :].rearrange("p e t -> p (e t)"),
                                            start=True, stop=True)
                    if n:
                        last = nc.tensor.matmul(ps[:, 2, :], upper[:, :], src[:, :, :].rearrange("p e t -> p (e t)"),
                                                start=True, stop=True)
                    last.then_inc(prefixed, 1)
                pe.wait_ge(rhs_ready, 1)
                cols = EXPERTS * SLOTB * VALS
                all_rhs = rhs[:, 0, :, :, :].rearrange("p e a v -> p (e a v)")
                nc.tensor.matmul(ps[:, 3, 0:cols], zero[:, :], all_rhs, start=True, stop=False, skip_group_check=True)
                def turn(i):
                    for n in range(2):
                        pe.wait_ge(oh_ready, 2 * i + n + 1)
                        for e in range(EXPERTS):
                            w = SLOTB * VALS
                            last = nc.tensor.matmul(
                                ps[:, 3, e * w:(e + 1) * w], onehot[n][:, e, :],
                                rhs[:, bass.ds(2 * i + n, 1), e, :, :].rearrange("p t a v -> p (t a v)"),
                                start=False, stop=False, skip_group_check=True)
                        last.then_inc(oh_used, 1)

                looped(pe, TILES // 2, turn)
                nc.tensor.matmul(ps[:, 3, 0:cols], zero[:, :], all_rhs, start=False, stop=True,
                                 skip_group_check=True).then_inc(compacted, 1)

            @block.vector
            def _(dve):
                chain = Chain(dve, steps, 0)
                v = nc.vector
                full = lambda t: t[:, :, :]
                dve.wait_ge(const_in, 16 * 5)
                v.tensor_copy(iota[:, :], iota_f[:, :])
                chain(v.tensor_reduce(top[:, :], logits[:, :, :].rearrange("p e t -> p t e"), AX.X, ALU.max))
                v.tensor_tensor(full(tmp), full(logits), over_experts(top[:, :]), ALU.subtract).then_inc(max_sub, 1)
                dve.wait_ge(exp_ready, 1)
                chain(v.tensor_reduce(den[:, :], probs[:, :, :].rearrange("p e t -> p t e"), AX.X, ALU.add))
                chain(v.reciprocal(den[:, :], den[:, :]))
                chain(v.tensor_tensor(full(probs), full(probs), over_experts(den[:, :]), ALU.mult))
                chain(v.memset(full(rank), 0.0))
                for d in range(1, EXPERTS):
                    lo, hi = probs[:, 0:EXPERTS - d, :], probs[:, d:EXPERTS, :]
                    n = EXPERTS - d
                    v.tensor_tensor(tmp[:, 0:n, :], hi, lo, ALU.is_gt)
                    chain(v.tensor_tensor(tmp2[:, 0:n, :], hi, lo, ALU.is_le))
                    chain(v.tensor_tensor(rank[:, 0:n, :], rank[:, 0:n, :], tmp[:, 0:n, :], ALU.add))
                    chain(v.tensor_tensor(rank[:, d:EXPERTS, :], rank[:, d:EXPERTS, :], tmp2[:, 0:n, :], ALU.add))
                chain(v.tensor_scalar(full(tmp), full(rank), 1.5, None, ALU.is_lt))
                chain(v.tensor_scalar(full(tmp2), full(tmp), 1.0, None, ALU.subtract))
                chain(v.tensor_tensor(full(gate), full(probs), full(tmp), ALU.mult))
                chain(v.tensor_tensor(full(gate), full(gate), full(tmp2), ALU.add))
                v.tensor_copy(gate_t[:, :, :], gate[:, :, :].rearrange("p e t -> p t e")).then_inc(gate_ready, 1)
                v.memset(thr[:, :], 0)
                v.memset(onesrow[:, :], 1.0)
                v.memset(zero[:, :], 0.0)
                chain(v.memset(bit[:, :], 1 << (BITS - 1)))
                with dve.Fori(0, BITS) as i:
                    search = Chain(dve, search_steps, SEARCH * i)
                    search(v.tensor_tensor(cand[:, :], thr[:, :], bit[:, :], ALU.bitwise_or))
                    search(v.tensor_tensor(full(tmp), full(gate), spread(cand[:, :].bitcast(FP32), TILES), ALU.is_ge))
                    v.tensor_reduce(part[:, :], full(tmp), AX.X, ALU.add).then_inc(cmp_ready, 1)
                    search(v.tensor_single_scalar(bit[:, :], bit[:, :], 1, ALU.logical_shift_right))
                    dve.wait_ge(counted, i + 1)
                    search(v.tensor_scalar(keep[:, :], ps[:, 0, 0:EXPERTS], CAP - 0.5, None, ALU.is_ge))
                    dve.sem_inc(passed, 1)
                    search(v.copy_predicated(thr[:, :], keep[:, :], cand[:, :]))
                    assert search.n == SEARCH
                limit = spread(thr[:, :].bitcast(FP32), TILES)
                v.tensor_tensor(full(tmp), full(gate), limit, ALU.is_gt)
                chain(v.tensor_tensor(full(tied), full(gate), limit, ALU.is_equal))

                def running(n, out):
                    dve.wait_ge(prefixed, n + 1)
                    chain(v.tensor_copy(total[:, :, :].rearrange("p e t -> p (e t)"), ps[:, 1, :]))
                    for e in range(EXPERTS):
                        last = v.tensor_tensor_scan(out[:, e, :], onesrow[:, :], total[:, e, :], 0.0, ALU.mult, ALU.add)
                    chain(last)
                    chain(v.tensor_tensor(full(out), full(out), full(total), ALU.subtract))
                    chain(v.tensor_tensor(full(out).rearrange("p e t -> p (e t)"), ps[:, 2, :],
                                          full(out).rearrange("p e t -> p (e t)"), ALU.add))

                v.tensor_copy(part[:, :], part[:, :]).then_inc(prefix_ask, 1)
                dve.wait_ge(prefixed, 1)
                chain(v.tensor_reduce(need[:, :], ps[:, 1, :].rearrange("p (e t) -> p e t", t=TILES), AX.X, ALU.add))
                chain(v.tensor_scalar(need[:, :], need[:, :], -1.0, CAP + 0.5, ALU.mult, ALU.add))
                v.tensor_copy(part[:, :], part[:, :]).then_inc(prefix_ask, 1)
                running(1, slot)
                chain(v.tensor_tensor(full(slot), full(slot), spread(need[:, :], TILES), ALU.is_lt))
                chain(v.tensor_tensor(full(slot), full(slot), full(tied), ALU.mult))
                v.tensor_tensor(full(chosen), full(slot), full(tmp), ALU.add).then_inc(prefix_ask, 1)
                running(2, slot)
                chain(v.tensor_tensor(full(slot), full(slot), full(chosen), ALU.mult))
                chain(v.tensor_scalar(full(slot), full(slot), 1.0, None, ALU.subtract))
                chain(v.tensor_scalar(full(blk), full(slot), P - 0.5, None, ALU.is_ge))
                for a in range(2, SLOTB):
                    chain(v.tensor_scalar(full(tmp), full(slot), a * P - 0.5, None, ALU.is_ge))
                    chain(v.tensor_tensor(full(blk), full(blk), full(tmp), ALU.add))
                chain(v.tensor_scalar(full(tmp), full(blk), -float(P), None, ALU.mult))
                chain(v.tensor_tensor(slot_t[:, :, :].rearrange("p t e -> p e t"), full(slot), full(tmp), ALU.add))
                for a in range(SLOTB):
                    chain(v.tensor_scalar(full(tmp), full(blk), float(a), None, ALU.is_equal))
                    for n in range(VALS):
                        last = v.tensor_tensor(rhs[:, :, :, a, n].rearrange("p t e -> p e t"), full(tmp),
                                               over_experts(tparts[:, :, n]), ALU.mult)
                    chain(last)
                v.tensor_copy(part[:, :], part[:, :]).then_inc(rhs_ready, 1)
                def turn(i):
                    for n in range(2):
                        dve.wait_ge(oh_used, 2 * i)
                        for e in range(EXPERTS):
                            last = v.tensor_scalar(onehot[n][:, e, :], iota[:, :],
                                                   slot_t[:, bass.ds(2 * i + n, 1), e], None, ALU.is_equal)
                        last.then_inc(oh_ready, 1)

                looped(dve, TILES // 2, turn)
                dve.wait_ge(compacted, 1)
                cols = EXPERTS * SLOTB * VALS
                chain(v.tensor_copy(found[:, :, :, :].rearrange("p e a v -> p (e a v)"), ps[:, 3, 0:cols]))
                chain(v.tensor_scalar(full(row_f), found[:, :, :, 1], float(P), None, ALU.mult))
                chain(v.tensor_tensor(full(row_f), full(row_f), found[:, :, :, 2], ALU.add))
                v.tensor_copy(full(gather_row), full(row_f))
                chain(v.tensor_copy(full(occupied), found[:, :, :, 0]))
                chain(v.tensor_scalar(full(row_g), full(occupied), -1.0, 1.0, ALU.mult, ALU.add))
                chain(v.tensor_tensor(full(row_g), full(row_g),
                                      slots[:, :].rearrange("p (o a) -> p o a", o=1)
                                      .broadcast_to((P, EXPERTS, SLOTB)), ALU.mult))
                chain(v.tensor_tensor(full(row_g), full(row_g), full(row_f), ALU.add))
                chain(v.tensor_copy(full(scatter_row), full(row_g)))


def experts(nc, w1_in, w2_in, g2, identity, h_d, z_d, occupied, gather_row, scatter_row):
    FC = FFN // P
    HW = E + EXPERTS
    size = [min(P, CAP - s * P) for s in range(SLOTB)]
    with ExitStack() as ctx:
        sb = lambda name, shape, dt=FP32: ctx.enter_context(nc.sbuf_tensor("e_" + name, shape, dt))
        sem = lambda name: ctx.enter_context(nc.semaphore("e_" + name))
        pair = lambda name: [sem(f"{name}{n}") for n in range(2)]
        ident = sb("ident", [P, P])
        g2c = sb("g2c", [P, KC])
        w1 = [sb(f"w1{n}", [P, KC, FFN]) for n in range(2)]
        w2 = [sb(f"w2{n}", [P, FC, E]) for n in range(2)]
        xe = [sb(f"xe{n}", [P, SLOTB, HW]) for n in range(2)]
        xet = sb("xet", [P, KC, CAP])
        ht = sb("ht", [P, FC, CAP])
        gates = [sb(f"gates{n}", [P, SLOTB]) for n in range(2)]
        ye = [sb(f"ye{n}", [P, SLOTB, E]) for n in range(2)]
        ps = ctx.enter_context(nc.psum_tensor("e_ps", [P, 8, 512], FP32))
        const_in, w_in, xe_in, added = sem("const_in"), pair("w_in"), pair("xe_in"), sem("added")
        flipped, xet_ready, up, ht_ready = sem("flipped"), sem("xet_ready"), sem("up"), sem("ht_ready")
        down, gates_ready, ye_ready = sem("down"), sem("gates_ready"), sem("ye_ready")

        with nc.Block() as block:

            @block.sync
            def _(sp):
                sp.dma_start(ident[:, :], identity).then_inc(const_in, 16)
                sp.dma_start(g2c[:, :], g2).then_inc(const_in, 16)
                def turn(i):
                    for n in range(2):
                        sp.wait_ge(down, SLOTB * 2 * i)
                        sp.dma_start(w1[n][:, :, :], w1_in[2 * i + n, :, :].rearrange("(k p) f -> p k f", p=P)
                                     ).then_inc(w_in[n], 16)
                        sp.dma_start(w2[n][:, :, :], w2_in[2 * i + n, :, :].rearrange("(k p) f -> p k f", p=P)
                                     ).then_inc(w_in[n], 16)

                looped(sp, EXPERTS // 2, turn)

            @block.gpsimd
            def _(pool):
                def gather(e):
                    if e >= 2:
                        pool.wait_ge(flipped, e - 1)
                        pool.wait_ge(gates_ready, e - 1)
                    for s in range(SLOTB):
                        pool.indirect_dma_start(
                            out=xe[e % 2][0:size[s], s, :], out_offset=None, in_=h_d[:, :],
                            in_offset=bass.IndirectOffsetOnAxis(ap=gather_row[0:size[s], e, s:s + 1], axis=0),
                        ).then_inc(xe_in[e % 2], 16)

                gather(0)
                for e in range(EXPERTS):
                    if e + 1 < EXPERTS:
                        gather(e + 1)
                    pool.wait_ge(ye_ready, SLOTB * (e + 1))
                    if e:
                        pool.wait_ge(added, 16 * SLOTB * e)
                    for s in range(SLOTB):
                        pool.indirect_dma_start(
                            out=z_d[:, :],
                            out_offset=bass.IndirectOffsetOnAxis(ap=scatter_row[0:size[s], e, s:s + 1], axis=0),
                            in_=ye[e % 2][0:size[s], s, :], in_offset=None, compute_op=ALU.add,
                        ).then_inc(added, 16)
                pool.wait_ge(added, 16 * SLOTB * EXPERTS)

            @block.tensor
            def _(pe):
                pe.wait_ge(const_in, 32)
                def turn(i):
                    for n in range(2):
                        e = 2 * i + n
                        pe.wait_ge(xe_in[n], 16 * SLOTB * (i + 1))
                        pe.wait_ge(xet_ready, KC * e)
                        for k in range(KC):
                            for s in range(SLOTB):
                                last = nc.tensor.transpose(ps[:, k, s * P:s * P + size[s]],
                                                           xe[n][0:size[s], s, k * P:(k + 1) * P],
                                                           ident[0:size[s], 0:size[s]])
                        last.then_inc(flipped, 1)
                        pe.wait_ge(w_in[n], 32 * (i + 1))
                        pe.wait_ge(xet_ready, KC * e + KC)
                        for f in range(FC):
                            pe.wait_ge(ht_ready, FC * e + max(f - 1, 0))
                            for k in range(KC):
                                last = nc.tensor.matmul(ps[:, 2 + f % 2, 0:CAP], w1[n][:, k, f * P:(f + 1) * P],
                                                        xet[:, k, :], start=(k == 0), stop=(k == KC - 1))
                            last.then_inc(up, 1)
                        pe.wait_ge(ht_ready, FC * (e + 1))
                        pe.wait_ge(ye_ready, SLOTB * e)
                        for s in range(SLOTB):
                            for f in range(FC):
                                last = nc.tensor.matmul(ps[0:size[s], 4 + s, 0:E], ht[:, f, s * P:s * P + size[s]],
                                                        w2[n][:, f, :], start=(f == 0), stop=(f == FC - 1))
                            last.then_inc(down, 1)

                looped(pe, EXPERTS // 2, turn)

            @block.scalar
            def _(act):
                act.wait_ge(const_in, 32)
                def turn(i):
                    for n in range(2):
                        e = 2 * i + n
                        act.wait_ge(flipped, e + 1)
                        act.wait_ge(up, FC * e)
                        for k in range(KC):
                            nc.scalar.activation(xet[:, k, :], ps[:, k, 0:CAP], ACT.Copy,
                                                 scale=g2c[:, k:k + 1]).then_inc(xet_ready, 1)
                        act.wait_ge(down, SLOTB * e)
                        for f in range(FC):
                            act.wait_ge(up, FC * e + f + 1)
                            nc.scalar.activation(ht[:, f, :], ps[:, 2 + f % 2, 0:CAP], ACT.Relu).then_inc(ht_ready, 1)

                looped(act, EXPERTS // 2, turn)

            @block.vector
            def _(dve):
                def turn(i):
                    for n in range(2):
                        e = 2 * i + n
                        dve.wait_ge(xe_in[n], 16 * SLOTB * (i + 1))
                        full, rest = SLOTB - 1, size[-1]
                        nc.vector.tensor_tensor(gates[n][:, 0:full], xe[n][:, 0:full, bass.ds(E + e, 1)]
                                                .rearrange("p s o -> p (s o)"),
                                                occupied[:, bass.ds(e, 1), 0:full].rearrange("p o s -> p (o s)"), ALU.mult)
                        nc.vector.tensor_tensor(gates[n][0:rest, full:], xe[n][0:rest, full:, bass.ds(E + e, 1)]
                                                .rearrange("p s o -> p (s o)"),
                                                occupied[0:rest, bass.ds(e, 1), full:].rearrange("p o s -> p (o s)"),
                                                ALU.mult).then_inc(gates_ready, 1)
                        dve.wait_ge(gates_ready, e + 1)
                        dve.wait_ge(added, 16 * SLOTB * 2 * i)
                        for s in range(SLOTB):
                            dve.wait_ge(down, SLOTB * e + s + 1)
                            nc.vector.tensor_scalar(ye[n][0:size[s], s, :], ps[0:size[s], 4 + s, 0:E],
                                                    gates[n][0:size[s], s:s + 1], None,
                                                    ALU.mult).then_inc(ye_ready, 1)

                looped(dve, EXPERTS // 2, turn)


def finish(nc, x, w_out_t, bo_rows, identity, y_d, z_d, out):
    with ExitStack() as ctx:
        sb = lambda name, shape, dt=FP32: ctx.enter_context(nc.sbuf_tensor("f_" + name, shape, dt))
        sem = lambda name: ctx.enter_context(nc.semaphore("f_" + name))
        pair = lambda name: [sem(f"{name}{n}") for n in range(2)]
        wo = sb("wo", [P, KC, E])
        bo = sb("bo", [P, E])
        ident = sb("ident", [P, P])
        xin = [sb(f"x{n}", [P, CT, E]) for n in range(2)]
        z = [sb(f"z{n}", [P, CT, E]) for n in range(2)]
        g = [sb(f"g{n}", [P, CT, E]) for n in range(2)]
        s_sb = [sb(f"s{n}", [P, CT, E]) for n in range(2)]
        res = [sb(f"res{n}", [P, CT, E]) for n in range(2)]
        ps = ctx.enter_context(nc.psum_tensor("f_ps", [P, 6, 512], FP32))
        w_in, x_in, z_in, out_out = sem("w_in"), pair("x_in"), pair("z_in"), pair("out_out")
        g_ready, gated, res_ready = sem("g_ready"), sem("gated"), sem("res_ready")
        heads = HeadsOut(nc, ctx, "f_out", ps, 1, wo, ident, y_d)

        def rows(b, half):
            return bass.ds(b * T + half * CH, CH)

        with nc.Block() as block:

            @block.sync
            def _(sp):
                for dst, src in ((wo[:, :, :], w_out_t.rearrange("(k p) n -> p k n", p=P)),
                                 (bo[:, :], bo_rows.broadcast_to((P, E))), (ident[:, :], identity)):
                    sp.dma_start(dst, src).then_inc(w_in, 16)

                def load(b, half):
                    heads.load(sp, b, half)
                    for dst, src, s in ((xin, x, x_in), (z, z_d, z_in)):
                        sp.dma_start(dst[half][:, :, :], src[rows(b, half), :].rearrange("(t p) e -> p t e", p=P)
                                     ).then_inc(s[half], 16)

                load(0, 0)
                load(0, 1)
                def turn(b):
                    for half in range(2):
                        sp.wait_ge(res_ready, 2 * b + half + 1)
                        load(b + 1, half)

                looped(sp, B - 1, turn)

            @block.gpsimd
            def _(pool):
                def turn(b):
                    for half in range(2):
                        pool.wait_ge(res_ready, 2 * b + half + 1)
                        pool.dma_start(out[rows(b, half), :].rearrange("(t p) e -> p t e", p=P), res[half][:, :, :]
                                       ).then_inc(out_out[half], 16)

                looped(pool, B, turn)
                for half in range(2):
                    pool.wait_ge(out_out[half], 16 * B)

            @block.tensor
            def _(pe):
                pe.wait_ge(w_in, 16 * 3)
                def turn(b):
                    for half in range(2):
                        heads.tensor(pe, b, half)

                looped(pe, B, turn)

            @block.scalar
            def _(act):
                def turn(b):
                    for half in range(2):
                        act.wait_ge(z_in[half], 16 * b + 16)
                        nc.scalar.activation(g[half][:, :, :], z[half][:, :, :], ACT.Silu).then_inc(g_ready, 1)
                        for t in range(CT):
                            heads.scalar(act, b, half, t)

                looped(act, B, turn)

            @block.vector
            def _(dve):
                dve.wait_ge(w_in, 16 * 3)
                def turn(b):
                    for half in range(2):
                        c = 2 * b + half
                        dve.wait_ge(x_in[half], 16 * b + 16)
                        dve.wait_ge(out_out[half], 16 * b)
                        for t in range(CT + 2):
                            if t < CT:
                                heads.vector(dve, b, half, t)
                            if t >= 2:
                                dve.wait_ge(heads.projected, CT * c + t - 1)
                                nc.vector.tensor_tensor(s_sb[half][:, t - 2, :], ps[:, 4 + t % 2, 0:E], bo[:, :],
                                                        ALU.add).then_inc(heads.taken, 1)
                        dve.wait_ge(heads.taken, CT * (c + 1))
                        dve.wait_ge(g_ready, c + 1)
                        nc.vector.tensor_tensor(s_sb[half][:, :, :], s_sb[half][:, :, :], g[half][:, :, :],
                                                ALU.mult).then_inc(gated, 1)
                        dve.wait_ge(gated, c + 1)
                        nc.vector.tensor_tensor(res[half][:, :, :], s_sb[half][:, :, :], xin[half][:, :, :],
                                                ALU.add).then_inc(res_ready, 1)

                looped(dve, B, turn)


def program(nc, x, w_main_t, w_out_t, bo, g1, w_qkv, w_o, g2, w_router, w1, w2, rope_main, rope_head, identity,
            causal_mask, ones, upper, iota, token_parts, slot_rows, out):
    scratch = lambda name, shape, dt=FP32: nc.dram_tensor(name, shape, dt, kind="Internal").ap()
    xn_d = scratch("xn_scratch", (TOK, E))
    qk_d = scratch("qk_scratch", (UNITS, 2, PARTS, GH * HD, T), BF16)
    v_d = scratch("v_scratch", (UNITS, T, GH * VW))
    y_d = scratch("y_scratch", (UNITS, P, T))
    z_d = scratch("z_scratch", (TOK + SLOTB * P, E))
    h_d = scratch("h_scratch", (TOK, E + EXPERTS))
    project(nc, x, w_main_t, w_qkv, g1, rope_main, rope_head, identity, xn_d, qk_d, v_d)
    attend(nc, identity, causal_mask, qk_d, v_d, y_d)
    with ExitStack() as ctx:
        keep = lambda name, shape, dt=FP32: ctx.enter_context(nc.sbuf_tensor(name, shape, dt))
        logits = keep("logits", [P, EXPERTS, TILES])
        occupied = keep("occupied", [P, EXPERTS, SLOTB])
        gather_row = keep("gather_row", [P, EXPERTS, SLOTB], U32)
        scatter_row = keep("scatter_row", [P, EXPERTS, SLOTB], U32)
        block_mid(nc, w_o, w_router, g2, identity, xn_d, y_d, z_d, h_d, logits)
        route(nc, ones, upper, iota, token_parts, slot_rows, h_d, logits, occupied, gather_row, scatter_row)
        experts(nc, w1, w2, g2, identity, h_d, z_d, occupied, gather_row, scatter_row)
    finish(nc, x, w_out_t, bo, identity, y_d, z_d, out)


def _constants(np):
    def rotary(width, exponents):
        theta = np.repeat((10000.0 ** exponents).astype(np.float32), 2)
        angle = (np.arange(T, dtype=np.float32)[:, None] * theta[None, :]).astype(np.float64)
        sign = np.where(np.arange(width) % 2 == 0, -1.0, 1.0)
        return np.stack([np.cos(angle), np.sin(angle) * sign]).astype(np.float32)

    row, col = np.arange(P)[:, None], np.arange(P)[None, :]
    eye = (row == col).astype(np.float32)
    mask = np.zeros((P, 512), np.float32)
    mask[:, 512 - P:] = np.where(col > row, -BIG, 0.0)
    parts = np.zeros((P, TILES, 3), np.float32)
    parts[:, :, 0] = 1.0
    parts[:, :, 1] = np.arange(TILES)[None, :]
    parts[:, :, 2] = np.arange(P)[:, None]
    return {
        "rope_main": rotary(E, -np.arange(0, E, 2) / E),
        "rope_head": rotary(HD, -2.0 * np.arange(HD // 2) / HD),
        "identity": eye,
        "causal_mask": mask,
        "ones": np.ones((P, P), np.float32),
        "upper": (col >= row).astype(np.float32),
        "iota": np.broadcast_to(col, (P, P)).astype(np.float32),
        "token_parts": parts,
        "slot_rows": (TOK + np.arange(SLOTB)[None, :] * P + np.arange(P)[:, None]).astype(np.float32),
    }


def kernel(**inputs):
    import numpy as np
    import concourse.bacc as bacc
    from concourse.bass_utils import run_bass_kernel_spmd

    a = {k: np.asarray(v) for k, v in inputs.items()}
    columns = lambda v: np.ascontiguousarray(v.reshape(KC, P).T)
    arrays = {
        "x": a["L0_attn_input"].reshape(TOK, E),
        "w_main_t": np.concatenate([a["L0_attn_Wq"].T, a["L0_attn_Wk"].T, a["L0_attn_Wv"].T], axis=1),
        "w_out_t": np.ascontiguousarray(a["L0_attn_Wo"].T),
        "bo": a["L0_attn_bo"].reshape(1, E),
        "g1": columns(a["L0_ffn_g1"]),
        "w_qkv": a["L0_ffn_w_qkv"],
        "w_o": a["L0_ffn_w_o"],
        "g2": columns(a["L0_ffn_g2"]),
        "w_router": a["L0_ffn_w_router"],
        "w1": a["L0_ffn_w1"],
        "w2": a["L0_ffn_w2"],
        **_constants(np),
    }
    nc = bacc.Bacc("TRN2", target_bir_lowering=False, num_devices=1)
    args, maps = [], {}
    for name, array in arrays.items():
        maps[f"in_{name}"] = np.ascontiguousarray(array)
        args.append(nc.dram_tensor(f"in_{name}", array.shape, mybir.dt.from_np(array.dtype), kind="ExternalInput").ap())
    args.append(nc.dram_tensor("out_y", (TOK, E), FP32, kind="ExternalOutput").ap())
    program(nc, *args)
    result = run_bass_kernel_spmd(nc, [maps], core_ids=[0])
    return result.results[0]["out_y"].reshape(B, T, E)
```

```python
from contextlib import ExitStack

import concourse.bass as bass
from concourse import mybir

FP32, BF16 = mybir.dt.float32, mybir.dt.bfloat16
I32, U32 = mybir.dt.int32, mybir.dt.uint32
ALU = mybir.AluOpType
ACT = mybir.ActivationFunctionType
AX = mybir.AxisListType

B, T, E = 8, 1024, 256
TOK = B * T
P = 128
HEADS, HD = 16, 16
GROUPS, GH = 4, 4
KC = E // P
CH = 512
CT = CH // P
TT = T // P
TILES = TOK // P
UNITS = 2 * B * GROUPS
UB = B * GROUPS
VW = 32
PARTS = 3
Q_PART = (0, 0, 1, 1, 0, 2)
K_PART = (0, 1, 0, 1, 2, 0)
BANDS = len(Q_PART)
SROWS = BANDS * HD
EXPERTS, FFN, CAP = 8, 512, 320
SLOTB = (CAP + P - 1) // P
LN_EPS, RMS_EPS = 1e-5, 1e-6
BIG = 3e38


def apart(engine, sem, value, passed):
    engine.wait_ge(sem, value)
    engine.sem_inc(passed, 1)


def looped(engine, count, body):
    body(0)
    with engine.Fori(1, count) as i:
        body(i)


class Chain:

    def __init__(self, engine, sem, base):
        self.engine, self.sem, self.base, self.n = engine, sem, base, 0

    def __call__(self, instruction):
        self.n += 1
        instruction.then_inc(self.sem, 1)
        self.engine.wait_ge(self.sem, self.base + self.n)


NORM_STEPS = 6


def project(nc, x, w_main_t, w_qkv, g1, rope_main, rope_head, identity, xn_d, qk_d, v_d):
    with ExitStack() as ctx:
        sb = lambda name, shape, dt=FP32: ctx.enter_context(nc.sbuf_tensor("a_" + name, shape, dt))
        sem = lambda name: ctx.enter_context(nc.semaphore("a_" + name))
        pair = lambda name: [sem(f"{name}{n}") for n in range(2)]

        w1 = sb("w1", [P, KC, 3 * E])
        w2 = sb("w2", [P, KC, 3 * E])
        g1c = sb("g1c", [P, KC])
        ident = sb("ident", [P, P])
        cs1 = sb("cs1", [P, 2, TT, E])
        cs2 = sb("cs2", [P, 2, TT, HD])
        xin = [sb(f"xin{n}", [P, CT, E]) for n in range(2)]
        xn = [sb(f"xn{n}", [P, CT, E]) for n in range(2)]
        xr = [sb(f"xr{n}", [P, CT, E]) for n in range(2)]
        rx = [sb(f"rx{n}", [P, CT, E]) for n in range(2)]
        rope_a = sb("rope_a", [P, CT, E])
        rope_b = sb("rope_b", [P, CT, E])
        junk = sb("junk", [P, CT, E])
        stats = sb("stats", [P, CT, 6])
        mv = sb("mv", [P, CT, 2])
        var = sb("var", [P, CT])
        rstd = sb("rstd", [P, CT])
        ssq = sb("ssq", [P, CT])
        ms = sb("ms", [P, CT])
        rrms = sb("rrms", [P, CT])
        neghalf = sb("neghalf", [P, CT])
        xt = [sb(f"xt{n}", [P, 3, KC, CH]) for n in range(2)]
        qkr = sb("qkr", [P, CT, 2 * E])
        ra = sb("ra", [P, 2, 2 * E])
        rb = sb("rb", [P, 2, 2 * E])
        parts = [sb(f"parts{n}", [P, PARTS, CH], BF16) for n in range(2)]
        rest = [sb(f"rest{n}", [P, CH]) for n in range(2)]
        vst = [sb(f"vst{n}", [P, 2, CT, HEADS, VW]) for n in range(2)]
        ps = ctx.enter_context(nc.psum_tensor("a_ps", [P, 8, 512], FP32))

        w_in = sem("w_in")
        x_in = pair("x_in")
        xn_out = pair("xn_out")
        qk_out = pair("qk_out")
        v_out = pair("v_out")
        consts = sem("consts")
        vconst = sem("vconst")
        w_ready = sem("w_ready")
        var_ready = sem("var_ready")
        rsq = sem("rsq")
        dchain = sem("dchain")
        passed = sem("passed")
        normed = sem("normed")
        flipped = sem("flipped")
        xt_ready = sem("xt_ready")
        proj = sem("proj")
        rel_dve = sem("rel_dve")
        rel_act = sem("rel_act")
        rotated = sem("rotated")
        hi_ready = sem("hi_ready")
        rest_ready = sem("rest_ready")
        mid_ready = sem("mid_ready")
        lo_ready = pair("lo_ready")

        def chunk_rows(b, half):
            return bass.ds(b * T + half * CH, CH)

        with nc.Block() as block:

            @block.sync
            def _(sp):
                for dst, src in ((w1[:, :, :], w_main_t.rearrange("(k p) n -> p k n", p=P)),
                                 (w2[:, :, :], w_qkv.rearrange("(k p) n -> p k n", p=P)),
                                 (g1c[:, :], g1),
                                 (ident[:, :], identity),
                                 (cs1[:, :, :, :], rope_main.rearrange("c (t p) e -> p c t e", p=P)),
                                 (cs2[:, :, :, :], rope_head.rearrange("c (t p) e -> p c t e", p=P))):
                    sp.dma_start(dst, src).then_inc(w_in, 16)

                def store(b, half):
                    c = 2 * b + half
                    sp.wait_ge(normed, c + 1)
                    sp.dma_start(xn_d[chunk_rows(b, half), :].rearrange("(t p) e -> p t e", p=P),
                                 xn[half][:, :, :]).then_inc(xn_out[half], 16)
                    sp.wait_ge(rel_act, CT * c + CT)
                    for a in range(2):
                        for g in range(GROUPS):
                            unit = b * GROUPS + (a * UB + g)
                            sp.dma_start(
                                v_d[unit, half * CH:(half + 1) * CH, :].rearrange("(t p) n -> p t n", p=P),
                                vst[half][:, a, :, g * GH:(g + 1) * GH, :].rearrange("p t h v -> p t (h v)"),
                            ).then_inc(v_out[half], 16)
                    for n in range(8):
                        a, m = 1 - n // 4, n % 4
                        sp.wait_ge(lo_ready[n % 2], 4 * c + n // 2 + 1)
                        for gi in range(2):
                            unit = b * GROUPS + (a * UB + 2 * (m % 2) + gi)
                            sp.dma_start(
                                qk_d[unit, m // 2, :, :, half * CH:(half + 1) * CH].rearrange("s r t -> r s t"),
                                parts[n % 2][64 * gi:64 * gi + 64, :, :],
                            ).then_inc(qk_out[n % 2], 16)

                def turn(b):
                    for half in range(2):
                        store(b, half)

                looped(sp, B, turn)
                for half in range(2):
                    sp.wait_ge(xn_out[half], 16 * B)
                    sp.wait_ge(v_out[half], 16 * 2 * GROUPS * B)
                    sp.wait_ge(qk_out[half], 16 * 2 * 4 * 2 * B)

            @block.gpsimd
            def _(pool):
                nc.gpsimd.memset(neghalf[:, :], -0.5).then_inc(consts, 1)
                for n in range(2):
                    nc.gpsimd.memset(vst[n][:, :, :, :, HD + 1:VW], 0.0).then_inc(vconst, 1)
                    nc.gpsimd.memset(vst[n][:, :, :, :, HD:HD + 1], 1.0).then_inc(vconst, 1)
                pool.wait_ge(consts, 1)

                def load(b, half):
                    pool.dma_start(xin[half][:, :, :],
                                   x[chunk_rows(b, half), :].rearrange("(t p) e -> p t e", p=P)
                                   ).then_inc(x_in[half], 16)

                def roots(c):
                    pool.wait_ge(var_ready, 2 * c + 1)
                    nc.gpsimd.tensor_tensor(out=rstd[:, :], in0=var[:, :], in1=neghalf[:, :],
                                            op=ALU.pow).then_inc(rsq, 1)
                    pool.wait_ge(var_ready, 2 * c + 2)
                    nc.gpsimd.tensor_tensor(out=rrms[:, :], in0=ms[:, :], in1=neghalf[:, :],
                                            op=ALU.pow).then_inc(rsq, 1)

                def lows(c):
                    for n in range(8):
                        s = n % 2
                        pool.wait_ge(mid_ready, 8 * c + n + 1)
                        nc.gpsimd.tensor_tensor(out=parts[s][:, 2, :], in0=rest[s][:, :], in1=parts[s][:, 1, :],
                                                op=ALU.subtract).then_inc(lo_ready[s], 1)

                def step(b, half):
                    c = 2 * b + half
                    roots(c + 1)
                    load(b + 1, half)
                    lows(c)

                load(0, 0)
                load(0, 1)
                roots(0)
                def turn(b):
                    for half in range(2):
                        step(b, half)

                looped(pool, B - 1, turn)
                roots(2 * B - 1)
                lows(2 * B - 2)
                lows(2 * B - 1)

            @block.vector
            def _(dve):
                dve.wait_ge(w_in, 16 * 6)
                for k in range(KC):
                    nc.vector.tensor_scalar(w2[:, k, :], w2[:, k, :], g1c[:, k:k + 1], None,
                                            ALU.mult).then_inc(w_ready, 1)
                dve.wait_ge(w_ready, KC)
                nc.vector.tensor_scalar(w1[:, :, 0:E], w1[:, :, 0:E], 0.25, None, ALU.mult).then_inc(w_ready, 1)
                nc.vector.tensor_scalar(w2[:, :, 0:E], w2[:, :, 0:E], 0.25, None, ALU.mult).then_inc(w_ready, 1)

                def norms(b, half, first=False):
                    c = 2 * b + half
                    chain = Chain(dve, dchain, c * NORM_STEPS)
                    dve.wait_ge(x_in[half], 16 * b + 16)
                    if not first:
                        dve.wait_ge(flipped, CT * (c - 1))
                        dve.wait_ge(xn_out[half], 16 * b)
                    for t in range(CT):
                        last = nc.vector.bn_stats(stats[:, t, :], xin[half][:, t, :])
                    chain(last)
                    dve.sem_inc(passed, 1)
                    for t in range(CT):
                        last = nc.vector.bn_aggr(mv[:, t, :], stats[:, t, :])
                    chain(last)
                    nc.vector.tensor_scalar(var[:, :], mv[:, :, 1], LN_EPS, None, ALU.add).then_inc(var_ready, 1)
                    dve.wait_ge(rsq, 2 * c + 1)
                    for t in range(CT):
                        last = nc.vector.tensor_scalar(xn[half][:, t, :], xin[half][:, t, :], mv[:, t, 0:1],
                                                       rstd[:, t:t + 1], ALU.subtract, ALU.mult)
                    chain(last)
                    for t in range(CT):
                        last = nc.vector.tensor_tensor_reduce(
                            out=junk[:, t, :], in0=xn[half][:, t, :], in1=xn[half][:, t, :], scale=1.0, scalar=0.0,
                            op0=ALU.mult, op1=ALU.add, accum_out=ssq[:, t:t + 1])
                    chain(last)
                    nc.vector.tensor_scalar(ms[:, :], ssq[:, :], 1.0 / E, RMS_EPS, ALU.mult,
                                            ALU.add).then_inc(var_ready, 1)
                    cos = cs1[:, 0, half * CT:(half + 1) * CT, :]
                    sin = cs1[:, 1, half * CT:(half + 1) * CT, :]
                    nc.vector.tensor_tensor(rope_a[:, :, :], xn[half][:, :, :], cos, ALU.mult)
                    for o in range(2):
                        last = nc.vector.tensor_tensor(rope_b[:, :, o::2], xn[half][:, :, 1 - o::2],
                                                       sin[:, :, o::2], ALU.mult)
                    chain(last)
                    chain(nc.vector.tensor_tensor(rx[half][:, :, :], rope_a[:, :, :], rope_b[:, :, :], ALU.add))
                    dve.wait_ge(rsq, 2 * c + 2)
                    for t in range(CT):
                        last = nc.vector.tensor_scalar(xr[half][:, t, :], xn[half][:, t, :], rrms[:, t:t + 1],
                                                       None, ALU.mult)
                    last.then_inc(normed, 1)
                    assert chain.n == NORM_STEPS

                def rotate(b, half):
                    c = 2 * b + half
                    for t in range(CT):
                        dve.wait_ge(proj, 16 * c + 2 * t + 1)
                        qk = ps[:, 4 + (2 * t) % 4, :].rearrange("p (h d) -> p h d", d=HD)
                        cos = cs2[:, 0, half * CT + t, :].rearrange("p (o d) -> p o d", o=1).broadcast_to((P, 2 * HEADS, HD))
                        sin = cs2[:, 1, half * CT + t, :].rearrange("p (o d) -> p o d", o=1).broadcast_to((P, 2 * HEADS, HD))
                        ra_v = ra[:, t % 2, :].rearrange("p (h d) -> p h d", d=HD)
                        rb_v = rb[:, t % 2, :].rearrange("p (h d) -> p h d", d=HD)
                        if t != 1:
                            dve.wait_ge(rotated, CT * c + max(t - 1, 0))
                        nc.vector.tensor_tensor(ra_v, qk, cos, ALU.mult)
                        nc.vector.tensor_tensor(rb_v[:, :, 0::2], qk[:, :, 1::2], sin[:, :, 0::2], ALU.mult)
                        nc.vector.tensor_tensor(rb_v[:, :, 1::2], qk[:, :, 0::2], sin[:, :, 1::2],
                                                ALU.mult).then_inc(rel_dve, 1)
                        dve.wait_ge(rel_dve, 12 * c + t + 1)
                        nc.vector.tensor_tensor(qkr[:, t, :], ra[:, t % 2, :], rb[:, t % 2, :], ALU.add).then_inc(rotated, 1)

                def rests(b, half):
                    c = 2 * b + half
                    for n in range(8):
                        s = n % 2
                        dve.wait_ge(hi_ready, 8 * c + n + 1)
                        dve.wait_ge(lo_ready[s], 4 * c + n // 2)
                        nc.vector.tensor_tensor(rest[s][:, :], ps[:, 4 + n % 4, :], parts[s][:, 0, :],
                                                ALU.subtract).then_inc(rel_dve, 1)

                norms(0, 0, first=True)
                def turn(b):
                    for half in range(2):
                        norms(b + half, 1 - half)
                        rotate(b, half)
                        rests(b, half)

                looped(dve, B - 1, turn)
                norms(B - 1, 1)
                for half in range(2):
                    rotate(B - 1, half)
                    rests(B - 1, half)

            @block.scalar
            def _(act):
                act.wait_ge(vconst, 4)
                def evacuate(b, half):
                    c = 2 * b + half
                    for t in range(CT):
                        act.wait_ge(flipped, CT * c + t + 1)
                        bank = 2 * (t % 2)
                        nc.scalar.copy(xt[half][:, :, :, t * P:(t + 1) * P].rearrange("p s k t -> p (s k) t"),
                                       ps[:, bank:bank + 2, :].rearrange("p b c -> p (b c)")[:, 0:6 * P]
                                       .rearrange("p (s t) -> p s t", t=P)).then_inc(xt_ready, 1)
                    act.wait_ge(v_out[half], 16 * 2 * GROUPS * b)
                    for t in range(CT):
                        act.wait_ge(proj, 16 * c + 2 * t + 2)
                        nc.scalar.copy(vst[half][:, :, t, :, 0:HD],
                                       ps[:, 4 + (2 * t + 1) % 4, :].rearrange("p (a h d) -> p a h d", a=2, d=HD)
                                       ).then_inc(rel_act, 1)
                    for n in range(8):
                        s = n % 2
                        act.wait_ge(proj, 16 * c + 8 + n + 1)
                        act.wait_ge(qk_out[s], 32 * (4 * c + n // 2))
                        nc.scalar.copy(parts[s][:, 0, :], ps[:, 4 + n % 4, :]).then_inc(hi_ready, 1)
                        act.wait_ge(rel_dve, 12 * c + 4 + n + 1)
                        nc.scalar.copy(parts[s][:, 1, :], rest[s][:, :]).then_inc(mid_ready, 1)

                def turn(b):
                    for half in range(2):
                        evacuate(b, half)

                looped(act, B, turn)

            @block.tensor
            def _(pe):
                pe.wait_ge(w_in, 16 * 6)
                pe.wait_ge(w_ready, KC + 2)

                def chunk(b, half):
                    c = 2 * b + half
                    pe.wait_ge(normed, c + 1)
                    for t in range(CT):
                        if t < 2:
                            pe.wait_ge(xt_ready, CT * c)
                        else:
                            pe.wait_ge(xt_ready, CT * c + t - 1)
                        for s, src in enumerate((xn[half], rx[half], xr[half])):
                            for k in range(KC):
                                col = (s * KC + k) * P
                                last = nc.tensor.transpose(ps[:, 2 * (t % 2) + col // 512, col % 512:col % 512 + P],
                                                           src[:, t, k * P:(k + 1) * P], ident[:, :])
                        last.then_inc(flipped, 1)
                    pe.wait_ge(rel_dve, 12 * c)
                    pe.wait_ge(rel_act, CT * c)
                    for t in range(CT):
                        if t >= 2:
                            pe.wait_ge(rel_dve, 12 * c + t - 1)
                        pe.wait_ge(xt_ready, CT * c + t + 1)
                        tok = slice(t * P, (t + 1) * P)
                        for k in range(KC):
                            last = nc.tensor.matmul(ps[:, 4 + (2 * t) % 4, :], xt[half][:, 2, k, tok],
                                                    w2[:, k, 0:2 * E], start=(k == 0), stop=(k == KC - 1))
                        last.then_inc(proj, 1)
                        if t >= 2:
                            pe.wait_ge(rel_act, CT * c + t - 1)
                        for a, (s, w) in enumerate(((2, w2), (0, w1))):
                            for k in range(KC):
                                last = nc.tensor.matmul(ps[:, 4 + (2 * t + 1) % 4, a * E:(a + 1) * E],
                                                        xt[half][:, s, k, tok], w[:, k, 2 * E:3 * E],
                                                        start=(k == 0), stop=(k == KC - 1))
                        last.then_inc(proj, 1)
                    for m in range(4):
                        if m % 2 == 0:
                            pe.wait_ge(rel_dve, 12 * c + 3 + m // 2)
                        else:
                            pe.wait_ge(rel_act, CT * c + 3 + m // 2)
                        for k in range(KC):
                            last = nc.tensor.matmul(ps[:, 4 + m, :], w1[:, k, m * P:(m + 1) * P],
                                                    xt[half][:, 1, k, :], start=(k == 0), stop=(k == KC - 1))
                        last.then_inc(proj, 1)
                    pe.wait_ge(rotated, CT * (c + 1))
                    for m in range(4):
                        pe.wait_ge(rel_dve, 12 * c + 4 + m + 1)
                        for t in range(CT):
                            last = nc.tensor.transpose(ps[:, 4 + m, t * P:(t + 1) * P],
                                                       qkr[:, t, m * P:(m + 1) * P], ident[:, :])
                        last.then_inc(proj, 1)

                def turn(b):
                    for half in range(2):
                        chunk(b, half)

                looped(pe, B, turn)


RING = 4
PBUFS = 4
BANKS = 3

MAX_TILES = [(7, 0), (0, 0), (7, 1), (1, 0), (6, 0), (2, 0), (6, 1), (3, 0), (5, 0), (5, 1), (4, 0), (4, 1)]
MAXIMA = [(h, t, p) for h in range(GH) for t, p in MAX_TILES]
LAST_MAX = [max(k for k, it in enumerate(MAXIMA) if it[0] == h) for h in range(GH)]
ROWS = [(h, half) for h in range(GH) for half in range(2)]
SCORES = ([(j, half, (h,)) for j in range(4) for h in range(GH) for half in range(2)]
          + [(j, 1, (h,)) for j in (4, 5) for h in range(GH)]
          + [(6, 1, (0, 1)), (6, 1, (2, 3)), (7, 1, (0, 1, 2, 3))])
LAST_SCORES = [max(g for g, it in enumerate(SCORES) if it[0] == j) for j in range(TT)]
VALUES = [(j, half) for j in range(TT) for half in range(j // 4, 2)]

RPU = len(SCORES) + len(ROWS)
MPU = len(MAXIMA)
FIRST_ROW_LAG = 5
MAX_AHEAD = 11
VALUES_LAG = 3
PERIOD = ("MMSSMSMVSMSMMSSMSMVSMSSMMVMSRSMMMVMSMSRMMSMSVSMSMSMVSSMRMSMM"
          "SVSMSMSSMMSRMSSMVSMMSSMVSMSMMRSVMSMSMSVSMSMRMMRRMSV")


def unit_steps():
    steps, n, g, row, k, m = [], 0, 0, 0, MAX_AHEAD, -VALUES_LAG
    for kind in PERIOD:
        if kind == "S":
            steps.append(("scores", n, g))
            n, g = n + 1, g + 1
        elif kind == "R":
            steps.append(("row", n, row))
            n, row = n + 1, row + 1
        elif kind == "M":
            steps.append(("max", 1 + k // MPU, k % MPU))
            k += 1
        else:
            steps.append(("values", m // len(VALUES), m % len(VALUES)))
            m += 1
    return steps


STEPS = unit_steps()
LAST_ROW = max(step[1] for step in STEPS if step[0] == "row")


def attend(nc, identity, causal_mask, qk_d, v_d, y_d):
    with ExitStack() as ctx:
        sb = lambda name, shape, dt=FP32: ctx.enter_context(nc.sbuf_tensor("b_" + name, shape, dt))
        pb = lambda name, shape: ctx.enter_context(nc.psum_tensor("b_" + name, shape, FP32))
        sem = lambda name: ctx.enter_context(nc.semaphore("b_" + name))

        qs = [sb(f"qs{r}", [P, GH, T], BF16) for r in range(RING)]
        ks = [sb(f"ks{r}", [P, GH, T], BF16) for r in range(RING)]
        vv = [sb(f"vv{r}", [P, TT, GH * VW]) for r in range(RING)]
        yo = [sb(f"yo{r}", [P, T]) for r in range(2)]
        probs = [sb(f"probs{r}", [P, GH, T]) for r in range(PBUFS)]
        ident_f = sb("ident_f", [P, P])
        ident = sb("ident", [P, P], BF16)
        mask = sb("mask", [P, 512])
        junk = sb("junk", [P, BANKS, 512])
        pmax = sb("pmax", [P, GH, TT, 2])
        negm = sb("negm", [P, GH, TT])
        nrest = sb("nrest", [P, GH, TT])
        mparts = sb("mparts", [P, GH, TT, PARTS], BF16)
        acc = pb("acc", [P, 2, 512])
        st = pb("st", [P, BANKS, 512])
        sm = pb("sm", [P, BANKS, 512])

        const_in, consts = sem("const_in"), sem("consts")
        qk_in, v_in = [sem(f"qk_in{r}") for r in range(RING)], [sem(f"v_in{r}") for r in range(RING)]
        y_out = [sem(f"y_out{n}") for n in range(2)]
        st_ready, st_read = sem("st_ready"), sem("st_read")
        sm_ready, sm_read = sem("sm_ready"), sem("sm_read")
        mask_done, pv_done = sem("mask_done"), sem("pv_done")
        negm_ready, split_chain, mparts_ready = sem("negm_ready"), sem("split_chain"), sem("mparts_ready")
        y_ready = sem("y_ready")
        dve_passed, pool_passed = sem("dve_passed"), sem("pool_passed")

        def st_uses(unit, n):
            return len(ROWS) + RPU * unit + n

        def st_bank(n):
            return (len(ROWS) + n) % BANKS

        def over_units(engine, do_step):
            def shifted(i, r, d, step):
                do_step(i + (r + d) // RING, (r + d) % RING, step)

            def period(i, r):
                n = 0
                for kind, a, b in STEPS:
                    if kind == "scores" or kind == "row":
                        if kind == "scores" or not isinstance(i, int) or RING * i + r + 1 < UNITS:
                            do_step(i, r, (kind, n, b))
                            n += 1
                    elif not isinstance(i, int) or 0 <= RING * i + r + a < UNITS:
                        shifted(i, r, a, (kind, b))

            stream = [(0, k) for k in range(MPU)] + [(1, k) for k in range(MAX_AHEAD)]
            for n, (r, k) in enumerate(stream):
                do_step(0, r, ("max", k))
                if n - FIRST_ROW_LAG in LAST_MAX:
                    for m in range(2):
                        row = 2 * LAST_MAX.index(n - FIRST_ROW_LAG) + m
                        do_step(0, -1, ("row", RPU - len(ROWS) + row, row))
            for r in range(RING):
                period(0, r)
            with engine.Fori(1, UNITS // RING - 1) as i:
                for r in range(RING):
                    period(i, r)
            for r in range(RING):
                period(UNITS // RING - 1, r)
            for m in range(len(VALUES) - VALUES_LAG, len(VALUES)):
                do_step(UNITS // RING - 1, RING - 1, ("values", m))

        with nc.Block() as block:

            @block.sync
            def _(sp):
                sp.dma_start(ident_f[:, :], identity).then_inc(const_in, 16)
                sp.dma_start(mask[:, :], causal_mask).then_inc(const_in, 16)

                def load(i, r):
                    unit = RING * i + r
                    for band in range(BANDS):
                        rows = slice(band * HD, (band + 1) * HD)
                        for which, part, dst in ((0, Q_PART[band], qs[r]), (1, K_PART[band], ks[r])):
                            sp.dma_start(dst[rows, :, :],
                                         qk_d[unit, which, part, :, :].rearrange("(h f) t -> f h t", f=HD)
                                         ).then_inc(qk_in[r], 16)
                    sp.dma_start(vv[r][:, :, :], v_d[unit, :, :].rearrange("(t p) n -> p t n", p=P)
                                 ).then_inc(v_in[r], 16)

                def store(i, r):
                    sp.wait_ge(y_ready, RING * i + r + 1)
                    sp.dma_start(y_d[RING * i + r, :, :], yo[r % 2][:, :]).then_inc(y_out[r % 2], 16)

                def turn(i):
                    for r in range(RING):
                        sp.wait_ge(pv_done, TT * (RING * i + r + 1))
                        load(i + 1, r)
                        store(i, r)

                for r in range(RING):
                    load(0, r)
                looped(sp, UNITS // RING - 1, turn)
                for r in range(RING):
                    store(UNITS // RING - 1, r)
                for n in range(2):
                    sp.wait_ge(y_out[n], 16 * UNITS // 2)

            @block.tensor
            def _(pe):
                pe.wait_ge(const_in, 32)
                pe.wait_ge(consts, RING + 2)

                def do_step(i, r, step):
                    unit = RING * i + r
                    if step[0] == "max":
                        k = step[1]
                        h, t, piece = MAXIMA[k]
                        if k == 0:
                            pe.wait_ge(qk_in[r], 16 * 2 * BANDS * (i + 1))
                        if not isinstance(unit, int) or MPU * unit + k >= BANKS:
                            pe.wait_ge(sm_read, MPU * unit + k - BANKS + 1)
                        n = min((t + 1) * P - 512 * piece, 512)
                        nc.tensor.matmul(sm[:, k % BANKS, 0:n], qs[r][0:SROWS, h, t * P:(t + 1) * P],
                                         ks[r][0:SROWS, h, 512 * piece:512 * piece + n], start=True,
                                         stop=True).then_inc(sm_ready, 1)
                    elif step[0] == "values":
                        j, half = VALUES[step[1]]
                        if step[1] == 0:
                            pe.wait_ge(y_ready, unit)
                            pe.wait_ge(v_in[r], 16 * (i + 1))
                        if half == j // 4:
                            pe.wait_ge(mask_done, TT * unit + j + 1)
                        lo = max(j * P - 512 * half, 0)
                        for h in range(GH):
                            last = nc.tensor.matmul(acc[VW * h:VW * (h + 1), half, lo:512],
                                                    vv[r][:, j, VW * h:VW * (h + 1)],
                                                    probs[j % PBUFS][:, h, 512 * half + lo:512 * (half + 1)],
                                                    start=(j == 0), stop=(j == (3 if half == 0 else 7)))
                        if half:
                            last.then_inc(pv_done, 1)
                    else:
                        kind, n, m = step
                        uses = st_uses(unit, n)
                        if kind == "scores" and m == 0:
                            first = isinstance(unit, int) and unit == 0
                            pe.wait_ge(st_read, len(ROWS) if first else st_uses(unit - 1, LAST_ROW + 1))
                        if not isinstance(unit, int) or uses >= BANKS:
                            pe.wait_ge(st_read, uses - BANKS + 1)
                        if kind == "scores":
                            j, half, heads = SCORES[m]
                            lo = max(j * P - 512 * half, 0)
                            w = 512 - lo
                            for x, h in enumerate(heads):
                                last = nc.tensor.matmul(st[:, st_bank(n), x * w:(x + 1) * w],
                                                        ks[r][0:SROWS + PARTS, h, j * P:(j + 1) * P],
                                                        qs[r][0:SROWS + PARTS, h, 512 * half + lo:512 * (half + 1)],
                                                        start=True, stop=True)
                        else:
                            h, half = ROWS[m]
                            pe.wait_ge(mparts_ready, GH * (unit + 1) + h + 1)
                            for x in range(4):
                                last = nc.tensor.matmul(st[SROWS:SROWS + PARTS, st_bank(n), x * P:(x + 1) * P],
                                                        mparts[:, h, 4 * half + x, :], ident[:, :],
                                                        start=True, stop=True)
                        last.then_inc(st_ready, 1)

                over_units(pe, do_step)

            @block.scalar
            def _(act):
                act.wait_ge(consts, RING + 2)

                def do_step(i, r, step):
                    unit = RING * i + r
                    if step[0] == "scores":
                        _, n, g = step
                        j, half, heads = SCORES[g]
                        free = TT * unit + j - PBUFS + 1
                        if g == 0 or SCORES[g - 1][0] != j:
                            if not isinstance(free, int) or free > 0:
                                act.wait_ge(pv_done, free)
                        lo = max(j * P - 512 * half, 0)
                        w = 512 - lo
                        act.wait_ge(st_ready, st_uses(unit, n) + 1)
                        nc.scalar.activation(probs[j % PBUFS][:, heads[0]:heads[-1] + 1, 512 * half + lo:512 * (half + 1)],
                                             st[:, st_bank(n), 0:len(heads) * w].rearrange("p (h c) -> p h c", c=w),
                                             ACT.Exp).then_inc(st_read, 1)
                    elif step[0] == "row":
                        _, n, m = step
                        h, half = ROWS[m]
                        act.wait_ge(st_ready, st_uses(unit, n) + 1)
                        nc.scalar.copy(qs[(r + 1) % RING][SROWS:SROWS + PARTS, h, 512 * half:512 * (half + 1)],
                                       st[SROWS:SROWS + PARTS, st_bank(n), :]).then_inc(st_read, 1)
                    elif step[0] == "values" and step[1] == len(VALUES) - 1:
                        act.wait_ge(pv_done, TT * (unit + 1))
                        if not isinstance(unit, int) or unit >= 2:
                            act.wait_ge(y_out[r % 2], 16 * (2 * i + r // 2))
                        nc.scalar.copy(yo[r % 2][:, :], acc[:, :, :].rearrange("p b c -> p (b c)")
                                       ).then_inc(y_ready, 1)

                over_units(act, do_step)

            @block.vector
            def _(dve):
                def do_step(i, r, step):
                    if step[0] != "max":
                        return
                    unit, k = RING * i + r, step[1]
                    h, t, piece = MAXIMA[k]
                    bank = k % BANKS
                    n = min((t + 1) * P - 512 * piece, 512)
                    if piece == t // 4:
                        apart(dve, sm_ready, MPU * unit + k + 1, dve_passed)
                        nc.vector.tensor_tensor_reduce(
                            out=junk[:, bank, 0:n], in0=sm[:, bank, 0:n], in1=mask[:, 512 - n:512], scale=1.0,
                            scalar=-BIG, op0=ALU.add, op1=ALU.max,
                            accum_out=pmax[:, h, t, 1:2]).then_inc(sm_read, 1)
                    else:
                        dve.wait_ge(sm_ready, MPU * unit + k + 1)
                        nc.vector.tensor_reduce(pmax[:, h, t, 0:1], sm[:, bank, 0:n], AX.X,
                                                ALU.max).then_inc(sm_read, 1)
                    if k == LAST_MAX[h]:
                        dve.wait_ge(sm_read, MPU * unit + k + 1)
                        nc.vector.tensor_reduce(negm[:, h, :], pmax[:, h, :, :], AX.X, ALU.max,
                                                negate=True).then_inc(negm_ready, 1)

                for r in range(RING):
                    nc.vector.memset(ks[r][SROWS:SROWS + PARTS, :, :], 1.0).then_inc(consts, 1)
                nc.vector.memset(pmax[:, :, :, :], -BIG).then_inc(consts, 1)
                dve.wait_ge(const_in, 32)
                nc.vector.tensor_copy(ident[:, :], ident_f[:, :]).then_inc(consts, 1)
                dve.wait_ge(consts, RING + 2)
                over_units(dve, do_step)

            @block.gpsimd
            def _(pool):
                def do_step(i, r, step):
                    unit = RING * i + r
                    if step[0] == "scores" and step[2] in LAST_SCORES:
                        j = LAST_SCORES.index(step[2])
                        apart(pool, st_read, st_uses(unit, step[1]) + 1, pool_passed)
                        diag = probs[j % PBUFS][:, :, j * P:(j + 1) * P]
                        nc.gpsimd.affine_select(out=diag, in_=diag, compare_op=ALU.is_ge, fill=0.0, base=0,
                                                pattern=[[0, GH], [1, P]],
                                                channel_multiplier=-1).then_inc(mask_done, 1)
                    elif step[0] == "max" and step[1] in LAST_MAX:
                        h = LAST_MAX.index(step[1])
                        apart(pool, negm_ready, GH * unit + h + 1, pool_passed)
                        chain = Chain(pool, split_chain, 3 * (GH * unit + h))
                        chain(nc.gpsimd.tensor_copy(mparts[:, h, :, 0], negm[:, h, :]))
                        chain(nc.gpsimd.tensor_tensor(out=nrest[:, h, :], in0=negm[:, h, :], in1=mparts[:, h, :, 0],
                                                      op=ALU.subtract))
                        pool.sem_inc(pool_passed, 1)
                        chain(nc.gpsimd.tensor_copy(mparts[:, h, :, 1], nrest[:, h, :]))
                        nc.gpsimd.tensor_tensor(out=mparts[:, h, :, 2], in0=nrest[:, h, :], in1=mparts[:, h, :, 1],
                                                op=ALU.subtract).then_inc(mparts_ready, 1)

                over_units(pool, do_step)


class HeadsOut:

    def __init__(self, nc, ctx, tag, ps, attention, w_out, ident, y_d):
        sb = lambda name, shape, dt=FP32: ctx.enter_context(nc.sbuf_tensor(f"{tag}_{name}", shape, dt))
        sem = lambda name: ctx.enter_context(nc.semaphore(f"{tag}_{name}"))
        self.nc, self.ps, self.attention, self.w_out, self.ident, self.y_d = nc, ps, attention, w_out, ident, y_d
        self.yt = [sb(f"yt{n}", [P, GROUPS, CH]) for n in range(2)]
        self.yn = [sb(f"yn{n}", [P, E]) for n in range(2)]
        self.ynt = [sb(f"ynt{n}", [P, KC, P]) for n in range(2)]
        self.rden = [sb(f"rden{n}", [P, HEADS]) for n in range(2)]
        self.y_in = [sem(f"y_in{n}") for n in range(2)]
        self.flipped, self.rden_ready, self.yn_ready = sem("flipped"), sem("rden_ready"), sem("yn_ready")
        self.back, self.ynt_ready, self.projected, self.taken = sem("back"), sem("ynt_ready"), sem("projected"), sem("taken")

    def load(self, queue, b, half):
        unit = b * GROUPS + self.attention * UB
        queue.dma_start(self.yt[half][:, :, :],
                        self.y_d[bass.ds(unit, GROUPS), :, half * CH:(half + 1) * CH].rearrange("g r t -> r g t")
                        ).then_inc(self.y_in[half], 16)

    def tensor(self, pe, b, half):
        c, nc, ps = 2 * b + half, self.nc, self.ps

        def flip(t):
            pe.wait_ge(self.yn_ready, CT * c + max(t - 1, 0))
            for g in range(GROUPS):
                last = nc.tensor.transpose(ps[:, t % 2, g * P:(g + 1) * P],
                                           self.yt[half][:, g, t * P:(t + 1) * P], self.ident[:, :])
            last.then_inc(self.flipped, 1)

        def back(t):
            pe.wait_ge(self.yn_ready, CT * c + t + 1)
            if t != 1:
                pe.wait_ge(self.ynt_ready, CT * c + max(t - 1, 0))
            for k in range(KC):
                last = nc.tensor.transpose(ps[:, 2 + t % 2, k * P:(k + 1) * P],
                                           self.yn[t % 2][:, k * P:(k + 1) * P], self.ident[:, :])
            last.then_inc(self.back, 1)

        def out(t):
            pe.wait_ge(self.ynt_ready, CT * c + t + 1)
            if t != 1:
                pe.wait_ge(self.taken, CT * c + max(t - 1, 0))
            for k in range(KC):
                last = nc.tensor.matmul(ps[:, 4 + t % 2, 0:E], self.ynt[t % 2][:, k, :], self.w_out[:, k, :],
                                        start=(k == 0), stop=(k == KC - 1))
            last.then_inc(self.projected, 1)

        pe.wait_ge(self.y_in[half], 16 * b + 16)
        flip(0)
        flip(1)
        back(0)
        for t in range(2, CT):
            flip(t)
            back(t - 1)
            out(t - 2)
        back(CT - 1)
        out(CT - 2)
        out(CT - 1)

    def vector(self, dve, b, half, t):
        c, nc = 2 * b + half, self.nc
        dve.wait_ge(self.flipped, CT * c + t + 1)
        y = self.ps[:, t % 2, :].rearrange("p (h v) -> p h v", v=VW)
        nc.vector.reciprocal(self.rden[t % 2][:, :], y[:, :, HD]).then_inc(self.rden_ready, 1)
        dve.wait_ge(self.rden_ready, CT * c + t + 1)
        if t != 1:
            dve.wait_ge(self.back, CT * c + max(t - 1, 0))
        nc.vector.tensor_tensor(self.yn[t % 2][:, :].rearrange("p (h d) -> p h d", d=HD), y[:, :, 0:HD],
                                self.rden[t % 2][:, :].rearrange("p (h o) -> p h o", o=1)
                                .broadcast_to((P, HEADS, HD)), ALU.mult).then_inc(self.yn_ready, 1)

    def scalar(self, act, b, half, t):
        c = 2 * b + half
        act.wait_ge(self.back, CT * c + t + 1)
        if t != 1:
            act.wait_ge(self.projected, CT * c + max(t - 1, 0))
        self.nc.scalar.copy(self.ynt[t % 2][:, :, :],
                            self.ps[:, 2 + t % 2, 0:KC * P].rearrange("p (k t) -> p k t", k=KC)
                            ).then_inc(self.ynt_ready, 1)


def staggered(engine, lead, follow):
    lead(0, 0)
    def turn(b):
        for half in range(2):
            lead(b + half, 1 - half)
            follow(b, half)

    looped(engine, B - 1, turn)
    lead(B - 1, 1)
    for half in range(2):
        follow(B - 1, half)


def block_mid(nc, w_o, w_router, g2, identity, xn_d, y_d, z_d, h_d, logits):
    with ExitStack() as ctx:
        sb = lambda name, shape, dt=FP32: ctx.enter_context(nc.sbuf_tensor("c_" + name, shape, dt))
        sem = lambda name: ctx.enter_context(nc.semaphore("c_" + name))
        pair = lambda name: [sem(f"{name}{n}") for n in range(2)]
        wo = sb("wo", [P, KC, E])
        wr = sb("wr", [P, KC, EXPERTS])
        g2c = sb("g2c", [P, KC])
        ident = sb("ident", [P, P])
        xn = [sb(f"xn{n}", [P, CT, E]) for n in range(2)]
        z = [sb(f"z{n}", [P, CT, E]) for n in range(2)]
        h = [sb(f"h{n}", [P, CT, E]) for n in range(2)]
        ht = sb("ht", [P, KC, CH])
        junk = sb("junk", [P, CT, E])
        ssq = sb("ssq", [P, CT])
        ms = sb("ms", [P, CT])
        rrms = sb("rrms", [P, CT])
        neghalf = sb("neghalf", [P, CT])
        zeros = sb("zeros", [P, SLOTB, E])
        ps = ctx.enter_context(nc.psum_tensor("c_ps", [P, 8, 512], FP32))
        w_in, consts = sem("w_in"), sem("consts")
        xn_in, z_out, h_out = pair("xn_in"), pair("z_out"), pair("h_out")
        ms_ready, rsq, h_ready, h_flipped, ht_ready = sem("ms_ready"), sem("rsq"), sem("h_ready"), sem("h_flipped"), sem("ht_ready")
        routed, logits_ready, ssq_ready, dump_out = sem("routed"), sem("logits_ready"), sem("ssq_ready"), sem("dump_out")
        heads = HeadsOut(nc, ctx, "c_out", ps, 0, wo, ident, y_d)

        def rows(b, half):
            return bass.ds(b * T + half * CH, CH)

        with nc.Block() as block:

            @block.sync
            def _(sp):
                for dst, src in ((wo[:, :, :], w_o.rearrange("(k p) n -> p k n", p=P)),
                                 (wr[:, :, :], w_router.rearrange("(k p) n -> p k n", p=P)),
                                 (g2c[:, :], g2), (ident[:, :], identity)):
                    sp.dma_start(dst, src).then_inc(w_in, 16)

                def load(b, half):
                    heads.load(sp, b, half)
                    sp.dma_start(xn[half][:, :, :], xn_d[rows(b, half), :].rearrange("(t p) e -> p t e", p=P)
                                 ).then_inc(xn_in[half], 16)

                load(0, 0)
                load(0, 1)
                def turn(b):
                    for half in range(2):
                        sp.wait_ge(h_ready, 2 * b + half + 1)
                        load(b + 1, half)

                looped(sp, B - 1, turn)

            @block.gpsimd
            def _(pool):
                nc.gpsimd.memset(neghalf[:, :], -0.5).then_inc(consts, 1)
                nc.gpsimd.memset(zeros[:, :, :], 0.0).then_inc(consts, 1)
                pool.wait_ge(consts, 2)
                pool.dma_start(z_d[TOK:TOK + SLOTB * P, :].rearrange("(s p) e -> p s e", p=P), zeros[:, :, :]
                               ).then_inc(dump_out, 16)
                def turn(b):
                    for half in range(2):
                        c = 2 * b + half
                        pool.wait_ge(ms_ready, c + 1)
                        nc.gpsimd.tensor_tensor(out=rrms[:, :], in0=ms[:, :], in1=neghalf[:, :],
                                                op=ALU.pow).then_inc(rsq, 1)
                        pool.dma_start(z_d[rows(b, half), :].rearrange("(t p) e -> p t e", p=P), z[half][:, :, :]
                                       ).then_inc(z_out[half], 16)
                        pool.wait_ge(h_ready, c + 1)
                        pool.dma_start(h_d[rows(b, half), 0:E].rearrange("(t p) e -> p t e", p=P), h[half][:, :, :]
                                       ).then_inc(h_out[half], 16)

                looped(pool, B, turn)
                pool.wait_ge(dump_out, 16)
                for half in range(2):
                    pool.wait_ge(z_out[half], 16 * B)
                    pool.wait_ge(h_out[half], 16 * B)

            @block.tensor
            def _(pe):
                pe.wait_ge(w_in, 16 * 4)

                def route(b, half):
                    c = 2 * b + half
                    pe.wait_ge(h_ready, c + 1)
                    pe.wait_ge(logits_ready, c)
                    pe.wait_ge(ht_ready, 2 * c)
                    for k in range(KC):
                        for t in range(CT):
                            last = nc.tensor.transpose(ps[:, 6 + k, t * P:(t + 1) * P],
                                                       h[half][:, t, k * P:(k + 1) * P], ident[:, :])
                    last.then_inc(h_flipped, 1)
                    pe.wait_ge(ht_ready, 2 * c + 2)
                    for t in range(CT):
                        for k in range(KC):
                            last = nc.tensor.matmul(ps[:, 6, t * EXPERTS:(t + 1) * EXPERTS],
                                                    ht[:, k, t * P:(t + 1) * P], wr[:, k, :],
                                                    start=(k == 0), stop=(k == KC - 1))
                    last.then_inc(routed, 1)

                staggered(pe, lambda b, half: heads.tensor(pe, b, half), route)

            @block.scalar
            def _(act):
                act.wait_ge(w_in, 16 * 4)

                def lead(b, half):
                    for t in range(CT):
                        heads.scalar(act, b, half, t)

                def follow(b, half):
                    c = 2 * b + half
                    act.wait_ge(h_flipped, c + 1)
                    act.wait_ge(routed, c)
                    for k in range(KC):
                        nc.scalar.activation(ht[:, k, :], ps[:, 6 + k, :], ACT.Copy,
                                             scale=g2c[:, k:k + 1]).then_inc(ht_ready, 1)

                staggered(act, lead, follow)

            @block.vector
            def _(dve):
                def lead(b, half):
                    c = 2 * b + half
                    dve.wait_ge(xn_in[half], 16 * b + 16)
                    dve.wait_ge(z_out[half], 16 * b)
                    dve.wait_ge(h_out[half], 16 * b)
                    for t in range(CT + 2):
                        if t < CT:
                            heads.vector(dve, b, half, t)
                        if t >= 2:
                            dve.wait_ge(heads.projected, CT * c + t - 1)
                            nc.vector.tensor_tensor(z[half][:, t - 2, :], ps[:, 4 + t % 2, 0:E], xn[half][:, t - 2, :],
                                                    ALU.add).then_inc(heads.taken, 1)
                    dve.wait_ge(heads.taken, CT * (c + 1))
                    for t in range(CT):
                        last = nc.vector.tensor_tensor_reduce(
                            out=junk[:, t, :], in0=z[half][:, t, :], in1=z[half][:, t, :], scale=1.0, scalar=0.0,
                            op0=ALU.mult, op1=ALU.add, accum_out=ssq[:, t:t + 1])
                    last.then_inc(ssq_ready, 1)
                    dve.wait_ge(ssq_ready, c + 1)
                    nc.vector.tensor_scalar(ms[:, :], ssq[:, :], 1.0 / E, RMS_EPS, ALU.mult, ALU.add).then_inc(ms_ready, 1)
                    dve.wait_ge(rsq, c + 1)
                    for t in range(CT):
                        last = nc.vector.tensor_scalar(h[half][:, t, :], z[half][:, t, :], rrms[:, t:t + 1], None,
                                                       ALU.mult)
                    last.then_inc(h_ready, 1)

                def follow(b, half):
                    c = 2 * b + half
                    dve.wait_ge(routed, c + 1)
                    nc.vector.tensor_copy(logits[:, :, bass.ds(b * TT + half * CT, CT)],
                                          ps[:, 6, 0:CT * EXPERTS].rearrange("p (t e) -> p e t", e=EXPERTS)
                                          ).then_inc(logits_ready, 1)

                staggered(dve, lead, follow)


def route(nc, ones_in, upper_in, iota_in, token_parts, slot_rows, h_d, logits, occupied, gather_row, scatter_row):
    N = EXPERTS * TILES
    VALS = 3
    with ExitStack() as ctx:
        sb = lambda name, shape, dt=FP32: ctx.enter_context(nc.sbuf_tensor("d_" + name, shape, dt))
        sem = lambda name: ctx.enter_context(nc.semaphore("d_" + name))
        ones = sb("ones", [P, P])
        upper = sb("upper", [P, P])
        iota_f = sb("iota_f", [P, P])
        iota = sb("iota", [P, P], BF16)
        tparts = sb("tparts", [P, TILES, VALS])
        slots = sb("slots", [P, SLOTB])
        zero = sb("zero", [P, P], BF16)
        probs = sb("probs", [P, EXPERTS, TILES])
        gate = sb("gate", [P, EXPERTS, TILES])
        gate_t = sb("gate_t", [P, TILES, EXPERTS])
        rank = sb("rank", [P, EXPERTS, TILES])
        tmp = sb("tmp", [P, EXPERTS, TILES])
        tmp2 = sb("tmp2", [P, EXPERTS, TILES])
        tied = sb("tied", [P, EXPERTS, TILES])
        chosen = sb("chosen", [P, EXPERTS, TILES])
        total = sb("total", [P, EXPERTS, TILES])
        onesrow = sb("onesrow", [P, TILES])
        top = sb("top", [P, TILES])
        den = sb("den", [P, TILES])
        thr = sb("thr", [P, EXPERTS], I32)
        cand = sb("cand", [P, EXPERTS], I32)
        bit = sb("bit", [P, EXPERTS], I32)
        keep = sb("keep", [P, EXPERTS], I32)
        part = sb("part", [P, EXPERTS])
        need = sb("need", [P, EXPERTS])
        slot = sb("slot", [P, EXPERTS, TILES])
        blk = sb("blk", [P, EXPERTS, TILES])
        slot_t = sb("slot_t", [P, TILES, EXPERTS])
        rhs = sb("rhs", [P, TILES, EXPERTS, SLOTB, VALS], BF16)
        onehot = [sb(f"onehot{n}", [P, EXPERTS, P], BF16) for n in range(2)]
        found = sb("found", [P, EXPERTS, SLOTB, VALS])
        row_f = sb("row_f", [P, EXPERTS, SLOTB])
        row_g = sb("row_g", [P, EXPERTS, SLOTB])
        ps = ctx.enter_context(nc.psum_tensor("d_ps", [P, 4, 512], FP32))
        const_in, steps, exp_ready, gates_out = sem("const_in"), sem("steps"), sem("exp_ready"), sem("gates_out")
        search_steps, counted, cmp_ready = sem("search_steps"), sem("counted"), sem("cmp_ready")
        prefixed, prefix_ask = sem("prefixed"), sem("prefix_ask")
        oh_ready, oh_used, compacted, rhs_ready, gate_ready = sem("oh_ready"), sem("oh_used"), sem("compacted"), sem("rhs_ready"), sem("gate_ready")
        max_sub = sem("max_sub")
        passed = sem("passed")
        BITS = 30
        SEARCH = 5

        def spread(ap, n):
            return ap.rearrange("p (e o) -> p e o", o=1).broadcast_to((P, EXPERTS, n))

        def over_experts(ap):
            return ap.rearrange("p (o t) -> p o t", o=1).broadcast_to((P, EXPERTS, TILES))

        with nc.Block() as block:

            @block.sync
            def _(sp):
                for dst, src in ((ones[:, :], ones_in), (upper[:, :], upper_in), (iota_f[:, :], iota_in),
                                 (tparts[:, :, :], token_parts), (slots[:, :], slot_rows)):
                    sp.dma_start(dst, src).then_inc(const_in, 16)
                sp.wait_ge(gate_ready, 1)
                sp.dma_start(h_d[:, E:E + EXPERTS].rearrange("(t p) e -> p t e", p=P), gate_t[:, :, :]
                             ).then_inc(gates_out, 16)
                sp.wait_ge(gates_out, 16)

            @block.scalar
            def _(act):
                act.wait_ge(max_sub, 1)
                nc.scalar.activation(probs[:, :, :], tmp[:, :, :], ACT.Exp).then_inc(exp_ready, 1)

            @block.tensor
            def _(pe):
                pe.wait_ge(const_in, 16 * 5)
                with pe.Fori(0, BITS) as i:
                    pe.wait_ge(cmp_ready, i + 1)
                    nc.tensor.matmul(ps[:, 0, 0:EXPERTS], ones[:, :], part[:, :], start=True, stop=True
                                     ).then_inc(counted, 1)
                for n, src in enumerate((tmp, tied, chosen)):
                    pe.wait_ge(prefix_ask, n + 1)
                    last = nc.tensor.matmul(ps[:, 1, :], ones[:, :], src[:, :, :].rearrange("p e t -> p (e t)"),
                                            start=True, stop=True)
                    if n:
                        last = nc.tensor.matmul(ps[:, 2, :], upper[:, :], src[:, :, :].rearrange("p e t -> p (e t)"),
                                                start=True, stop=True)
                    last.then_inc(prefixed, 1)
                pe.wait_ge(rhs_ready, 1)
                cols = EXPERTS * SLOTB * VALS
                all_rhs = rhs[:, 0, :, :, :].rearrange("p e a v -> p (e a v)")
                nc.tensor.matmul(ps[:, 3, 0:cols], zero[:, :], all_rhs, start=True, stop=False, skip_group_check=True)
                def turn(i):
                    for n in range(2):
                        pe.wait_ge(oh_ready, 2 * i + n + 1)
                        for e in range(EXPERTS):
                            w = SLOTB * VALS
                            last = nc.tensor.matmul(
                                ps[:, 3, e * w:(e + 1) * w], onehot[n][:, e, :],
                                rhs[:, bass.ds(2 * i + n, 1), e, :, :].rearrange("p t a v -> p (t a v)"),
                                start=False, stop=False, skip_group_check=True)
                        last.then_inc(oh_used, 1)

                looped(pe, TILES // 2, turn)
                nc.tensor.matmul(ps[:, 3, 0:cols], zero[:, :], all_rhs, start=False, stop=True,
                                 skip_group_check=True).then_inc(compacted, 1)

            @block.vector
            def _(dve):
                chain = Chain(dve, steps, 0)
                v = nc.vector
                full = lambda t: t[:, :, :]
                dve.wait_ge(const_in, 16 * 5)
                v.tensor_copy(iota[:, :], iota_f[:, :])
                chain(v.tensor_reduce(top[:, :], logits[:, :, :].rearrange("p e t -> p t e"), AX.X, ALU.max))
                v.tensor_tensor(full(tmp), full(logits), over_experts(top[:, :]), ALU.subtract).then_inc(max_sub, 1)
                dve.wait_ge(exp_ready, 1)
                chain(v.tensor_reduce(den[:, :], probs[:, :, :].rearrange("p e t -> p t e"), AX.X, ALU.add))
                chain(v.reciprocal(den[:, :], den[:, :]))
                chain(v.tensor_tensor(full(probs), full(probs), over_experts(den[:, :]), ALU.mult))
                chain(v.memset(full(rank), 0.0))
                for d in range(1, EXPERTS):
                    lo, hi = probs[:, 0:EXPERTS - d, :], probs[:, d:EXPERTS, :]
                    n = EXPERTS - d
                    v.tensor_tensor(tmp[:, 0:n, :], hi, lo, ALU.is_gt)
                    chain(v.tensor_tensor(tmp2[:, 0:n, :], hi, lo, ALU.is_le))
                    chain(v.tensor_tensor(rank[:, 0:n, :], rank[:, 0:n, :], tmp[:, 0:n, :], ALU.add))
                    chain(v.tensor_tensor(rank[:, d:EXPERTS, :], rank[:, d:EXPERTS, :], tmp2[:, 0:n, :], ALU.add))
                chain(v.tensor_scalar(full(tmp), full(rank), 1.5, None, ALU.is_lt))
                chain(v.tensor_scalar(full(tmp2), full(tmp), 1.0, None, ALU.subtract))
                chain(v.tensor_tensor(full(gate), full(probs), full(tmp), ALU.mult))
                chain(v.tensor_tensor(full(gate), full(gate), full(tmp2), ALU.add))
                v.tensor_copy(gate_t[:, :, :], gate[:, :, :].rearrange("p e t -> p t e")).then_inc(gate_ready, 1)
                v.memset(thr[:, :], 0)
                v.memset(onesrow[:, :], 1.0)
                v.memset(zero[:, :], 0.0)
                chain(v.memset(bit[:, :], 1 << (BITS - 1)))
                with dve.Fori(0, BITS) as i:
                    search = Chain(dve, search_steps, SEARCH * i)
                    search(v.tensor_tensor(cand[:, :], thr[:, :], bit[:, :], ALU.bitwise_or))
                    search(v.tensor_tensor(full(tmp), full(gate), spread(cand[:, :].bitcast(FP32), TILES), ALU.is_ge))
                    v.tensor_reduce(part[:, :], full(tmp), AX.X, ALU.add).then_inc(cmp_ready, 1)
                    search(v.tensor_single_scalar(bit[:, :], bit[:, :], 1, ALU.logical_shift_right))
                    dve.wait_ge(counted, i + 1)
                    search(v.tensor_scalar(keep[:, :], ps[:, 0, 0:EXPERTS], CAP - 0.5, None, ALU.is_ge))
                    dve.sem_inc(passed, 1)
                    search(v.copy_predicated(thr[:, :], keep[:, :], cand[:, :]))
                    assert search.n == SEARCH
                limit = spread(thr[:, :].bitcast(FP32), TILES)
                v.tensor_tensor(full(tmp), full(gate), limit, ALU.is_gt)
                chain(v.tensor_tensor(full(tied), full(gate), limit, ALU.is_equal))

                def running(n, out):
                    dve.wait_ge(prefixed, n + 1)
                    chain(v.tensor_copy(total[:, :, :].rearrange("p e t -> p (e t)"), ps[:, 1, :]))
                    for e in range(EXPERTS):
                        last = v.tensor_tensor_scan(out[:, e, :], onesrow[:, :], total[:, e, :], 0.0, ALU.mult, ALU.add)
                    chain(last)
                    chain(v.tensor_tensor(full(out), full(out), full(total), ALU.subtract))
                    chain(v.tensor_tensor(full(out).rearrange("p e t -> p (e t)"), ps[:, 2, :],
                                          full(out).rearrange("p e t -> p (e t)"), ALU.add))

                v.tensor_copy(part[:, :], part[:, :]).then_inc(prefix_ask, 1)
                dve.wait_ge(prefixed, 1)
                chain(v.tensor_reduce(need[:, :], ps[:, 1, :].rearrange("p (e t) -> p e t", t=TILES), AX.X, ALU.add))
                chain(v.tensor_scalar(need[:, :], need[:, :], -1.0, CAP + 0.5, ALU.mult, ALU.add))
                v.tensor_copy(part[:, :], part[:, :]).then_inc(prefix_ask, 1)
                running(1, slot)
                chain(v.tensor_tensor(full(slot), full(slot), spread(need[:, :], TILES), ALU.is_lt))
                chain(v.tensor_tensor(full(slot), full(slot), full(tied), ALU.mult))
                v.tensor_tensor(full(chosen), full(slot), full(tmp), ALU.add).then_inc(prefix_ask, 1)
                running(2, slot)
                chain(v.tensor_tensor(full(slot), full(slot), full(chosen), ALU.mult))
                chain(v.tensor_scalar(full(slot), full(slot), 1.0, None, ALU.subtract))
                chain(v.tensor_scalar(full(blk), full(slot), P - 0.5, None, ALU.is_ge))
                for a in range(2, SLOTB):
                    chain(v.tensor_scalar(full(tmp), full(slot), a * P - 0.5, None, ALU.is_ge))
                    chain(v.tensor_tensor(full(blk), full(blk), full(tmp), ALU.add))
                chain(v.tensor_scalar(full(tmp), full(blk), -float(P), None, ALU.mult))
                chain(v.tensor_tensor(slot_t[:, :, :].rearrange("p t e -> p e t"), full(slot), full(tmp), ALU.add))
                for a in range(SLOTB):
                    chain(v.tensor_scalar(full(tmp), full(blk), float(a), None, ALU.is_equal))
                    for n in range(VALS):
                        last = v.tensor_tensor(rhs[:, :, :, a, n].rearrange("p t e -> p e t"), full(tmp),
                                               over_experts(tparts[:, :, n]), ALU.mult)
                    chain(last)
                v.tensor_copy(part[:, :], part[:, :]).then_inc(rhs_ready, 1)
                def turn(i):
                    for n in range(2):
                        dve.wait_ge(oh_used, 2 * i)
                        for e in range(EXPERTS):
                            last = v.tensor_scalar(onehot[n][:, e, :], iota[:, :],
                                                   slot_t[:, bass.ds(2 * i + n, 1), e], None, ALU.is_equal)
                        last.then_inc(oh_ready, 1)

                looped(dve, TILES // 2, turn)
                dve.wait_ge(compacted, 1)
                cols = EXPERTS * SLOTB * VALS
                chain(v.tensor_copy(found[:, :, :, :].rearrange("p e a v -> p (e a v)"), ps[:, 3, 0:cols]))
                chain(v.tensor_scalar(full(row_f), found[:, :, :, 1], float(P), None, ALU.mult))
                chain(v.tensor_tensor(full(row_f), full(row_f), found[:, :, :, 2], ALU.add))
                v.tensor_copy(full(gather_row), full(row_f))
                chain(v.tensor_copy(full(occupied), found[:, :, :, 0]))
                chain(v.tensor_scalar(full(row_g), full(occupied), -1.0, 1.0, ALU.mult, ALU.add))
                chain(v.tensor_tensor(full(row_g), full(row_g),
                                      slots[:, :].rearrange("p (o a) -> p o a", o=1)
                                      .broadcast_to((P, EXPERTS, SLOTB)), ALU.mult))
                chain(v.tensor_tensor(full(row_g), full(row_g), full(row_f), ALU.add))
                chain(v.tensor_copy(full(scatter_row), full(row_g)))


def experts(nc, w1_in, w2_in, g2, identity, h_d, z_d, occupied, gather_row, scatter_row):
    FC = FFN // P
    HW = E + EXPERTS
    size = [min(P, CAP - s * P) for s in range(SLOTB)]
    with ExitStack() as ctx:
        sb = lambda name, shape, dt=FP32: ctx.enter_context(nc.sbuf_tensor("e_" + name, shape, dt))
        sem = lambda name: ctx.enter_context(nc.semaphore("e_" + name))
        pair = lambda name: [sem(f"{name}{n}") for n in range(2)]
        ident = sb("ident", [P, P])
        g2c = sb("g2c", [P, KC])
        w1 = [sb(f"w1{n}", [P, KC, FFN]) for n in range(2)]
        w2 = [sb(f"w2{n}", [P, FC, E]) for n in range(2)]
        xe = [sb(f"xe{n}", [P, SLOTB, HW]) for n in range(2)]
        xet = sb("xet", [P, KC, CAP])
        ht = sb("ht", [P, FC, CAP])
        gates = [sb(f"gates{n}", [P, SLOTB]) for n in range(2)]
        ye = [sb(f"ye{n}", [P, SLOTB, E]) for n in range(2)]
        ps = ctx.enter_context(nc.psum_tensor("e_ps", [P, 8, 512], FP32))
        const_in, w_in, xe_in, added = sem("const_in"), pair("w_in"), pair("xe_in"), sem("added")
        flipped, xet_ready, up, ht_ready = sem("flipped"), sem("xet_ready"), sem("up"), sem("ht_ready")
        down, gates_ready, ye_ready = sem("down"), sem("gates_ready"), sem("ye_ready")

        with nc.Block() as block:

            @block.sync
            def _(sp):
                sp.dma_start(ident[:, :], identity).then_inc(const_in, 16)
                sp.dma_start(g2c[:, :], g2).then_inc(const_in, 16)
                def turn(i):
                    for n in range(2):
                        sp.wait_ge(down, SLOTB * 2 * i)
                        sp.dma_start(w1[n][:, :, :], w1_in[2 * i + n, :, :].rearrange("(k p) f -> p k f", p=P)
                                     ).then_inc(w_in[n], 16)
                        sp.dma_start(w2[n][:, :, :], w2_in[2 * i + n, :, :].rearrange("(k p) f -> p k f", p=P)
                                     ).then_inc(w_in[n], 16)

                looped(sp, EXPERTS // 2, turn)

            @block.gpsimd
            def _(pool):
                def gather(e):
                    if e >= 2:
                        pool.wait_ge(flipped, e - 1)
                        pool.wait_ge(gates_ready, e - 1)
                    for s in range(SLOTB):
                        pool.indirect_dma_start(
                            out=xe[e % 2][0:size[s], s, :], out_offset=None, in_=h_d[:, :],
                            in_offset=bass.IndirectOffsetOnAxis(ap=gather_row[0:size[s], e, s:s + 1], axis=0),
                        ).then_inc(xe_in[e % 2], 16)

                gather(0)
                for e in range(EXPERTS):
                    if e + 1 < EXPERTS:
                        gather(e + 1)
                    pool.wait_ge(ye_ready, SLOTB * (e + 1))
                    if e:
                        pool.wait_ge(added, 16 * SLOTB * e)
                    for s in range(SLOTB):
                        pool.indirect_dma_start(
                            out=z_d[:, :],
                            out_offset=bass.IndirectOffsetOnAxis(ap=scatter_row[0:size[s], e, s:s + 1], axis=0),
                            in_=ye[e % 2][0:size[s], s, :], in_offset=None, compute_op=ALU.add,
                        ).then_inc(added, 16)
                pool.wait_ge(added, 16 * SLOTB * EXPERTS)

            @block.tensor
            def _(pe):
                pe.wait_ge(const_in, 32)
                def turn(i):
                    for n in range(2):
                        e = 2 * i + n
                        pe.wait_ge(xe_in[n], 16 * SLOTB * (i + 1))
                        pe.wait_ge(xet_ready, KC * e)
                        for k in range(KC):
                            for s in range(SLOTB):
                                last = nc.tensor.transpose(ps[:, k, s * P:s * P + size[s]],
                                                           xe[n][0:size[s], s, k * P:(k + 1) * P],
                                                           ident[0:size[s], 0:size[s]])
                        last.then_inc(flipped, 1)
                        pe.wait_ge(w_in[n], 32 * (i + 1))
                        pe.wait_ge(xet_ready, KC * e + KC)
                        for f in range(FC):
                            pe.wait_ge(ht_ready, FC * e + max(f - 1, 0))
                            for k in range(KC):
                                last = nc.tensor.matmul(ps[:, 2 + f % 2, 0:CAP], w1[n][:, k, f * P:(f + 1) * P],
                                                        xet[:, k, :], start=(k == 0), stop=(k == KC - 1))
                            last.then_inc(up, 1)
                        pe.wait_ge(ht_ready, FC * (e + 1))
                        pe.wait_ge(ye_ready, SLOTB * e)
                        for s in range(SLOTB):
                            for f in range(FC):
                                last = nc.tensor.matmul(ps[0:size[s], 4 + s, 0:E], ht[:, f, s * P:s * P + size[s]],
                                                        w2[n][:, f, :], start=(f == 0), stop=(f == FC - 1))
                            last.then_inc(down, 1)

                looped(pe, EXPERTS // 2, turn)

            @block.scalar
            def _(act):
                act.wait_ge(const_in, 32)
                def turn(i):
                    for n in range(2):
                        e = 2 * i + n
                        act.wait_ge(flipped, e + 1)
                        act.wait_ge(up, FC * e)
                        for k in range(KC):
                            nc.scalar.activation(xet[:, k, :], ps[:, k, 0:CAP], ACT.Copy,
                                                 scale=g2c[:, k:k + 1]).then_inc(xet_ready, 1)
                        act.wait_ge(down, SLOTB * e)
                        for f in range(FC):
                            act.wait_ge(up, FC * e + f + 1)
                            nc.scalar.activation(ht[:, f, :], ps[:, 2 + f % 2, 0:CAP], ACT.Relu).then_inc(ht_ready, 1)

                looped(act, EXPERTS // 2, turn)

            @block.vector
            def _(dve):
                def turn(i):
                    for n in range(2):
                        e = 2 * i + n
                        dve.wait_ge(xe_in[n], 16 * SLOTB * (i + 1))
                        full, rest = SLOTB - 1, size[-1]
                        nc.vector.tensor_tensor(gates[n][:, 0:full], xe[n][:, 0:full, bass.ds(E + e, 1)]
                                                .rearrange("p s o -> p (s o)"),
                                                occupied[:, bass.ds(e, 1), 0:full].rearrange("p o s -> p (o s)"), ALU.mult)
                        nc.vector.tensor_tensor(gates[n][0:rest, full:], xe[n][0:rest, full:, bass.ds(E + e, 1)]
                                                .rearrange("p s o -> p (s o)"),
                                                occupied[0:rest, bass.ds(e, 1), full:].rearrange("p o s -> p (o s)"),
                                                ALU.mult).then_inc(gates_ready, 1)
                        dve.wait_ge(gates_ready, e + 1)
                        dve.wait_ge(added, 16 * SLOTB * 2 * i)
                        for s in range(SLOTB):
                            dve.wait_ge(down, SLOTB * e + s + 1)
                            nc.vector.tensor_scalar(ye[n][0:size[s], s, :], ps[0:size[s], 4 + s, 0:E],
                                                    gates[n][0:size[s], s:s + 1], None,
                                                    ALU.mult).then_inc(ye_ready, 1)

                looped(dve, EXPERTS // 2, turn)


def finish(nc, x, w_out_t, bo_rows, identity, y_d, z_d, out):
    with ExitStack() as ctx:
        sb = lambda name, shape, dt=FP32: ctx.enter_context(nc.sbuf_tensor("f_" + name, shape, dt))
        sem = lambda name: ctx.enter_context(nc.semaphore("f_" + name))
        pair = lambda name: [sem(f"{name}{n}") for n in range(2)]
        wo = sb("wo", [P, KC, E])
        bo = sb("bo", [P, E])
        ident = sb("ident", [P, P])
        xin = [sb(f"x{n}", [P, CT, E]) for n in range(2)]
        z = [sb(f"z{n}", [P, CT, E]) for n in range(2)]
        g = [sb(f"g{n}", [P, CT, E]) for n in range(2)]
        s_sb = [sb(f"s{n}", [P, CT, E]) for n in range(2)]
        res = [sb(f"res{n}", [P, CT, E]) for n in range(2)]
        ps = ctx.enter_context(nc.psum_tensor("f_ps", [P, 6, 512], FP32))
        w_in, x_in, z_in, out_out = sem("w_in"), pair("x_in"), pair("z_in"), pair("out_out")
        g_ready, gated, res_ready = sem("g_ready"), sem("gated"), sem("res_ready")
        heads = HeadsOut(nc, ctx, "f_out", ps, 1, wo, ident, y_d)

        def rows(b, half):
            return bass.ds(b * T + half * CH, CH)

        with nc.Block() as block:

            @block.sync
            def _(sp):
                for dst, src in ((wo[:, :, :], w_out_t.rearrange("(k p) n -> p k n", p=P)),
                                 (bo[:, :], bo_rows.broadcast_to((P, E))), (ident[:, :], identity)):
                    sp.dma_start(dst, src).then_inc(w_in, 16)

                def load(b, half):
                    heads.load(sp, b, half)
                    for dst, src, s in ((xin, x, x_in), (z, z_d, z_in)):
                        sp.dma_start(dst[half][:, :, :], src[rows(b, half), :].rearrange("(t p) e -> p t e", p=P)
                                     ).then_inc(s[half], 16)

                load(0, 0)
                load(0, 1)
                def turn(b):
                    for half in range(2):
                        sp.wait_ge(res_ready, 2 * b + half + 1)
                        load(b + 1, half)

                looped(sp, B - 1, turn)

            @block.gpsimd
            def _(pool):
                def turn(b):
                    for half in range(2):
                        pool.wait_ge(res_ready, 2 * b + half + 1)
                        pool.dma_start(out[rows(b, half), :].rearrange("(t p) e -> p t e", p=P), res[half][:, :, :]
                                       ).then_inc(out_out[half], 16)

                looped(pool, B, turn)
                for half in range(2):
                    pool.wait_ge(out_out[half], 16 * B)

            @block.tensor
            def _(pe):
                pe.wait_ge(w_in, 16 * 3)
                def turn(b):
                    for half in range(2):
                        heads.tensor(pe, b, half)

                looped(pe, B, turn)

            @block.scalar
            def _(act):
                def turn(b):
                    for half in range(2):
                        act.wait_ge(z_in[half], 16 * b + 16)
                        nc.scalar.activation(g[half][:, :, :], z[half][:, :, :], ACT.Silu).then_inc(g_ready, 1)
                        for t in range(CT):
                            heads.scalar(act, b, half, t)

                looped(act, B, turn)

            @block.vector
            def _(dve):
                dve.wait_ge(w_in, 16 * 3)
                def turn(b):
                    for half in range(2):
                        c = 2 * b + half
                        dve.wait_ge(x_in[half], 16 * b + 16)
                        dve.wait_ge(out_out[half], 16 * b)
                        for t in range(CT + 2):
                            if t < CT:
                                heads.vector(dve, b, half, t)
                            if t >= 2:
                                dve.wait_ge(heads.projected, CT * c + t - 1)
                                nc.vector.tensor_tensor(s_sb[half][:, t - 2, :], ps[:, 4 + t % 2, 0:E], bo[:, :],
                                                        ALU.add).then_inc(heads.taken, 1)
                        dve.wait_ge(heads.taken, CT * (c + 1))
                        dve.wait_ge(g_ready, c + 1)
                        nc.vector.tensor_tensor(s_sb[half][:, :, :], s_sb[half][:, :, :], g[half][:, :, :],
                                                ALU.mult).then_inc(gated, 1)
                        dve.wait_ge(gated, c + 1)
                        nc.vector.tensor_tensor(res[half][:, :, :], s_sb[half][:, :, :], xin[half][:, :, :],
                                                ALU.add).then_inc(res_ready, 1)

                looped(dve, B, turn)


def program(nc, x, w_main_t, w_out_t, bo, g1, w_qkv, w_o, g2, w_router, w1, w2, rope_main, rope_head, identity,
            causal_mask, ones, upper, iota, token_parts, slot_rows, out):
    scratch = lambda name, shape, dt=FP32: nc.dram_tensor(name, shape, dt, kind="Internal").ap()
    xn_d = scratch("xn_scratch", (TOK, E))
    qk_d = scratch("qk_scratch", (UNITS, 2, PARTS, GH * HD, T), BF16)
    v_d = scratch("v_scratch", (UNITS, T, GH * VW))
    y_d = scratch("y_scratch", (UNITS, P, T))
    z_d = scratch("z_scratch", (TOK + SLOTB * P, E))
    h_d = scratch("h_scratch", (TOK, E + EXPERTS))
    project(nc, x, w_main_t, w_qkv, g1, rope_main, rope_head, identity, xn_d, qk_d, v_d)
    attend(nc, identity, causal_mask, qk_d, v_d, y_d)
    with ExitStack() as ctx:
        keep = lambda name, shape, dt=FP32: ctx.enter_context(nc.sbuf_tensor(name, shape, dt))
        logits = keep("logits", [P, EXPERTS, TILES])
        occupied = keep("occupied", [P, EXPERTS, SLOTB])
        gather_row = keep("gather_row", [P, EXPERTS, SLOTB], U32)
        scatter_row = keep("scatter_row", [P, EXPERTS, SLOTB], U32)
        block_mid(nc, w_o, w_router, g2, identity, xn_d, y_d, z_d, h_d, logits)
        route(nc, ones, upper, iota, token_parts, slot_rows, h_d, logits, occupied, gather_row, scatter_row)
        experts(nc, w1, w2, g2, identity, h_d, z_d, occupied, gather_row, scatter_row)
    finish(nc, x, w_out_t, bo, identity, y_d, z_d, out)


def _constants(np):
    def rotary(width, exponents):
        theta = np.repeat((10000.0 ** exponents).astype(np.float32), 2)
        angle = (np.arange(T, dtype=np.float32)[:, None] * theta[None, :]).astype(np.float64)
        sign = np.where(np.arange(width) % 2 == 0, -1.0, 1.0)
        return np.stack([np.cos(angle), np.sin(angle) * sign]).astype(np.float32)

    row, col = np.arange(P)[:, None], np.arange(P)[None, :]
    eye = (row == col).astype(np.float32)
    mask = np.zeros((P, 512), np.float32)
    mask[:, 512 - P:] = np.where(col > row, -BIG, 0.0)
    parts = np.zeros((P, TILES, 3), np.float32)
    parts[:, :, 0] = 1.0
    parts[:, :, 1] = np.arange(TILES)[None, :]
    parts[:, :, 2] = np.arange(P)[:, None]
    return {
        "rope_main": rotary(E, -np.arange(0, E, 2) / E),
        "rope_head": rotary(HD, -2.0 * np.arange(HD // 2) / HD),
        "identity": eye,
        "causal_mask": mask,
        "ones": np.ones((P, P), np.float32),
        "upper": (col >= row).astype(np.float32),
        "iota": np.broadcast_to(col, (P, P)).astype(np.float32),
        "token_parts": parts,
        "slot_rows": (TOK + np.arange(SLOTB)[None, :] * P + np.arange(P)[:, None]).astype(np.float32),
    }


def kernel(**inputs):
    import numpy as np
    import concourse.bacc as bacc
    from concourse.bass_utils import run_bass_kernel_spmd

    a = {k: np.asarray(v) for k, v in inputs.items()}
    columns = lambda v: np.ascontiguousarray(v.reshape(KC, P).T)
    arrays = {
        "x": a["L0_attn_input"].reshape(TOK, E),
        "w_main_t": np.concatenate([a["L0_attn_Wq"].T, a["L0_attn_Wk"].T, a["L0_attn_Wv"].T], axis=1),
        "w_out_t": np.ascontiguousarray(a["L0_attn_Wo"].T),
        "bo": a["L0_attn_bo"].reshape(1, E),
        "g1": columns(a["L0_ffn_g1"]),
        "w_qkv": a["L0_ffn_w_qkv"],
        "w_o": a["L0_ffn_w_o"],
        "g2": columns(a["L0_ffn_g2"]),
        "w_router": a["L0_ffn_w_router"],
        "w1": a["L0_ffn_w1"],
        "w2": a["L0_ffn_w2"],
        **_constants(np),
    }
    nc = bacc.Bacc("TRN2", target_bir_lowering=False, num_devices=1)
    args, maps = [], {}
    for name, array in arrays.items():
        maps[f"in_{name}"] = np.ascontiguousarray(array)
        args.append(nc.dram_tensor(f"in_{name}", array.shape, mybir.dt.from_np(array.dtype), kind="ExternalInput").ap())
    args.append(nc.dram_tensor("out_y", (TOK, E), FP32, kind="ExternalOutput").ap())
    program(nc, *args)
    result = run_bass_kernel_spmd(nc, [maps], core_ids=[0])
    return result.results[0]["out_y"].reshape(B, T, E)
```

```python
from contextlib import ExitStack

import concourse.bass as bass
from concourse import mybir

FP32, BF16 = mybir.dt.float32, mybir.dt.bfloat16
I32, U32 = mybir.dt.int32, mybir.dt.uint32
ALU = mybir.AluOpType
ACT = mybir.ActivationFunctionType
AX = mybir.AxisListType

B, T, E = 8, 1024, 256
TOK = B * T
P = 128
HEADS, HD = 16, 16
GROUPS, GH = 4, 4
KC = E // P
CH = 512
CT = CH // P
TT = T // P
TILES = TOK // P
UNITS = 2 * B * GROUPS
UB = B * GROUPS
VW = 32
YW = HD + 1
PARTS = 3
Q_PART = (0, 0, 1, 1, 0, 2)
K_PART = (0, 1, 0, 1, 2, 0)
BANDS = len(Q_PART)
SROWS = BANDS * HD
EXPERTS, FFN, CAP = 8, 512, 320
SLOTB = (CAP + P - 1) // P
LN_EPS, RMS_EPS = 1e-5, 1e-6
BIG = 3e38


def apart(engine, sem, value, passed):
    engine.wait_ge(sem, value)
    engine.sem_inc(passed, 1)


def looped(engine, count, body):
    body(0)
    with engine.Fori(1, count) as i:
        body(i)


def at_least(engine, sem, value):
    if not isinstance(value, int) or value > 0:
        engine.wait_ge(sem, value)


def over_quarters(engine, step, first, loop_end, end):
    def turn(b):
        for half in range(2):
            def chunk(d, half=half):
                bb, hh = b + (half + d) // 2, (half + d) % 2
                return (bb, hh, 2 * bb + hh) if not isinstance(b, int) or 0 <= bb < B else None

            for q in range(4):
                step(chunk, q)

    for b in range(first, 1):
        turn(b)
    with engine.Fori(1, loop_end) as b:
        turn(b)
    for b in range(loop_end, end):
        turn(b)


def ago(chunk, q, n):
    return chunk((q - n) // 4), (q - n) % 4


class Chain:

    def __init__(self, engine, sem, base):
        self.engine, self.sem, self.base, self.n = engine, sem, base, 0

    def __call__(self, instruction):
        self.n += 1
        instruction.then_inc(self.sem, 1)
        self.engine.wait_ge(self.sem, self.base + self.n)


NORM_STEPS = 4


def project(nc, x, w_main_t, w_qkv, g1, rope_main, rope_head, identity, xn_d, qk_d, v_d):
    with ExitStack() as ctx:
        sb = lambda name, shape, dt=FP32: ctx.enter_context(nc.sbuf_tensor("a_" + name, shape, dt))
        sem = lambda name: ctx.enter_context(nc.semaphore("a_" + name))
        pair = lambda name: [sem(f"{name}{n}") for n in range(2)]

        w1 = sb("w1", [P, KC, 3 * E])
        w2 = sb("w2", [P, KC, 3 * E])
        g1c = sb("g1c", [P, KC])
        ident = sb("ident", [P, P])
        cs1 = sb("cs1", [P, 2, TT, E])
        cs2 = sb("cs2", [P, 2, TT, HD])
        xin = [sb(f"xin{n}", [P, CT, E]) for n in range(2)]
        xn = [sb(f"xn{n}", [P, CT, E]) for n in range(2)]
        xr = [sb(f"xr{n}", [P, CT, E]) for n in range(2)]
        rx = [sb(f"rx{n}", [P, CT, E]) for n in range(2)]
        rope_a = sb("rope_a", [P, CT, E])
        rope_b = sb("rope_b", [P, CT, E])
        junk = sb("junk", [P, CT, E])
        stats = sb("stats", [P, CT, 6])
        mv = sb("mv", [P, CT, 2])
        var = sb("var", [P, CT])
        rstd = sb("rstd", [P, CT])
        ssq = sb("ssq", [P, CT])
        ms = sb("ms", [P, CT])
        rrms = sb("rrms", [P, CT])
        neghalf = sb("neghalf", [P, CT])
        xt = [sb(f"xt{n}", [P, 3, KC, CH]) for n in range(2)]
        qkr = [sb(f"qkr{n}", [P, CT, 2 * E]) for n in range(2)]
        ra = sb("ra", [P, 2, 2 * E])
        rb = sb("rb", [P, 2, 2 * E])
        main_parts = [sb(f"main_parts{n}", [P, PARTS, CH], BF16) for n in range(2)]
        main_rest = [sb(f"main_rest{n}", [P, CH]) for n in range(2)]
        turned_parts = [sb(f"turned_parts{n}", [P, PARTS, CH], BF16) for n in range(2)]
        turned_rest = [sb(f"turned_rest{n}", [P, CH]) for n in range(2)]
        vst = [sb(f"vst{n}", [P, 2, CT, HEADS, VW]) for n in range(2)]
        ps = ctx.enter_context(nc.psum_tensor("a_ps", [P, 8, 512], FP32))

        w_in = sem("w_in")
        x_in = pair("x_in")
        xn_out = pair("xn_out")
        v_out = pair("v_out")
        main_out = pair("main_out")
        turned_out = pair("turned_out")
        consts = sem("consts")
        vconst = sem("vconst")
        w_ready = sem("w_ready")
        var_ready, rsq, dchain, passed = sem("var_ready"), sem("rsq"), sem("dchain"), sem("passed")
        roped, rx_ready, xr_ready = sem("roped"), sem("rx_ready"), sem("xr_ready")
        flipped, xt_ready = sem("flipped"), sem("xt_ready")
        qk_done, qk_read, rotated = sem("qk_done"), sem("qk_read"), sem("rotated")
        v_done, v_read = sem("v_done"), sem("v_read")
        main_done, main_hi, main_read = sem("main_done"), sem("main_hi"), sem("main_read")
        main_mid, main_lo = sem("main_mid"), sem("main_lo")
        turned_done, turned_hi, turned_read = sem("turned_done"), sem("turned_hi"), sem("turned_read")
        turned_mid, turned_lo = sem("turned_mid"), sem("turned_lo")

        def chunk_rows(b, half):
            return bass.ds(b * T + half * CH, CH)

        def run(engine, step):
            over_quarters(engine, step, -1, B - 2, B + 1)

        with nc.Block() as block:

            @block.sync
            def _(sp):
                for dst, src in ((w1[:, :, :], w_main_t.rearrange("(k p) n -> p k n", p=P)),
                                 (w2[:, :, :], w_qkv.rearrange("(k p) n -> p k n", p=P)),
                                 (g1c[:, :], g1),
                                 (ident[:, :], identity),
                                 (cs1[:, :, :, :], rope_main.rearrange("c (t p) e -> p c t e", p=P)),
                                 (cs2[:, :, :, :], rope_head.rearrange("c (t p) e -> p c t e", p=P))):
                    sp.dma_start(dst, src).then_inc(w_in, 16)

                def store_parts(b, half, q, a, lo, parts, out):
                    c = 2 * b + half
                    sp.wait_ge(lo, CT * c + q + 1)
                    for gi in range(2):
                        unit = b * GROUPS + (a * UB + 2 * (q % 2) + gi)
                        sp.dma_start(qk_d[unit, q // 2, :, :, half * CH:(half + 1) * CH].rearrange("s r t -> r s t"),
                                     parts[q % 2][64 * gi:64 * gi + 64, :, :]).then_inc(out[q % 2], 16)

                def step(chunk, q):
                    if q == 2 and chunk(2):
                        b, half, c = chunk(2)
                        sp.wait_ge(var_ready, 2 * c + 2)
                        sp.dma_start(xn_d[chunk_rows(b, half), :].rearrange("(t p) e -> p t e", p=P),
                                     xn[half][:, :, :]).then_inc(xn_out[half], 16)
                    if q == 0 and chunk(-1):
                        b, half, c = chunk(-1)
                        sp.wait_ge(v_read, CT * (c + 1))
                        for a in range(2):
                            for g in range(GROUPS):
                                unit = b * GROUPS + (a * UB + g)
                                sp.dma_start(
                                    v_d[unit, half * CH:(half + 1) * CH, :].rearrange("(t p) n -> p t n", p=P),
                                    vst[half][:, a, :, g * GH:(g + 1) * GH, :].rearrange("p t h v -> p t (h v)"),
                                ).then_inc(v_out[half], 16)
                    at, p = ago(chunk, q, 1)
                    if at:
                        store_parts(at[0], at[1], p, 1, main_lo, main_parts, main_out)
                    at, p = ago(chunk, q, 5)
                    if at:
                        store_parts(at[0], at[1], p, 0, turned_lo, turned_parts, turned_out)

                run(sp, step)
                for half in range(2):
                    sp.wait_ge(xn_out[half], 16 * B)
                    sp.wait_ge(v_out[half], 16 * 2 * GROUPS * B)
                    sp.wait_ge(main_out[half], 16 * 2 * 2 * 2 * B)
                    sp.wait_ge(turned_out[half], 16 * 2 * 2 * 2 * B)

            @block.gpsimd
            def _(pool):
                def load(b, half):
                    pool.dma_start(xin[half][:, :, :],
                                   x[chunk_rows(b, half), :].rearrange("(t p) e -> p t e", p=P)
                                   ).then_inc(x_in[half], 16)

                load(0, 0)
                load(0, 1)
                nc.gpsimd.memset(neghalf[:, :], -0.5).then_inc(consts, 1)
                for n in range(2):
                    nc.gpsimd.memset(vst[n][:, :, :, :, HD + 1:VW], 0.0).then_inc(vconst, 1)
                    nc.gpsimd.memset(vst[n][:, :, :, :, HD:HD + 1], 1.0).then_inc(vconst, 1)
                pool.wait_ge(consts, 1)

                def low(c, q, mid, rest, parts, lo):
                    pool.wait_ge(mid, CT * c + q + 1)
                    nc.gpsimd.tensor_tensor(out=parts[q % 2][:, 2, :], in0=rest[q % 2][:, :],
                                            in1=parts[q % 2][:, 1, :], op=ALU.subtract).then_inc(lo, 1)

                def step(chunk, q):
                    if q == 3 and chunk(2):
                        _, half, c = chunk(2)
                        at_least(pool, flipped, CT * (c - 1))
                        pool.wait_ge(roped, c + 1)
                        nc.gpsimd.tensor_tensor(out=rx[half][:, :, :], in0=rope_a[:, :, :], in1=rope_b[:, :, :],
                                                op=ALU.add).then_inc(rx_ready, 1)
                    at, p = ago(chunk, q, 1)
                    if at:
                        low(at[2], p, main_mid, main_rest, main_parts, main_lo)
                    at, p = ago(chunk, q, 5)
                    if at:
                        low(at[2], p, turned_mid, turned_rest, turned_parts, turned_lo)
                    if chunk(2):
                        c = chunk(2)[2]
                        if q == 0:
                            pool.wait_ge(var_ready, 2 * c + 1)
                            nc.gpsimd.tensor_tensor(out=rstd[:, :], in0=var[:, :], in1=neghalf[:, :],
                                                    op=ALU.pow).then_inc(rsq, 1)
                        elif q == 1:
                            at_least(pool, xr_ready, c)
                            pool.wait_ge(var_ready, 2 * c + 2)
                            nc.gpsimd.tensor_tensor(out=rrms[:, :], in0=ms[:, :], in1=neghalf[:, :],
                                                    op=ALU.pow).then_inc(rsq, 1)
                        elif q == 2 and chunk(4):
                            load(chunk(4)[0], chunk(4)[1])

                run(pool, step)

            @block.vector
            def _(dve):
                def scale_weights():
                    dve.wait_ge(w_in, 16 * 6)
                    for k in range(KC):
                        nc.vector.tensor_scalar(w2[:, k, :], w2[:, k, :], g1c[:, k:k + 1], None,
                                                ALU.mult).then_inc(w_ready, 1)
                    dve.wait_ge(w_ready, KC)
                    nc.vector.tensor_scalar(w1[:, :, 0:E], w1[:, :, 0:E], 0.25, None, ALU.mult).then_inc(w_ready, 1)
                    nc.vector.tensor_scalar(w2[:, :, 0:E], w2[:, :, 0:E], 0.25, None, ALU.mult).then_inc(w_ready, 1)

                def norms(b, half, c, q):
                    chain = Chain(dve, dchain, c * NORM_STEPS)
                    if q == 0:
                        dve.wait_ge(x_in[half], 16 * b + 16)
                        for t in range(CT):
                            last = nc.vector.bn_stats(stats[:, t, :], xin[half][:, t, :])
                        chain(last)
                        dve.sem_inc(passed, 1)
                        for t in range(CT):
                            last = nc.vector.bn_aggr(mv[:, t, :], stats[:, t, :])
                        chain(last)
                        nc.vector.tensor_scalar(var[:, :], mv[:, :, 1], LN_EPS, None, ALU.add).then_inc(var_ready, 1)
                    elif q == 1:
                        chain.n = 2
                        at_least(dve, flipped, CT * (c - 1))
                        at_least(dve, xn_out[half], 16 * b)
                        dve.wait_ge(rsq, 2 * c + 1)
                        for t in range(CT):
                            last = nc.vector.tensor_scalar(xn[half][:, t, :], xin[half][:, t, :], mv[:, t, 0:1],
                                                           rstd[:, t:t + 1], ALU.subtract, ALU.mult)
                        chain(last)
                        for t in range(CT):
                            last = nc.vector.tensor_tensor_reduce(
                                out=junk[:, t, :], in0=xn[half][:, t, :], in1=xn[half][:, t, :], scale=1.0,
                                scalar=0.0, op0=ALU.mult, op1=ALU.add, accum_out=ssq[:, t:t + 1])
                        chain(last)
                        nc.vector.tensor_scalar(ms[:, :], ssq[:, :], 1.0 / E, RMS_EPS, ALU.mult,
                                                ALU.add).then_inc(var_ready, 1)
                    elif q == 2:
                        if isinstance(c, int) and c == 0:
                            scale_weights()
                        at_least(dve, rx_ready, c)
                        cos = cs1[:, 0, half * CT:(half + 1) * CT, :]
                        sin = cs1[:, 1, half * CT:(half + 1) * CT, :]
                        nc.vector.tensor_tensor(rope_a[:, :, :], xn[half][:, :, :], cos, ALU.mult)
                        for o in range(2):
                            last = nc.vector.tensor_tensor(rope_b[:, :, o::2], xn[half][:, :, 1 - o::2],
                                                           sin[:, :, o::2], ALU.mult)
                        last.then_inc(roped, 1)

                def rotate(half, c, t):
                    s = CT * c + t
                    cos = cs2[:, 0, half * CT + t, :].rearrange("p (o d) -> p o d", o=1).broadcast_to((P, 2 * HEADS, HD))
                    sin = cs2[:, 1, half * CT + t, :].rearrange("p (o d) -> p o d", o=1).broadcast_to((P, 2 * HEADS, HD))
                    qk = ps[:, 4, :].rearrange("p (h d) -> p h d", d=HD)
                    ra_v = ra[:, t % 2, :].rearrange("p (h d) -> p h d", d=HD)
                    rb_v = rb[:, t % 2, :].rearrange("p (h d) -> p h d", d=HD)
                    at_least(dve, rotated, s - 1)
                    if t == 0:
                        at_least(dve, turned_done, CT * (c - 1))
                    dve.wait_ge(qk_done, s + 1)
                    nc.vector.tensor_tensor(ra_v, qk, cos, ALU.mult)
                    nc.vector.tensor_tensor(rb_v[:, :, 0::2], qk[:, :, 1::2], sin[:, :, 0::2], ALU.mult)
                    nc.vector.tensor_tensor(rb_v[:, :, 1::2], qk[:, :, 0::2], sin[:, :, 1::2],
                                            ALU.mult).then_inc(qk_read, 1)
                    dve.wait_ge(qk_read, s + 1)
                    nc.vector.tensor_tensor(qkr[half][:, t, :], ra[:, t % 2, :], rb[:, t % 2, :],
                                            ALU.add).then_inc(rotated, 1)

                def rest_of(c, q, bank, hi, lo, rest, parts, read):
                    s = CT * c + q
                    dve.wait_ge(hi, s + 1)
                    at_least(dve, lo, s - 1)
                    nc.vector.tensor_tensor(rest[q % 2][:, :], ps[:, bank, :], parts[q % 2][:, 0, :],
                                            ALU.subtract).then_inc(read, 1)

                def step(chunk, q):
                    if chunk(0):
                        rotate(chunk(0)[1], chunk(0)[2], q)
                    if chunk(2):
                        norms(*chunk(2), q)
                    if chunk(0):
                        rest_of(chunk(0)[2], q, 6, main_hi, main_lo, main_rest, main_parts, main_read)
                    if chunk(-1):
                        rest_of(chunk(-1)[2], q, 7, turned_hi, turned_lo, turned_rest, turned_parts, turned_read)

                run(dve, step)

            @block.scalar
            def _(act):
                act.wait_ge(vconst, 4)

                def high(c, q, bank, done, out, parts, hi):
                    act.wait_ge(done, CT * c + q + 1)
                    at_least(act, out[q % 2], 32 * (2 * c + q // 2))
                    nc.scalar.copy(parts[q % 2][:, 0, :], ps[:, bank, :]).then_inc(hi, 1)

                def middle(c, q, read, rest, parts, mid):
                    act.wait_ge(read, CT * c + q + 1)
                    nc.scalar.copy(parts[q % 2][:, 1, :], rest[q % 2][:, :]).then_inc(mid, 1)

                def step(chunk, q):
                    if q == 3 and chunk(2):
                        _, half, c = chunk(2)
                        at_least(act, flipped, CT * (c - 1))
                        act.wait_ge(rsq, 2 * c + 2)
                        for t in range(CT):
                            last = nc.scalar.mul(xr[half][:, t, :], xn[half][:, t, :], rrms[:, t:t + 1])
                        last.then_inc(xr_ready, 1)
                    if chunk(1):
                        _, half, c = chunk(1)
                        bank = 2 * (q % 2)
                        act.wait_ge(flipped, CT * c + q + 1)
                        nc.scalar.copy(xt[half][:, :, :, q * P:(q + 1) * P].rearrange("p s k t -> p (s k) t"),
                                       ps[:, bank:bank + 2, :].rearrange("p b c -> p (b c)")[:, 0:6 * P]
                                       .rearrange("p (s t) -> p s t", t=P)).then_inc(xt_ready, 1)
                    at, p = ago(chunk, q, 1)
                    if at:
                        middle(at[2], p, main_read, main_rest, main_parts, main_mid)
                    at, p = ago(chunk, q, 5)
                    if at:
                        middle(at[2], p, turned_read, turned_rest, turned_parts, turned_mid)
                    if chunk(0):
                        b, half, c = chunk(0)
                        if q == 0:
                            at_least(act, v_out[half], 16 * 2 * GROUPS * b)
                        act.wait_ge(v_done, CT * c + q + 1)
                        nc.scalar.copy(vst[half][:, :, q, :, 0:HD],
                                       ps[:, 5, :].rearrange("p (a h d) -> p a h d", a=2, d=HD)).then_inc(v_read, 1)
                        high(c, q, 6, main_done, main_out, main_parts, main_hi)
                    if chunk(-1):
                        high(chunk(-1)[2], q, 7, turned_done, turned_out, turned_parts, turned_hi)

                run(act, step)

            @block.tensor
            def _(pe):
                pe.wait_ge(w_in, 16 * 6)
                pe.wait_ge(w_ready, KC + 2)

                def step(chunk, q):
                    if chunk(1):
                        _, half, c = chunk(1)
                        if q == 0:
                            pe.wait_ge(rx_ready, c + 1)
                            pe.wait_ge(xr_ready, c + 1)
                        at_least(pe, xt_ready, CT * c + q - 1)
                        for s, src in enumerate((xn[half], rx[half], xr[half])):
                            for k in range(KC):
                                col = (s * KC + k) * P
                                last = nc.tensor.transpose(ps[:, 2 * (q % 2) + col // 512, col % 512:col % 512 + P],
                                                           src[:, q, k * P:(k + 1) * P], ident[:, :])
                        last.then_inc(flipped, 1)
                    if chunk(0):
                        _, half, c = chunk(0)
                        s = CT * c + q
                        tok = slice(q * P, (q + 1) * P)
                        if q == 0:
                            pe.wait_ge(xt_ready, CT * (c + 1))
                        at_least(pe, qk_read, s)
                        for k in range(KC):
                            last = nc.tensor.matmul(ps[:, 4, :], xt[half][:, 2, k, tok], w2[:, k, 0:2 * E],
                                                    start=(k == 0), stop=(k == KC - 1))
                        last.then_inc(qk_done, 1)
                        at_least(pe, v_read, s)
                        for a, (src, w) in enumerate(((2, w2), (0, w1))):
                            for k in range(KC):
                                last = nc.tensor.matmul(ps[:, 5, a * E:(a + 1) * E], xt[half][:, src, k, tok],
                                                        w[:, k, 2 * E:3 * E], start=(k == 0), stop=(k == KC - 1))
                        last.then_inc(v_done, 1)
                        at_least(pe, main_read, s)
                        for k in range(KC):
                            last = nc.tensor.matmul(ps[:, 6, :], w1[:, k, q * P:(q + 1) * P], xt[half][:, 1, k, :],
                                                    start=(k == 0), stop=(k == KC - 1))
                        last.then_inc(main_done, 1)
                    if chunk(-1):
                        _, half, c = chunk(-1)
                        if q == 0:
                            pe.wait_ge(rotated, CT * (c + 1))
                        at_least(pe, turned_read, CT * c + q)
                        for t in range(CT):
                            last = nc.tensor.transpose(ps[:, 7, t * P:(t + 1) * P], qkr[half][:, t, q * P:(q + 1) * P],
                                                       ident[:, :])
                        last.then_inc(turned_done, 1)

                run(pe, step)


RING = 4
PBUFS = 4
BANKS = 3

MAX_TILES = [(7, 0), (0, 0), (7, 1), (1, 0), (6, 0), (2, 0), (6, 1), (3, 0), (5, 0), (5, 1), (4, 0), (4, 1)]
MAXIMA = [(h, t, p) for h in range(GH) for t, p in MAX_TILES]
LAST_MAX = [max(k for k, it in enumerate(MAXIMA) if it[0] == h) for h in range(GH)]
ROWS = [0, 1]
RD = GH // len(ROWS)
SCORES = ([(j, half, (h,)) for j in range(4) for h in range(GH) for half in range(2)]
          + [(j, 1, (h,)) for j in (4, 5) for h in range(GH)]
          + [(6, 1, (0, 1)), (6, 1, (2, 3)), (7, 1, (0, 1, 2, 3))])
LAST_SCORES = [max(g for g, it in enumerate(SCORES) if it[0] == j) for j in range(TT)]
VALUES = [(j, half) for j in range(TT) for half in range(j // 4, 2)]

RPU = len(SCORES) + len(ROWS)
MPU = len(MAXIMA)
FIRST_ROW_LAG = 5
MAX_AHEAD = 21
VALUES_LAG = 3
PERIOD = ("MMSSMSMVSMSMSMMSVSMSMRVMSSMMSMVMSSMSMMSSMSMSMSMVMSSSMMSMSVMS"
          "MSSMMVMSMSMSVMSSMSMMVMRSMVSMSMSMVMMSMSMSSMSMV")


def unit_steps():
    steps, n, g, row, k, m = [], 0, 0, 0, MAX_AHEAD, -VALUES_LAG
    for kind in PERIOD:
        if kind == "S":
            steps.append(("scores", n, g))
            n, g = n + 1, g + 1
        elif kind == "R":
            steps.append(("row", n, row))
            n, row = n + 1, row + 1
        elif kind == "M":
            steps.append(("max", 1 + k // MPU, k % MPU))
            k += 1
        else:
            steps.append(("values", m // len(VALUES), m % len(VALUES)))
            m += 1
    return steps


STEPS = unit_steps()
ROW_PLACES = [step[1] for step in STEPS if step[0] == "row"]


def attend(nc, identity, causal_mask, qk_d, v_d, y_d):
    with ExitStack() as ctx:
        sb = lambda name, shape, dt=FP32: ctx.enter_context(nc.sbuf_tensor("b_" + name, shape, dt))
        pb = lambda name, shape: ctx.enter_context(nc.psum_tensor("b_" + name, shape, FP32))
        sem = lambda name: ctx.enter_context(nc.semaphore("b_" + name))

        qs = [sb(f"qs{r}", [P, GH, T], BF16) for r in range(RING)]
        ks = [sb(f"ks{r}", [P, GH, T], BF16) for r in range(RING)]
        vv = [sb(f"vv{r}", [P, TT, GH * VW]) for r in range(RING)]
        yo = [sb(f"yo{r}", [P, T]) for r in range(2)]
        probs = [sb(f"probs{r}", [P, GH, T]) for r in range(PBUFS)]
        ident_f = sb("ident_f", [P, P])
        ident = sb("ident", [P, P], BF16)
        mask = sb("mask", [P, 512])
        junk = sb("junk", [P, BANKS, 512])
        pmax = sb("pmax", [P, GH, TT, 2])
        negm = sb("negm", [P, GH, TT])
        nrest = sb("nrest", [P, GH, TT])
        mparts = [sb(f"mparts{m}", [P, PARTS, RD, TT], BF16) for m in ROWS]
        mrows = [sb(f"mrows{m}", [PARTS * RD * TT, P], BF16) for m in ROWS]
        acc = pb("acc", [P, 2, 512])
        st = pb("st", [P, BANKS, 512])
        sm = pb("sm", [P, BANKS, 512])

        const_in, ident_ready, pmax_ready, ones_ready = (sem("const_in"), sem("ident_ready"), sem("pmax_ready"),
                                                         sem("ones_ready"))
        qk_in, v_in = [sem(f"qk_in{r}") for r in range(RING)], [sem(f"v_in{r}") for r in range(RING)]
        y_out = [sem(f"y_out{n}") for n in range(2)]
        st_ready, st_read = sem("st_ready"), sem("st_read")
        sm_ready, sm_read = sem("sm_ready"), sem("sm_read")
        mask_done, pv_done = sem("mask_done"), sem("pv_done")
        negm_ready, split_chain, mparts_ready = sem("negm_ready"), sem("split_chain"), sem("mparts_ready")
        y_ready, rows_in = sem("y_ready"), sem("rows_in")
        dve_passed, pool_passed = sem("dve_passed"), sem("pool_passed")

        def st_uses(unit, n):
            return len(ROWS) + RPU * unit + n

        def st_bank(n):
            return (len(ROWS) + n) % BANKS

        def over_units(engine, do_step):
            def shifted(i, r, d, step):
                do_step(i + (r + d) // RING, (r + d) % RING, step)

            def period(i, r):
                n = 0
                for kind, a, b in STEPS:
                    if kind == "scores" or kind == "row":
                        if kind == "scores" or not isinstance(i, int) or RING * i + r + 1 < UNITS:
                            do_step(i, r, (kind, n, b))
                            n += 1
                    elif not isinstance(i, int) or 0 <= RING * i + r + a < UNITS:
                        shifted(i, r, a, (kind, b))

            stream = [(0, k) for k in range(MPU)] + [(1, k) for k in range(MAX_AHEAD)]
            for n, (r, k) in enumerate(stream):
                do_step(0, r, ("max", k))
                if n - FIRST_ROW_LAG in LAST_MAX:
                    h = LAST_MAX.index(n - FIRST_ROW_LAG)
                    if h % RD == RD - 1:
                        do_step(0, -1, ("row", RPU - len(ROWS) + h // RD, h // RD))
            for r in range(RING):
                period(0, r)
            with engine.Fori(1, UNITS // RING - 1) as i:
                for r in range(RING):
                    period(i, r)
            for r in range(RING):
                period(UNITS // RING - 1, r)
            for m in range(len(VALUES) - VALUES_LAG, len(VALUES)):
                do_step(UNITS // RING - 1, RING - 1, ("values", m))

        with nc.Block() as block:

            @block.sync
            def _(sp):
                sp.dma_start(ident_f[:, :], identity).then_inc(const_in, 16)
                sp.dma_start(mask[:, :], causal_mask).then_inc(const_in, 16)

                def load(i, r):
                    unit = RING * i + r
                    for band in range(BANDS):
                        rows = slice(band * HD, (band + 1) * HD)
                        for which, part, dst in ((0, Q_PART[band], qs[r]), (1, K_PART[band], ks[r])):
                            sp.dma_start(dst[rows, :, :],
                                         qk_d[unit, which, part, :, :].rearrange("(h f) t -> f h t", f=HD)
                                         ).then_inc(qk_in[r], 16)
                    sp.dma_start(vv[r][:, :, :], v_d[unit, :, :].rearrange("(t p) n -> p t n", p=P)
                                 ).then_inc(v_in[r], 16)

                def store(i, r):
                    sp.wait_ge(y_ready, RING * i + r + 1)
                    for h in range(GH):
                        sp.dma_start(y_d[RING * i + r, h, :, :], yo[r % 2][VW * h:VW * h + YW, :]
                                     ).then_inc(y_out[r % 2], 16)

                def rows(i, r):
                    i, r = i + r // RING, r % RING
                    unit = RING * i + r
                    if isinstance(unit, int) and unit >= UNITS:
                        return
                    for m in ROWS:
                        first = isinstance(unit, int) and unit == 0
                        sp.wait_ge(st_read, m + 1 if first else st_uses(unit - 1, ROW_PLACES[m] + 1))
                        for p in range(PARTS):
                            sp.dma_start(qs[r][SROWS + p:SROWS + p + 1, RD * m:RD * (m + 1), :]
                                         .rearrange("o h (t q) -> o (h t) q", q=P),
                                         mrows[m][p * RD * TT:(p + 1) * RD * TT, :]).then_inc(rows_in, 16)

                def turn(i):
                    for r in range(RING):
                        sp.wait_ge(pv_done, TT * (RING * i + r + 1))
                        load(i + 1, r)
                        store(i, r)
                        rows(i, r + 2)

                for r in range(RING):
                    load(0, r)
                rows(0, 0)
                rows(0, 1)
                looped(sp, UNITS // RING - 1, turn)
                for r in range(RING):
                    store(UNITS // RING - 1, r)
                    rows(UNITS // RING - 1, r + 2)
                for n in range(2):
                    sp.wait_ge(y_out[n], 16 * GH * UNITS // 2)

            @block.tensor
            def _(pe):
                def do_step(i, r, step):
                    unit = RING * i + r
                    if step[0] == "max":
                        k = step[1]
                        h, t, piece = MAXIMA[k]
                        if k == 0:
                            pe.wait_ge(qk_in[r], 16 * 2 * BANDS * (i + 1))
                        if not isinstance(unit, int) or MPU * unit + k >= BANKS:
                            pe.wait_ge(sm_read, MPU * unit + k - BANKS + 1)
                        n = min((t + 1) * P - 512 * piece, 512)
                        nc.tensor.matmul(sm[:, k % BANKS, 0:n], qs[r][0:SROWS, h, t * P:(t + 1) * P],
                                         ks[r][0:SROWS, h, 512 * piece:512 * piece + n], start=True,
                                         stop=True).then_inc(sm_ready, 1)
                    elif step[0] == "values":
                        j, half = VALUES[step[1]]
                        if step[1] == 0:
                            pe.wait_ge(y_ready, unit)
                            pe.wait_ge(v_in[r], 16 * (i + 1))
                        if half == j // 4:
                            pe.wait_ge(mask_done, TT * unit + j + 1)
                        lo = max(j * P - 512 * half, 0)
                        for h in range(GH):
                            last = nc.tensor.matmul(acc[VW * h:VW * (h + 1), half, lo:512],
                                                    vv[r][:, j, VW * h:VW * (h + 1)],
                                                    probs[j % PBUFS][:, h, 512 * half + lo:512 * (half + 1)],
                                                    start=(j == 0), stop=(j == (3 if half == 0 else 7)))
                        if half:
                            last.then_inc(pv_done, 1)
                    else:
                        kind, n, m = step
                        uses = st_uses(unit, n)
                        if kind == "scores" and m == 0:
                            if isinstance(unit, int) and unit == 0:
                                pe.wait_ge(ones_ready, RING)
                            pe.wait_ge(rows_in, 16 * PARTS * len(ROWS) * (unit + 1))
                        if not isinstance(unit, int) or uses >= BANKS:
                            pe.wait_ge(st_read, uses - BANKS + 1)
                        if kind == "scores":
                            j, half, heads = SCORES[m]
                            lo = max(j * P - 512 * half, 0)
                            w = 512 - lo
                            for x, h in enumerate(heads):
                                last = nc.tensor.matmul(st[:, st_bank(n), x * w:(x + 1) * w],
                                                        ks[r][0:SROWS + PARTS, h, j * P:(j + 1) * P],
                                                        qs[r][0:SROWS + PARTS, h, 512 * half + lo:512 * (half + 1)],
                                                        start=True, stop=True)
                        else:
                            if m == 0 and isinstance(unit, int) and unit < 0:
                                pe.wait_ge(ident_ready, 1)
                            pe.wait_ge(mparts_ready, GH * (unit + 1) + RD * (m + 1))
                            last = nc.tensor.matmul(st[0:PARTS * RD * TT, st_bank(n), 0:P],
                                                    mparts[m][:, :, :, :].rearrange("p s h t -> p (s h t)"),
                                                    ident[:, :], start=True, stop=True)
                        last.then_inc(st_ready, 1)

                over_units(pe, do_step)

            @block.scalar
            def _(act):
                def do_step(i, r, step):
                    unit = RING * i + r
                    if step[0] == "scores":
                        _, n, g = step
                        j, half, heads = SCORES[g]
                        free = TT * unit + j - PBUFS + 1
                        if g == 0 or SCORES[g - 1][0] != j:
                            if not isinstance(free, int) or free > 0:
                                act.wait_ge(pv_done, free)
                        lo = max(j * P - 512 * half, 0)
                        w = 512 - lo
                        act.wait_ge(st_ready, st_uses(unit, n) + 1)
                        nc.scalar.activation(probs[j % PBUFS][:, heads[0]:heads[-1] + 1, 512 * half + lo:512 * (half + 1)],
                                             st[:, st_bank(n), 0:len(heads) * w].rearrange("p (h c) -> p h c", c=w),
                                             ACT.Exp).then_inc(st_read, 1)
                    elif step[0] == "row":
                        _, n, m = step
                        act.wait_ge(st_ready, st_uses(unit, n) + 1)
                        nc.scalar.copy(mrows[m][:, :], st[0:PARTS * RD * TT, st_bank(n), 0:P]).then_inc(st_read, 1)
                    elif step[0] == "values" and step[1] == len(VALUES) - 1:
                        act.wait_ge(pv_done, TT * (unit + 1))
                        if not isinstance(unit, int) or unit >= 2:
                            act.wait_ge(y_out[r % 2], 16 * GH * (2 * i + r // 2))
                        nc.scalar.copy(yo[r % 2][:, :], acc[:, :, :].rearrange("p b c -> p (b c)")
                                       ).then_inc(y_ready, 1)

                over_units(act, do_step)

            @block.vector
            def _(dve):
                def do_step(i, r, step):
                    if step[0] != "max":
                        return
                    unit, k = RING * i + r, step[1]
                    h, t, piece = MAXIMA[k]
                    bank = k % BANKS
                    n = min((t + 1) * P - 512 * piece, 512)
                    if piece == t // 4:
                        apart(dve, sm_ready, MPU * unit + k + 1, dve_passed)
                        nc.vector.tensor_tensor_reduce(
                            out=junk[:, bank, 0:n], in0=sm[:, bank, 0:n], in1=mask[:, 512 - n:512], scale=1.0,
                            scalar=-BIG, op0=ALU.add, op1=ALU.max,
                            accum_out=pmax[:, h, t, 1:2]).then_inc(sm_read, 1)
                    else:
                        dve.wait_ge(sm_ready, MPU * unit + k + 1)
                        nc.vector.tensor_reduce(pmax[:, h, t, 0:1], sm[:, bank, 0:n], AX.X,
                                                ALU.max).then_inc(sm_read, 1)
                    if k == LAST_MAX[h]:
                        dve.wait_ge(sm_read, MPU * unit + k + 1)
                        nc.vector.tensor_reduce(negm[:, h, :], pmax[:, h, :, :], AX.X, ALU.max,
                                                negate=True).then_inc(negm_ready, 1)

                nc.vector.memset(pmax[:, :, :, :], -BIG).then_inc(pmax_ready, 1)
                dve.wait_ge(const_in, 32)
                nc.vector.tensor_copy(ident[:, :], ident_f[:, :]).then_inc(ident_ready, 1)
                dve.wait_ge(pmax_ready, 1)
                over_units(dve, do_step)

            @block.gpsimd
            def _(pool):
                def do_step(i, r, step):
                    unit = RING * i + r
                    if step[0] == "scores" and step[2] in LAST_SCORES:
                        j = LAST_SCORES.index(step[2])
                        apart(pool, st_read, st_uses(unit, step[1]) + 1, pool_passed)
                        diag = probs[j % PBUFS][:, :, j * P:(j + 1) * P]
                        nc.gpsimd.affine_select(out=diag, in_=diag, compare_op=ALU.is_ge, fill=0.0, base=0,
                                                pattern=[[0, GH], [1, P]],
                                                channel_multiplier=-1).then_inc(mask_done, 1)
                    elif step[0] == "max" and step[1] in LAST_MAX:
                        h = LAST_MAX.index(step[1])
                        apart(pool, negm_ready, GH * unit + h + 1, pool_passed)
                        chain = Chain(pool, split_chain, 3 * (GH * unit + h))
                        part = lambda p: mparts[h // RD][:, p, h % RD, :]
                        chain(nc.gpsimd.tensor_copy(part(0), negm[:, h, :]))
                        chain(nc.gpsimd.tensor_tensor(out=nrest[:, h, :], in0=negm[:, h, :], in1=part(0),
                                                      op=ALU.subtract))
                        pool.sem_inc(pool_passed, 1)
                        chain(nc.gpsimd.tensor_copy(part(1), nrest[:, h, :]))
                        nc.gpsimd.tensor_tensor(out=part(2), in0=nrest[:, h, :], in1=part(1),
                                                op=ALU.subtract).then_inc(mparts_ready, 1)

                for r in range(RING):
                    nc.gpsimd.memset(ks[r][SROWS:SROWS + PARTS, :, :], 1.0).then_inc(ones_ready, 1)
                pool.wait_ge(ones_ready, RING)
                over_units(pool, do_step)


class HeadsOut:

    def __init__(self, nc, ctx, tag, ps, attention, w_out, ident, y_d):
        sb = lambda name, shape, dt=FP32: ctx.enter_context(nc.sbuf_tensor(f"{tag}_{name}", shape, dt))
        sem = lambda name: ctx.enter_context(nc.semaphore(f"{tag}_{name}"))
        self.nc, self.ps, self.attention, self.w_out, self.ident, self.y_d = nc, ps, attention, w_out, ident, y_d
        self.yt = [sb(f"yt{n}", [P, GROUPS, CH]) for n in range(2)]
        self.yn = [sb(f"yn{n}", [P, E]) for n in range(2)]
        self.ynt = [sb(f"ynt{n}", [P, KC, P]) for n in range(2)]
        self.rden = [sb(f"rden{n}", [P, HEADS]) for n in range(2)]
        self.y_in = [sem(f"y_in{n}") for n in range(2)]
        self.cleared = sem("cleared")
        self.flipped, self.rden_ready, self.yn_ready = sem("flipped"), sem("rden_ready"), sem("yn_ready")
        self.back, self.ynt_ready, self.projected, self.taken = sem("back"), sem("ynt_ready"), sem("projected"), sem("taken")

    def clear(self):
        for n in range(2):
            self.nc.vector.memset(self.yt[n][:, :, :], 0.0).then_inc(self.cleared, 1)

    def load(self, queue, b, half):
        unit = b * GROUPS + self.attention * UB
        for h in range(GH):
            queue.dma_start(self.yt[half][VW * h:VW * h + YW, :, :],
                            self.y_d[bass.ds(unit, GROUPS), h, :, half * CH:(half + 1) * CH]
                            .rearrange("g r t -> r g t")).then_inc(self.y_in[half], 16)

    def tensor(self, pe, chunk, q):
        nc, ps = self.nc, self.ps
        if chunk(0):
            b, half, c = chunk(0)
            s = CT * c + q
            if q == 0:
                pe.wait_ge(self.y_in[half], 16 * GH * (b + 1))
            at_least(pe, self.yn_ready, s - 1)
            for g in range(GROUPS):
                last = nc.tensor.transpose(ps[:, q % 2, g * P:(g + 1) * P],
                                           self.yt[half][:, g, q * P:(q + 1) * P], self.ident[:, :])
            last.then_inc(self.flipped, 1)
        at, t = ago(chunk, q, 1)
        if at:
            s = CT * at[2] + t
            pe.wait_ge(self.yn_ready, s + 1)
            at_least(pe, self.ynt_ready, s - 1)
            for k in range(KC):
                last = nc.tensor.transpose(ps[:, 2 + t % 2, k * P:(k + 1) * P],
                                           self.yn[t % 2][:, k * P:(k + 1) * P], self.ident[:, :])
            last.then_inc(self.back, 1)
        at, t = ago(chunk, q, 2)
        if at:
            s = CT * at[2] + t
            pe.wait_ge(self.ynt_ready, s + 1)
            at_least(pe, self.taken, s - 1)
            for k in range(KC):
                last = nc.tensor.matmul(ps[:, 4 + t % 2, 0:E], self.ynt[t % 2][:, k, :], self.w_out[:, k, :],
                                        start=(k == 0), stop=(k == KC - 1))
            last.then_inc(self.projected, 1)

    def vector(self, dve, chunk, q):
        if not chunk(0):
            return
        nc, s = self.nc, CT * chunk(0)[2] + q
        dve.wait_ge(self.flipped, s + 1)
        y = self.ps[:, q % 2, :].rearrange("p (h v) -> p h v", v=VW)
        nc.vector.reciprocal(self.rden[q % 2][:, :], y[:, :, HD]).then_inc(self.rden_ready, 1)
        dve.wait_ge(self.rden_ready, s + 1)
        at_least(dve, self.back, s - 1)
        nc.vector.tensor_tensor(self.yn[q % 2][:, :].rearrange("p (h d) -> p h d", d=HD), y[:, :, 0:HD],
                                self.rden[q % 2][:, :].rearrange("p (h o) -> p h o", o=1)
                                .broadcast_to((P, HEADS, HD)), ALU.mult).then_inc(self.yn_ready, 1)

    def scalar(self, act, chunk, q):
        at, t = ago(chunk, q, 1)
        if at:
            s = CT * at[2] + t
            act.wait_ge(self.back, s + 1)
            at_least(act, self.projected, s - 1)
            self.nc.scalar.copy(self.ynt[t % 2][:, :, :],
                                self.ps[:, 2 + t % 2, 0:KC * P].rearrange("p (k t) -> p k t", k=KC)
                                ).then_inc(self.ynt_ready, 1)


def over_out_quarters(engine, step):
    over_quarters(engine, step, 0, B - 1, B + 1)


def block_mid(nc, w_o, w_router, g2, identity, xn_d, y_d, z_d, h_d, logits):
    with ExitStack() as ctx:
        sb = lambda name, shape, dt=FP32: ctx.enter_context(nc.sbuf_tensor("c_" + name, shape, dt))
        sem = lambda name: ctx.enter_context(nc.semaphore("c_" + name))
        pair = lambda name: [sem(f"{name}{n}") for n in range(2)]
        wo = sb("wo", [P, KC, E])
        wr = sb("wr", [P, KC, EXPERTS])
        g2c = sb("g2c", [P, KC])
        ident = sb("ident", [P, P])
        xn = [sb(f"xn{n}", [P, CT, E]) for n in range(2)]
        z = [sb(f"z{n}", [P, CT, E]) for n in range(2)]
        h = [sb(f"h{n}", [P, CT, E]) for n in range(2)]
        ht = sb("ht", [P, KC, CH])
        junk = sb("junk", [P, CT, E])
        ssq = sb("ssq", [P, CT])
        ms = sb("ms", [P, CT])
        rrms = sb("rrms", [P, CT])
        neghalf = sb("neghalf", [P, CT])
        zeros = sb("zeros", [P, SLOTB, E])
        ps = ctx.enter_context(nc.psum_tensor("c_ps", [P, 8, 512], FP32))
        w_in, consts = sem("w_in"), sem("consts")
        xn_in, z_out, h_out = pair("xn_in"), pair("z_out"), pair("h_out")
        ms_ready, rsq, h_ready, h_flipped, ht_ready = sem("ms_ready"), sem("rsq"), sem("h_ready"), sem("h_flipped"), sem("ht_ready")
        routed, logits_ready, ssq_ready, dump_out = sem("routed"), sem("logits_ready"), sem("ssq_ready"), sem("dump_out")
        heads = HeadsOut(nc, ctx, "c_out", ps, 0, wo, ident, y_d)

        def rows(b, half):
            return bass.ds(b * T + half * CH, CH)

        with nc.Block() as block:

            @block.sync
            def _(sp):
                for dst, src in ((wo[:, :, :], w_o.rearrange("(k p) n -> p k n", p=P)),
                                 (wr[:, :, :], w_router.rearrange("(k p) n -> p k n", p=P)),
                                 (g2c[:, :], g2), (ident[:, :], identity)):
                    sp.dma_start(dst, src).then_inc(w_in, 16)

                def load_xn(b, half):
                    sp.dma_start(xn[half][:, :, :], xn_d[rows(b, half), :].rearrange("(t p) e -> p t e", p=P)
                                 ).then_inc(xn_in[half], 16)

                def step(chunk, q):
                    if q == 0 and chunk(-1) and chunk(1):
                        sp.wait_ge(heads.flipped, CT * chunk(0)[2])
                        heads.load(sp, *chunk(1)[:2])
                    if q == 0 and chunk(-2):
                        b, half, c = chunk(-2)
                        sp.wait_ge(h_ready, c + 1)
                        sp.dma_start(h_d[rows(b, half), 0:E].rearrange("(t p) e -> p t e", p=P), h[half][:, :, :]
                                     ).then_inc(h_out[half], 16)
                    if q == 2 and chunk(-1):
                        b, half, c = chunk(-1)
                        sp.wait_ge(heads.taken, CT * (c + 1))
                        if chunk(1):
                            load_xn(*chunk(1)[:2])
                        sp.dma_start(z_d[rows(b, half), :].rearrange("(t p) e -> p t e", p=P), z[half][:, :, :]
                                     ).then_inc(z_out[half], 16)

                for half in range(2):
                    sp.wait_ge(heads.cleared, half + 1)
                    heads.load(sp, 0, half)
                    load_xn(0, half)
                over_out_quarters(sp, step)
                for half in range(2):
                    sp.wait_ge(z_out[half], 16 * B)
                    sp.wait_ge(h_out[half], 16 * B)

            @block.gpsimd
            def _(pool):
                nc.gpsimd.memset(neghalf[:, :], -0.5).then_inc(consts, 1)
                nc.gpsimd.memset(zeros[:, :, :], 0.0).then_inc(consts, 1)
                pool.wait_ge(consts, 2)
                pool.dma_start(z_d[TOK:TOK + SLOTB * P, :].rearrange("(s p) e -> p s e", p=P), zeros[:, :, :]
                               ).then_inc(dump_out, 16)

                def step(chunk, q):
                    if q == 2 and chunk(-1):
                        pool.wait_ge(ms_ready, chunk(-1)[2] + 1)
                        nc.gpsimd.tensor_tensor(out=rrms[:, :], in0=ms[:, :], in1=neghalf[:, :],
                                                op=ALU.pow).then_inc(rsq, 1)

                over_out_quarters(pool, step)
                pool.wait_ge(dump_out, 16)

            @block.tensor
            def _(pe):
                pe.wait_ge(w_in, 16 * 4)

                def step(chunk, q):
                    heads.tensor(pe, chunk, q)
                    if q == 0 and chunk(-2):
                        _, half, c = chunk(-2)
                        pe.wait_ge(h_ready, c + 1)
                        at_least(pe, logits_ready, c)
                        for k in range(KC):
                            for t in range(CT):
                                last = nc.tensor.transpose(ps[:, 6 + k, t * P:(t + 1) * P],
                                                           h[half][:, t, k * P:(k + 1) * P], ident[:, :])
                        last.then_inc(h_flipped, 1)
                    if q == 2 and chunk(-2):
                        pe.wait_ge(ht_ready, 2 * (chunk(-2)[2] + 1))
                        for t in range(CT):
                            for k in range(KC):
                                last = nc.tensor.matmul(ps[:, 6, t * EXPERTS:(t + 1) * EXPERTS],
                                                        ht[:, k, t * P:(t + 1) * P], wr[:, k, :],
                                                        start=(k == 0), stop=(k == KC - 1))
                        last.then_inc(routed, 1)

                over_out_quarters(pe, step)

            @block.scalar
            def _(act):
                act.wait_ge(w_in, 16 * 4)

                def step(chunk, q):
                    heads.scalar(act, chunk, q)
                    if q == 1 and chunk(-2):
                        c = chunk(-2)[2]
                        act.wait_ge(h_flipped, c + 1)
                        for k in range(KC):
                            nc.scalar.activation(ht[:, k, :], ps[:, 6 + k, :], ACT.Copy,
                                                 scale=g2c[:, k:k + 1]).then_inc(ht_ready, 1)

                over_out_quarters(act, step)

            @block.vector
            def _(dve):
                heads.clear()
                def step(chunk, q):
                    heads.vector(dve, chunk, q)
                    at, t = ago(chunk, q, 2)
                    if at:
                        b, half, c = at
                        if t == 0:
                            dve.wait_ge(xn_in[half], 16 * b + 16)
                            at_least(dve, z_out[half], 16 * b)
                        dve.wait_ge(heads.projected, CT * c + t + 1)
                        nc.vector.tensor_tensor(z[half][:, t, :], ps[:, 4 + t % 2, 0:E], xn[half][:, t, :],
                                                ALU.add).then_inc(heads.taken, 1)
                    if q == 2 and chunk(-1):
                        _, half, c = chunk(-1)
                        dve.wait_ge(heads.taken, CT * (c + 1))
                        for t in range(CT):
                            last = nc.vector.tensor_tensor_reduce(
                                out=junk[:, t, :], in0=z[half][:, t, :], in1=z[half][:, t, :], scale=1.0, scalar=0.0,
                                op0=ALU.mult, op1=ALU.add, accum_out=ssq[:, t:t + 1])
                        last.then_inc(ssq_ready, 1)
                        dve.wait_ge(ssq_ready, c + 1)
                        nc.vector.tensor_scalar(ms[:, :], ssq[:, :], 1.0 / E, RMS_EPS, ALU.mult,
                                                ALU.add).then_inc(ms_ready, 1)
                    if q == 3 and chunk(-1):
                        b, half, c = chunk(-1)
                        at_least(dve, h_out[half], 16 * b)
                        at_least(dve, h_flipped, c - 1)
                        dve.wait_ge(rsq, c + 1)
                        for t in range(CT):
                            last = nc.vector.tensor_scalar(h[half][:, t, :], z[half][:, t, :], rrms[:, t:t + 1], None,
                                                           ALU.mult)
                        last.then_inc(h_ready, 1)
                    if q == 3 and chunk(-2):
                        b, half, c = chunk(-2)
                        dve.wait_ge(routed, c + 1)
                        tiles = slice(b * TT + half * CT, b * TT + half * CT + CT) if isinstance(b, int) \
                            else bass.ds(b * TT + half * CT, CT)
                        nc.vector.tensor_copy(logits[:, :, tiles],
                                              ps[:, 6, 0:CT * EXPERTS].rearrange("p (t e) -> p e t", e=EXPERTS)
                                              ).then_inc(logits_ready, 1)

                over_out_quarters(dve, step)


def route(nc, ones_in, upper_in, iota_in, token_parts, slot_rows, h_d, logits, occupied, gather_row, scatter_row):
    N = EXPERTS * TILES
    OH = 4
    BITS, DIGITS = 30, 3
    VALS = 3
    with ExitStack() as ctx:
        sb = lambda name, shape, dt=FP32: ctx.enter_context(nc.sbuf_tensor("d_" + name, shape, dt))
        sem = lambda name: ctx.enter_context(nc.semaphore("d_" + name))
        ones = sb("ones", [P, P])
        upper = sb("upper", [P, P])
        iota_f = sb("iota_f", [P, P])
        iota = sb("iota", [P, P], BF16)
        tparts = sb("tparts", [P, TILES, VALS])
        slots = sb("slots", [P, SLOTB])
        zero = sb("zero", [P, P], BF16)
        probs = sb("probs", [P, EXPERTS, TILES])
        gate = sb("gate", [P, EXPERTS, TILES])
        gate_t = sb("gate_t", [P, TILES, EXPERTS])
        rank = sb("rank", [P, EXPERTS, TILES])
        tmp = sb("tmp", [P, EXPERTS, TILES])
        tmp2 = sb("tmp2", [P, EXPERTS, TILES])
        tied = sb("tied", [P, EXPERTS, TILES])
        chosen = sb("chosen", [P, EXPERTS, TILES])
        total = sb("total", [P, EXPERTS, TILES])
        onesrow = sb("onesrow", [P, TILES])
        top = sb("top", [P, TILES])
        den = sb("den", [P, TILES])
        thr = sb("thr", [P, EXPERTS], I32)
        digit = sb("digit", [P, DIGITS, EXPERTS], I32)
        cand = sb("cand", [P, DIGITS, EXPERTS], I32)
        keep = sb("keep", [P, DIGITS, EXPERTS], I32)
        above = sb("above", [P, DIGITS, EXPERTS, TILES])
        hits = sb("hits", [P, DIGITS, EXPERTS])
        part = sb("part", [P, EXPERTS])
        need = sb("need", [P, EXPERTS])
        slot = sb("slot", [P, EXPERTS, TILES])
        blk = sb("blk", [P, EXPERTS, TILES])
        slot_t = sb("slot_t", [P, TILES, EXPERTS], BF16)
        rhs = sb("rhs", [P, TILES, EXPERTS, SLOTB, VALS], BF16)
        onehot = [sb(f"onehot{n}", [P, EXPERTS, P], BF16) for n in range(OH)]
        found = sb("found", [P, EXPERTS, SLOTB, VALS])
        row_f = sb("row_f", [P, EXPERTS, SLOTB])
        row_g = sb("row_g", [P, EXPERTS, SLOTB])
        ps = ctx.enter_context(nc.psum_tensor("d_ps", [P, 4, 512], FP32))
        const_in, steps, exp_ready, gates_out = sem("const_in"), sem("steps"), sem("exp_ready"), sem("gates_out")
        search_steps, counted, cmp_ready = sem("search_steps"), sem("counted"), sem("cmp_ready")
        prefixed, prefix_ask = sem("prefixed"), sem("prefix_ask")
        oh_ready, oh_used, compacted, rhs_ready, gate_ready = sem("oh_ready"), sem("oh_used"), sem("compacted"), sem("rhs_ready"), sem("gate_ready")
        max_sub = sem("max_sub")
        passed = sem("passed")
        SEARCH = 4 + DIGITS

        def spread(ap, n):
            return ap.rearrange("p (e o) -> p e o", o=1).broadcast_to((P, EXPERTS, n))

        def over_experts(ap):
            return ap.rearrange("p (o t) -> p o t", o=1).broadcast_to((P, EXPERTS, TILES))

        with nc.Block() as block:

            @block.sync
            def _(sp):
                for dst, src in ((ones[:, :], ones_in), (upper[:, :], upper_in), (iota_f[:, :], iota_in),
                                 (tparts[:, :, :], token_parts), (slots[:, :], slot_rows)):
                    sp.dma_start(dst, src).then_inc(const_in, 16)
                sp.wait_ge(gate_ready, 1)
                sp.dma_start(h_d[:, E:E + EXPERTS].rearrange("(t p) e -> p t e", p=P), gate_t[:, :, :]
                             ).then_inc(gates_out, 16)
                sp.wait_ge(gates_out, 16)

            @block.scalar
            def _(act):
                act.wait_ge(max_sub, 1)
                nc.scalar.activation(probs[:, :, :], tmp[:, :, :], ACT.Exp).then_inc(exp_ready, 1)

            @block.tensor
            def _(pe):
                pe.wait_ge(const_in, 16 * 5)
                with pe.Fori(0, BITS // 2) as i:
                    pe.wait_ge(cmp_ready, i + 1)
                    nc.tensor.matmul(ps[:, 0, 0:DIGITS * EXPERTS], ones[:, :],
                                     hits[:, :, :].rearrange("p k e -> p (k e)"), start=True, stop=True
                                     ).then_inc(counted, 1)
                for n, src in enumerate((tmp, tied, chosen)):
                    pe.wait_ge(prefix_ask, n + 1)
                    last = nc.tensor.matmul(ps[:, 1, :], ones[:, :], src[:, :, :].rearrange("p e t -> p (e t)"),
                                            start=True, stop=True)
                    if n:
                        last = nc.tensor.matmul(ps[:, 2, :], upper[:, :], src[:, :, :].rearrange("p e t -> p (e t)"),
                                                start=True, stop=True)
                    last.then_inc(prefixed, 1)
                pe.wait_ge(rhs_ready, 1)
                cols = EXPERTS * SLOTB * VALS
                all_rhs = rhs[:, 0, :, :, :].rearrange("p e a v -> p (e a v)")
                nc.tensor.matmul(ps[:, 3, 0:cols], zero[:, :], all_rhs, start=True, stop=False, skip_group_check=True)
                def turn(i):
                    for n in range(OH):
                        pe.wait_ge(oh_ready, OH * i + n + 1)
                        for e in range(EXPERTS):
                            w = SLOTB * VALS
                            last = nc.tensor.matmul(
                                ps[:, 3, e * w:(e + 1) * w], onehot[n][:, e, :],
                                rhs[:, bass.ds(OH * i + n, 1), e, :, :].rearrange("p t a v -> p (t a v)"),
                                start=False, stop=False, skip_group_check=True)
                        last.then_inc(oh_used, 1)

                looped(pe, TILES // OH, turn)
                nc.tensor.matmul(ps[:, 3, 0:cols], zero[:, :], all_rhs, start=False, stop=True,
                                 skip_group_check=True).then_inc(compacted, 1)

            @block.vector
            def _(dve):
                chain = Chain(dve, steps, 0)
                v = nc.vector
                full = lambda t: t[:, :, :]
                dve.wait_ge(const_in, 16 * 5)
                v.tensor_copy(iota[:, :], iota_f[:, :])
                chain(v.tensor_reduce(top[:, :], logits[:, :, :].rearrange("p e t -> p t e"), AX.X, ALU.max))
                v.tensor_tensor(full(tmp), full(logits), over_experts(top[:, :]), ALU.subtract).then_inc(max_sub, 1)
                dve.wait_ge(exp_ready, 1)
                chain(v.tensor_reduce(den[:, :], probs[:, :, :].rearrange("p e t -> p t e"), AX.X, ALU.add))
                chain(v.reciprocal(den[:, :], den[:, :]))
                chain(v.tensor_tensor(full(probs), full(probs), over_experts(den[:, :]), ALU.mult))
                chain(v.memset(full(rank), 0.0))
                for d in range(1, EXPERTS):
                    lo, hi = probs[:, 0:EXPERTS - d, :], probs[:, d:EXPERTS, :]
                    n = EXPERTS - d
                    v.tensor_tensor(tmp[:, 0:n, :], hi, lo, ALU.is_gt)
                    chain(v.tensor_tensor(tmp2[:, 0:n, :], hi, lo, ALU.is_le))
                    chain(v.tensor_tensor(rank[:, 0:n, :], rank[:, 0:n, :], tmp[:, 0:n, :], ALU.add))
                    chain(v.tensor_tensor(rank[:, d:EXPERTS, :], rank[:, d:EXPERTS, :], tmp2[:, 0:n, :], ALU.add))
                chain(v.tensor_scalar(full(tmp), full(rank), 1.5, None, ALU.is_lt))
                chain(v.tensor_scalar(full(tmp2), full(tmp), 1.0, None, ALU.subtract))
                chain(v.tensor_tensor(full(gate), full(probs), full(tmp), ALU.mult))
                chain(v.tensor_tensor(full(gate), full(gate), full(tmp2), ALU.add))
                v.tensor_copy(gate_t[:, :, :], gate[:, :, :].rearrange("p e t -> p t e")).then_inc(gate_ready, 1)
                v.memset(thr[:, :], 0)
                v.memset(part[:, :], 0.0)
                v.memset(onesrow[:, :], 1.0)
                v.memset(zero[:, :], 0.0)
                for k in range(DIGITS):
                    last = v.memset(digit[:, k, :], (k + 1) << (BITS - 2))
                chain(last)
                with dve.Fori(0, BITS // 2) as i:
                    search = Chain(dve, search_steps, SEARCH * i)
                    search(v.tensor_tensor(cand[:, :, :], digit[:, :, :],
                                           thr[:, :].rearrange("p (o e) -> p o e", o=1)
                                           .broadcast_to((P, DIGITS, EXPERTS)), ALU.bitwise_or))
                    search(v.tensor_tensor(above[:, :, :, :],
                                           gate[:, :, :].rearrange("p (o e) t -> p o e t", o=1)
                                           .broadcast_to((P, DIGITS, EXPERTS, TILES)),
                                           cand[:, :, :].bitcast(FP32).rearrange("p k (e o) -> p k e o", o=1)
                                           .broadcast_to((P, DIGITS, EXPERTS, TILES)), ALU.is_ge))
                    v.tensor_reduce(hits[:, :, :], above[:, :, :, :], AX.X, ALU.add).then_inc(cmp_ready, 1)
                    search(v.tensor_single_scalar(digit[:, :, :], digit[:, :, :], 2, ALU.logical_shift_right))
                    dve.wait_ge(counted, i + 1)
                    search(v.tensor_scalar(keep[:, :, :].rearrange("p k e -> p (k e)"), ps[:, 0, 0:DIGITS * EXPERTS],
                                           CAP - 0.5, None, ALU.is_ge))
                    for k in range(DIGITS):
                        dve.sem_inc(passed, 1)
                        search(v.copy_predicated(thr[:, :], keep[:, k, :], cand[:, k, :]))
                    assert search.n == SEARCH
                limit = spread(thr[:, :].bitcast(FP32), TILES)
                v.tensor_tensor(full(tmp), full(gate), limit, ALU.is_gt)
                chain(v.tensor_tensor(full(tied), full(gate), limit, ALU.is_equal))

                def running(n, out):
                    dve.wait_ge(prefixed, n + 1)
                    chain(v.tensor_copy(total[:, :, :].rearrange("p e t -> p (e t)"), ps[:, 1, :]))
                    for e in range(EXPERTS):
                        last = v.tensor_tensor_scan(out[:, e, :], onesrow[:, :], total[:, e, :], 0.0, ALU.mult, ALU.add)
                    chain(last)
                    chain(v.tensor_tensor(full(out), full(out), full(total), ALU.subtract))
                    chain(v.tensor_tensor(full(out).rearrange("p e t -> p (e t)"), ps[:, 2, :],
                                          full(out).rearrange("p e t -> p (e t)"), ALU.add))

                v.tensor_copy(part[:, :], part[:, :]).then_inc(prefix_ask, 1)
                dve.wait_ge(prefixed, 1)
                chain(v.tensor_reduce(need[:, :], ps[:, 1, :].rearrange("p (e t) -> p e t", t=TILES), AX.X, ALU.add))
                chain(v.tensor_scalar(need[:, :], need[:, :], -1.0, CAP + 0.5, ALU.mult, ALU.add))
                v.tensor_copy(part[:, :], part[:, :]).then_inc(prefix_ask, 1)
                running(1, slot)
                chain(v.tensor_tensor(full(slot), full(slot), spread(need[:, :], TILES), ALU.is_lt))
                chain(v.tensor_tensor(full(slot), full(slot), full(tied), ALU.mult))
                v.tensor_tensor(full(chosen), full(slot), full(tmp), ALU.add).then_inc(prefix_ask, 1)
                running(2, slot)
                chain(v.tensor_tensor(full(slot), full(slot), full(chosen), ALU.mult))
                chain(v.tensor_scalar(full(slot), full(slot), 1.0, None, ALU.subtract))
                chain(v.tensor_scalar(full(blk), full(slot), P - 0.5, None, ALU.is_ge))
                for a in range(2, SLOTB):
                    chain(v.tensor_scalar(full(tmp), full(slot), a * P - 0.5, None, ALU.is_ge))
                    chain(v.tensor_tensor(full(blk), full(blk), full(tmp), ALU.add))
                chain(v.tensor_scalar(full(tmp), full(blk), -float(P), None, ALU.mult))
                chain(v.tensor_tensor(slot_t[:, :, :].rearrange("p t e -> p e t"), full(slot), full(tmp), ALU.add))
                for a in range(SLOTB):
                    chain(v.tensor_scalar(full(tmp), full(blk), float(a), None, ALU.is_equal))
                    for n in range(VALS):
                        last = v.tensor_tensor(rhs[:, :, :, a, n].rearrange("p t e -> p e t"), full(tmp),
                                               over_experts(tparts[:, :, n]), ALU.mult)
                    chain(last)
                v.tensor_copy(part[:, :], part[:, :]).then_inc(rhs_ready, 1)
                def turn(i):
                    for n in range(OH):
                        at_least(dve, oh_used, OH * (i - 1) + n + 1)
                        v.tensor_tensor(onehot[n][:, :, :],
                                        iota[:, :].rearrange("p (o s) -> p o s", o=1).broadcast_to((P, EXPERTS, P)),
                                        slot_t[:, bass.ds(OH * i + n, 1), :].rearrange("p t e -> p (t e)")
                                        .rearrange("p (e o) -> p e o", o=1).broadcast_to((P, EXPERTS, P)),
                                        ALU.is_equal).then_inc(oh_ready, 1)

                looped(dve, TILES // OH, turn)
                dve.wait_ge(compacted, 1)
                cols = EXPERTS * SLOTB * VALS
                chain(v.tensor_copy(found[:, :, :, :].rearrange("p e a v -> p (e a v)"), ps[:, 3, 0:cols]))
                chain(v.tensor_scalar(full(row_f), found[:, :, :, 1], float(P), None, ALU.mult))
                chain(v.tensor_tensor(full(row_f), full(row_f), found[:, :, :, 2], ALU.add))
                v.tensor_copy(full(gather_row), full(row_f))
                chain(v.tensor_copy(full(occupied), found[:, :, :, 0]))
                chain(v.tensor_scalar(full(row_g), full(occupied), -1.0, 1.0, ALU.mult, ALU.add))
                chain(v.tensor_tensor(full(row_g), full(row_g),
                                      slots[:, :].rearrange("p (o a) -> p o a", o=1)
                                      .broadcast_to((P, EXPERTS, SLOTB)), ALU.mult))
                chain(v.tensor_tensor(full(row_g), full(row_g), full(row_f), ALU.add))
                chain(v.tensor_copy(full(scatter_row), full(row_g)))


def experts(nc, w1_in, w2_in, g2, identity, h_d, z_d, occupied, gather_row, scatter_row):
    FC = FFN // P
    HW = E + EXPERTS
    size = [min(P, CAP - s * P) for s in range(SLOTB)]
    with ExitStack() as ctx:
        sb = lambda name, shape, dt=FP32: ctx.enter_context(nc.sbuf_tensor("e_" + name, shape, dt))
        sem = lambda name: ctx.enter_context(nc.semaphore("e_" + name))
        pair = lambda name: [sem(f"{name}{n}") for n in range(2)]
        ident = sb("ident", [P, P])
        g2c = sb("g2c", [P, KC])
        w1 = [sb(f"w1{n}", [P, KC, FFN]) for n in range(2)]
        w2 = [sb(f"w2{n}", [P, FC, E]) for n in range(2)]
        xe = [sb(f"xe{n}", [P, SLOTB, HW]) for n in range(2)]
        xet = sb("xet", [P, KC, CAP])
        ht = sb("ht", [P, FC, CAP])
        gates = [sb(f"gates{n}", [P, SLOTB]) for n in range(2)]
        ye = [sb(f"ye{n}", [P, SLOTB, E]) for n in range(2)]
        ps = ctx.enter_context(nc.psum_tensor("e_ps", [P, 8, 512], FP32))
        const_in, w_in, xe_in, added = sem("const_in"), pair("w_in"), pair("xe_in"), sem("added")
        flipped, xet_ready, up, ht_ready = sem("flipped"), sem("xet_ready"), sem("up"), sem("ht_ready")
        down, gates_ready, ye_ready = sem("down"), sem("gates_ready"), sem("ye_ready")

        with nc.Block() as block:

            @block.sync
            def _(sp):
                sp.dma_start(ident[:, :], identity).then_inc(const_in, 16)
                sp.dma_start(g2c[:, :], g2).then_inc(const_in, 16)
                def turn(i):
                    for n in range(2):
                        at_least(sp, down, SLOTB * (2 * i + n - 1))
                        sp.dma_start(w1[n][:, :, :], w1_in[2 * i + n, :, :].rearrange("(k p) f -> p k f", p=P)
                                     ).then_inc(w_in[n], 16)
                        sp.dma_start(w2[n][:, :, :], w2_in[2 * i + n, :, :].rearrange("(k p) f -> p k f", p=P)
                                     ).then_inc(w_in[n], 16)

                looped(sp, EXPERTS // 2, turn)

            @block.gpsimd
            def _(pool):
                def gather(e):
                    if e >= 2:
                        pool.wait_ge(flipped, e - 1)
                        pool.wait_ge(gates_ready, e - 1)
                    for s in range(SLOTB):
                        pool.indirect_dma_start(
                            out=xe[e % 2][0:size[s], s, :], out_offset=None, in_=h_d[:, :],
                            in_offset=bass.IndirectOffsetOnAxis(ap=gather_row[0:size[s], e, s:s + 1], axis=0),
                        ).then_inc(xe_in[e % 2], 16)

                gather(0)
                gather(1)
                for e in range(EXPERTS):
                    if e + 2 < EXPERTS:
                        gather(e + 2)
                    pool.wait_ge(ye_ready, SLOTB * (e + 1))
                    if e:
                        pool.wait_ge(added, 16 * SLOTB * e)
                    for s in range(SLOTB):
                        pool.indirect_dma_start(
                            out=z_d[:, :],
                            out_offset=bass.IndirectOffsetOnAxis(ap=scatter_row[0:size[s], e, s:s + 1], axis=0),
                            in_=ye[e % 2][0:size[s], s, :], in_offset=None, compute_op=ALU.add,
                        ).then_inc(added, 16)
                pool.wait_ge(added, 16 * SLOTB * EXPERTS)

            @block.tensor
            def _(pe):
                pe.wait_ge(const_in, 32)

                def flip(i, n):
                    pe.wait_ge(xe_in[n], 16 * SLOTB * (i + 1))
                    for k in range(KC):
                        for s in range(SLOTB):
                            last = nc.tensor.transpose(ps[:, k, s * P:s * P + size[s]],
                                                       xe[n][0:size[s], s, k * P:(k + 1) * P],
                                                       ident[0:size[s], 0:size[s]])
                    last.then_inc(flipped, 1)

                def turn(i, last_turn=False):
                    for n in range(2):
                        e = 2 * i + n
                        pe.wait_ge(w_in[n], 32 * (i + 1))
                        pe.wait_ge(xet_ready, KC * (e + 1))
                        for f in range(FC):
                            pe.wait_ge(ht_ready, FC * e + max(f - 1, 0))
                            for k in range(KC):
                                last = nc.tensor.matmul(ps[:, 2 + f % 2, 0:CAP], w1[n][:, k, f * P:(f + 1) * P],
                                                        xet[:, k, :], start=(k == 0), stop=(k == KC - 1))
                            last.then_inc(up, 1)
                        if not (last_turn and n):
                            flip(i + n, 1 - n)
                        pe.wait_ge(ht_ready, FC * (e + 1))
                        pe.wait_ge(ye_ready, SLOTB * e)
                        for s in range(SLOTB):
                            for f in range(FC):
                                last = nc.tensor.matmul(ps[0:size[s], 4 + s, 0:E], ht[:, f, s * P:s * P + size[s]],
                                                        w2[n][:, f, :], start=(f == 0), stop=(f == FC - 1))
                            last.then_inc(down, 1)

                flip(0, 0)
                looped(pe, EXPERTS // 2 - 1, turn)
                turn(EXPERTS // 2 - 1, last_turn=True)

            @block.scalar
            def _(act):
                act.wait_ge(const_in, 32)
                def turn(i):
                    for n in range(2):
                        e = 2 * i + n
                        act.wait_ge(flipped, e + 1)
                        act.wait_ge(up, FC * e)
                        for k in range(KC):
                            nc.scalar.activation(xet[:, k, :], ps[:, k, 0:CAP], ACT.Copy,
                                                 scale=g2c[:, k:k + 1]).then_inc(xet_ready, 1)
                        act.wait_ge(down, SLOTB * e)
                        for f in range(FC):
                            act.wait_ge(up, FC * e + f + 1)
                            nc.scalar.activation(ht[:, f, :], ps[:, 2 + f % 2, 0:CAP], ACT.Relu).then_inc(ht_ready, 1)

                looped(act, EXPERTS // 2, turn)

            @block.vector
            def _(dve):
                def turn(i):
                    for n in range(2):
                        e = 2 * i + n
                        dve.wait_ge(xe_in[n], 16 * SLOTB * (i + 1))
                        full, rest = SLOTB - 1, size[-1]
                        nc.vector.tensor_tensor(gates[n][:, 0:full], xe[n][:, 0:full, bass.ds(E + e, 1)]
                                                .rearrange("p s o -> p (s o)"),
                                                occupied[:, bass.ds(e, 1), 0:full].rearrange("p o s -> p (o s)"), ALU.mult)
                        nc.vector.tensor_tensor(gates[n][0:rest, full:], xe[n][0:rest, full:, bass.ds(E + e, 1)]
                                                .rearrange("p s o -> p (s o)"),
                                                occupied[0:rest, bass.ds(e, 1), full:].rearrange("p o s -> p (o s)"),
                                                ALU.mult).then_inc(gates_ready, 1)
                        dve.wait_ge(gates_ready, e + 1)
                        dve.wait_ge(added, 16 * SLOTB * 2 * i)
                        for s in range(SLOTB):
                            dve.wait_ge(down, SLOTB * e + s + 1)
                            nc.vector.tensor_scalar(ye[n][0:size[s], s, :], ps[0:size[s], 4 + s, 0:E],
                                                    gates[n][0:size[s], s:s + 1], None,
                                                    ALU.mult).then_inc(ye_ready, 1)

                looped(dve, EXPERTS // 2, turn)


def finish(nc, x, w_out_t, bo_rows, identity, y_d, z_d, out):
    with ExitStack() as ctx:
        sb = lambda name, shape, dt=FP32: ctx.enter_context(nc.sbuf_tensor("f_" + name, shape, dt))
        sem = lambda name: ctx.enter_context(nc.semaphore("f_" + name))
        pair = lambda name: [sem(f"{name}{n}") for n in range(2)]
        wo = sb("wo", [P, KC, E])
        bo = sb("bo", [P, E])
        ident = sb("ident", [P, P])
        xin = [sb(f"x{n}", [P, CT, E]) for n in range(2)]
        z = [sb(f"z{n}", [P, CT, E]) for n in range(2)]
        g = [sb(f"g{n}", [P, CT, E]) for n in range(2)]
        s_sb = [sb(f"s{n}", [P, CT, E]) for n in range(2)]
        res = [sb(f"res{n}", [P, CT, E]) for n in range(2)]
        ps = ctx.enter_context(nc.psum_tensor("f_ps", [P, 6, 512], FP32))
        w_in, x_in, z_in, out_out = sem("w_in"), pair("x_in"), pair("z_in"), pair("out_out")
        g_ready, gated, res_ready = sem("g_ready"), sem("gated"), sem("res_ready")
        heads = HeadsOut(nc, ctx, "f_out", ps, 1, wo, ident, y_d)

        def rows(b, half):
            return bass.ds(b * T + half * CH, CH)

        with nc.Block() as block:

            @block.sync
            def _(sp):
                for dst, src in ((wo[:, :, :], w_out_t.rearrange("(k p) n -> p k n", p=P)),
                                 (bo[:, :], bo_rows.broadcast_to((P, E))), (ident[:, :], identity)):
                    sp.dma_start(dst, src).then_inc(w_in, 16)

                def load(dst, src, arrived, b, half):
                    sp.dma_start(dst[half][:, :, :], src[rows(b, half), :].rearrange("(t p) e -> p t e", p=P)
                                 ).then_inc(arrived[half], 16)

                def step(chunk, q):
                    if q == 0 and chunk(-1) and chunk(1):
                        sp.wait_ge(heads.flipped, CT * chunk(0)[2])
                        heads.load(sp, *chunk(1)[:2])
                    if q == 1 and chunk(-1) and chunk(1):
                        sp.wait_ge(g_ready, chunk(0)[2])
                        load(z, z_d, z_in, *chunk(1)[:2])
                    if q == 3 and chunk(-1):
                        b, half, c = chunk(-1)
                        sp.wait_ge(res_ready, CT * (c + 1))
                        if chunk(1):
                            load(xin, x, x_in, *chunk(1)[:2])
                        sp.dma_start(out[rows(b, half), :].rearrange("(t p) e -> p t e", p=P), res[half][:, :, :]
                                     ).then_inc(out_out[half], 16)

                for half in range(2):
                    sp.wait_ge(heads.cleared, half + 1)
                    heads.load(sp, 0, half)
                    load(z, z_d, z_in, 0, half)
                    load(xin, x, x_in, 0, half)
                over_out_quarters(sp, step)
                for half in range(2):
                    sp.wait_ge(out_out[half], 16 * B)

            @block.gpsimd
            def _(pool):
                def step(chunk, q):
                    at, t = ago(chunk, q, 3)
                    if at:
                        b, half, c = at
                        if t == 0:
                            pool.wait_ge(x_in[half], 16 * b + 16)
                            at_least(pool, out_out[half], 16 * b)
                        pool.wait_ge(gated, CT * c + t + 1)
                        nc.gpsimd.tensor_tensor(out=res[half][:, t, :], in0=s_sb[half][:, t, :],
                                                in1=xin[half][:, t, :], op=ALU.add).then_inc(res_ready, 1)

                over_out_quarters(pool, step)

            @block.tensor
            def _(pe):
                pe.wait_ge(w_in, 16 * 3)
                over_out_quarters(pe, lambda chunk, q: heads.tensor(pe, chunk, q))

            @block.scalar
            def _(act):
                def step(chunk, q):
                    heads.scalar(act, chunk, q)
                    if q == 1 and chunk(0):
                        b, half, c = chunk(0)
                        act.wait_ge(z_in[half], 16 * b + 16)
                        at_least(act, gated, CT * (c - 1))
                        nc.scalar.activation(g[half][:, :, :], z[half][:, :, :], ACT.Silu).then_inc(g_ready, 1)

                over_out_quarters(act, step)

            @block.vector
            def _(dve):
                heads.clear()
                dve.wait_ge(w_in, 16 * 3)

                def step(chunk, q):
                    heads.vector(dve, chunk, q)
                    at, t = ago(chunk, q, 2)
                    if at:
                        _, half, c = at
                        at_least(dve, res_ready, CT * (c - 1))
                        dve.wait_ge(heads.projected, CT * c + t + 1)
                        nc.vector.tensor_tensor(s_sb[half][:, t, :], ps[:, 4 + t % 2, 0:E], bo[:, :],
                                                ALU.add).then_inc(heads.taken, 1)
                    at, t = ago(chunk, q, 3)
                    if at:
                        _, half, c = at
                        dve.wait_ge(g_ready, c + 1)
                        dve.wait_ge(heads.taken, CT * c + t + 1)
                        nc.vector.tensor_tensor(s_sb[half][:, t, :], s_sb[half][:, t, :], g[half][:, t, :],
                                                ALU.mult).then_inc(gated, 1)

                over_out_quarters(dve, step)


def program(nc, x, w_main_t, w_out_t, bo, g1, w_qkv, w_o, g2, w_router, w1, w2, rope_main, rope_head, identity,
            causal_mask, ones, upper, iota, token_parts, slot_rows, out):
    scratch = lambda name, shape, dt=FP32: nc.dram_tensor(name, shape, dt, kind="Internal").ap()
    xn_d = scratch("xn_scratch", (TOK, E))
    qk_d = scratch("qk_scratch", (UNITS, 2, PARTS, GH * HD, T), BF16)
    v_d = scratch("v_scratch", (UNITS, T, GH * VW))
    y_d = scratch("y_scratch", (UNITS, GH, YW, T))
    z_d = scratch("z_scratch", (TOK + SLOTB * P, E))
    h_d = scratch("h_scratch", (TOK, E + EXPERTS))
    project(nc, x, w_main_t, w_qkv, g1, rope_main, rope_head, identity, xn_d, qk_d, v_d)
    attend(nc, identity, causal_mask, qk_d, v_d, y_d)
    with ExitStack() as ctx:
        keep = lambda name, shape, dt=FP32: ctx.enter_context(nc.sbuf_tensor(name, shape, dt))
        logits = keep("logits", [P, EXPERTS, TILES])
        occupied = keep("occupied", [P, EXPERTS, SLOTB])
        gather_row = keep("gather_row", [P, EXPERTS, SLOTB], U32)
        scatter_row = keep("scatter_row", [P, EXPERTS, SLOTB], U32)
        block_mid(nc, w_o, w_router, g2, identity, xn_d, y_d, z_d, h_d, logits)
        route(nc, ones, upper, iota, token_parts, slot_rows, h_d, logits, occupied, gather_row, scatter_row)
        experts(nc, w1, w2, g2, identity, h_d, z_d, occupied, gather_row, scatter_row)
    finish(nc, x, w_out_t, bo, identity, y_d, z_d, out)


def _constants(np):
    def rotary(width, exponents):
        theta = np.repeat((10000.0 ** exponents).astype(np.float32), 2)
        angle = (np.arange(T, dtype=np.float32)[:, None] * theta[None, :]).astype(np.float64)
        sign = np.where(np.arange(width) % 2 == 0, -1.0, 1.0)
        return np.stack([np.cos(angle), np.sin(angle) * sign]).astype(np.float32)

    row, col = np.arange(P)[:, None], np.arange(P)[None, :]
    eye = (row == col).astype(np.float32)
    mask = np.zeros((P, 512), np.float32)
    mask[:, 512 - P:] = np.where(col > row, -BIG, 0.0)
    parts = np.zeros((P, TILES, 3), np.float32)
    parts[:, :, 0] = 1.0
    parts[:, :, 1] = np.arange(TILES)[None, :]
    parts[:, :, 2] = np.arange(P)[:, None]
    return {
        "rope_main": rotary(E, -np.arange(0, E, 2) / E),
        "rope_head": rotary(HD, -2.0 * np.arange(HD // 2) / HD),
        "identity": eye,
        "causal_mask": mask,
        "ones": np.ones((P, P), np.float32),
        "upper": (col >= row).astype(np.float32),
        "iota": np.broadcast_to(col, (P, P)).astype(np.float32),
        "token_parts": parts,
        "slot_rows": (TOK + np.arange(SLOTB)[None, :] * P + np.arange(P)[:, None]).astype(np.float32),
    }


def kernel(**inputs):
    import numpy as np
    import concourse.bacc as bacc
    from concourse.bass_utils import run_bass_kernel_spmd

    a = {k: np.asarray(v) for k, v in inputs.items()}
    columns = lambda v: np.ascontiguousarray(v.reshape(KC, P).T)
    arrays = {
        "x": a["L0_attn_input"].reshape(TOK, E),
        "w_main_t": np.concatenate([a["L0_attn_Wq"].T, a["L0_attn_Wk"].T, a["L0_attn_Wv"].T], axis=1),
        "w_out_t": np.ascontiguousarray(a["L0_attn_Wo"].T),
        "bo": a["L0_attn_bo"].reshape(1, E),
        "g1": columns(a["L0_ffn_g1"]),
        "w_qkv": a["L0_ffn_w_qkv"],
        "w_o": a["L0_ffn_w_o"],
        "g2": columns(a["L0_ffn_g2"]),
        "w_router": a["L0_ffn_w_router"],
        "w1": a["L0_ffn_w1"],
        "w2": a["L0_ffn_w2"],
        **_constants(np),
    }
    nc = bacc.Bacc("TRN2", target_bir_lowering=False, num_devices=1)
    args, maps = [], {}
    for name, array in arrays.items():
        maps[f"in_{name}"] = np.ascontiguousarray(array)
        args.append(nc.dram_tensor(f"in_{name}", array.shape, mybir.dt.from_np(array.dtype), kind="ExternalInput").ap())
    args.append(nc.dram_tensor("out_y", (TOK, E), FP32, kind="ExternalOutput").ap())
    program(nc, *args)
    result = run_bass_kernel_spmd(nc, [maps], core_ids=[0])
    return result.results[0]["out_y"].reshape(B, T, E)
```
